# Optimizing a Trainium2 kernel written in Bass

```python
import numpy as np
import jax
import jax.numpy as jnp

def _softmax(x, axis=-1):
    return jax.nn.softmax(x, axis=axis)

def _gelu(x):
    return jax.nn.gelu(x, approximate=True)

def _silu(x):
    return jax.nn.silu(x)

def _sigmoid(x):
    return jax.nn.sigmoid(x)

def _layernorm(x, axis=-1, eps=1e-05):
    m = jnp.mean(x, axis=axis, keepdims=True)
    v = jnp.var(x, axis=axis, keepdims=True)
    return (x - m) / jnp.sqrt(v + eps)

def _scatter_add(tgt, idx, src, axis=0):
    return tgt.at[idx].add(src)

def _segment_sum(src, seg, n):
    return jax.ops.segment_sum(src, seg, n)
kernel_name = 'mk_adaln_d2_jaxref_r8_1b7aad'

def setup_inputs(seed: int=0):
    np.random.seed(seed)
    _w = jnp.asarray

    def _L0_attn_setup():
        import jax, jax.numpy as jnp
        import numpy as np
        NUM_HEADS = 16
        key = jax.random.key(seed)
        kx, kq, kk, kv = jax.random.split(key, 4)
        N, S, D = (2, 512, 128)
        scale = 1.0 / np.sqrt(D)
        x = jax.random.normal(kx, (N, S, D), dtype=jnp.float32)
        Wq = jax.random.normal(kq, (D, D), dtype=jnp.float32) * scale
        Wk = jax.random.normal(kk, (D, D), dtype=jnp.float32) * scale
        Wv = jax.random.normal(kv, (D, D), dtype=jnp.float32) * scale
        return {'x': x, 'Wq': Wq, 'Wk': Wk, 'Wv': Wv}
    _L0_attn_in = _L0_attn_setup()

    def _L0_ffn_setup():
        import jax, jax.numpy as jnp
        import numpy as np
        B, S, DIM = (4, 512, 128)
        BASE_COUPLING = 0.1
        NUM_CYCLES = 3

        def _gelu(x):
            return jax.nn.gelu(x, approximate=False)

        def _coupling_net(h, w1, b1, w2, b2, w3, b3, w4, b4):
            h = _gelu(h @ w1 + b1)
            h = _gelu(h @ w2 + b2)
            h = _gelu(h @ w3 + b3)
            return jax.nn.sigmoid(h @ w4 + b4)

        def _global_net(h, w1, b1, w2, b2, w3, b3):
            h = _gelu(h @ w1 + b1)
            h = _gelu(h @ w2 + b2)
            return jax.nn.sigmoid(h @ w3 + b3)

        def _twist(x):
            o_r, o_i, p_r, p_i = jnp.split(x, 4, axis=-1)
            return jnp.concatenate([p_r, -p_i, -o_r, o_i], axis=-1)
        key = jax.random.key(seed)
        ks = jax.random.split(key, 9)
        d = DIM

        def w(k, fan_in, fan_out):
            return jax.random.normal(k, (fan_in, fan_out), dtype=jnp.float32) / np.sqrt(fan_in).astype(np.float32)
        inp = {'x': jax.random.normal(ks[0], (B, S, d), dtype=jnp.float32)}
        cn_dims = [(d, d), (d, d // 2), (d // 2, d // 4), (d // 4, 1)]
        for i, (a, b) in enumerate(cn_dims):
            inp[f'cn_w{i + 1}'] = w(ks[1 + i], a, b)
            inp[f'cn_b{i + 1}'] = jnp.zeros((b,), dtype=jnp.float32)
        gc_dims = [(d, d // 2), (d // 2, d // 4), (d // 4, 1)]
        for i, (a, b) in enumerate(gc_dims):
            inp[f'gc_w{i + 1}'] = w(ks[5 + i], a, b)
            inp[f'gc_b{i + 1}'] = jnp.zeros((b,), dtype=jnp.float32)
        inp['adaptive_range'] = jnp.full((1,), 0.2, dtype=jnp.float32)
        return inp
    _L0_ffn_in = _L0_ffn_setup()
    _L0_c = _w((lambda *s: np.random.randn(*s).astype(np.float32) * 0.05)(2, 128))
    _L0_wmod = _w((lambda *s: np.random.randn(*s).astype(np.float32) * 0.05)(128, 6 * 128) * 128 ** (-0.5))

    def _L1_attn_setup():
        import math
        import jax, jax.numpy as jnp
        import numpy as np
        from jax import lax
        D_MODEL = 128
        N_LAYERS = 2
        D_STATE = 16
        D_CONV = 4
        EXPAND = 2
        D_INNER = EXPAND * D_MODEL
        DT_RANK = math.ceil(D_MODEL / 16)
        BATCH = 2
        SEQLEN = 128
        BETA = 0.6
        ALPHA = 1.0
        EPS = 1e-05
        DT_MIN, DT_MAX, DT_FLOOR = (0.001, 0.1, 0.0001)

        def _rmsnorm(x, w):
            return x * jax.lax.rsqrt(jnp.mean(x * x, axis=-1, keepdims=True) + EPS) * w

        def _block(x, in_w, cw, cb, xp_w, dtw, dtb, a_log, dp, ow):
            B, L, _ = x.shape
            xz = jnp.einsum('bld,ed->ble', x, in_w)
            xb, z = jnp.split(xz, 2, axis=-1)
            xc = lax.conv_general_dilated(xb.transpose(0, 2, 1), cw[:, None, :], window_strides=(1,), padding=[(D_CONV - 1, 0)], dimension_numbers=('NCH', 'OIH', 'NCH'), feature_group_count=D_INNER)
            xb = jax.nn.silu((xc + cb[None, :, None]).transpose(0, 2, 1))
            dbc = jnp.einsum('ble,re->blr', xb, xp_w)
            delta = dbc[..., :DT_RANK]
            Bm = dbc[..., DT_RANK:DT_RANK + D_STATE]
            Cm = dbc[..., DT_RANK + D_STATE:]
            delta = jax.nn.softplus(jnp.einsum('blr,er->ble', delta, dtw) + dtb)
            dA = jnp.exp(delta[..., None] * -jnp.exp(a_log))
            mi = ALPHA * delta[..., None] * Bm[:, :, None, :] * xb[..., None]

            def scan_fn(carry, inp):
                h, v = carry
                dA_t, mi_t, C_t = inp
                v = BETA * v + mi_t
                h = dA_t * h + v
                y_t = jnp.einsum('ben,bn->be', h, C_t)
                return ((h, v), y_t)
            h0 = jnp.zeros((B, D_INNER, D_STATE), dtype=x.dtype)
            _, ys = lax.scan(scan_fn, (h0, h0), (dA.transpose(1, 0, 2, 3), mi.transpose(1, 0, 2, 3), Cm.transpose(1, 0, 2)))
            y = ys.transpose(1, 0, 2) + dp * xb
            y = y * jax.nn.silu(z)
            return jnp.einsum('ble,de->bld', y, ow)
        key = jax.random.key(seed)
        ks = jax.random.split(key, 10)
        std = 0.02
        nl = N_LAYERS
        x = jax.random.normal(ks[0], (BATCH, SEQLEN, D_MODEL), dtype=jnp.float32)
        in_proj_w = jax.random.normal(ks[1], (nl, 2 * D_INNER, D_MODEL), dtype=jnp.float32) * std
        conv_w = jax.random.normal(ks[2], (nl, D_INNER, D_CONV), dtype=jnp.float32) * std
        conv_b = jnp.zeros((nl, D_INNER), dtype=jnp.float32)
        x_proj_w = jax.random.normal(ks[3], (nl, DT_RANK + 2 * D_STATE, D_INNER), dtype=jnp.float32) * std
        dt_std = DT_RANK ** (-0.5)
        dt_w = jax.random.uniform(ks[4], (nl, D_INNER, DT_RANK), dtype=jnp.float32, minval=-dt_std, maxval=dt_std)
        dt = jnp.exp(jax.random.uniform(ks[5], (nl, D_INNER), dtype=jnp.float32) * (math.log(DT_MAX) - math.log(DT_MIN)) + math.log(DT_MIN))
        dt = jnp.clip(dt, DT_FLOOR, None)
        dt_b = dt + jnp.log(-jnp.expm1(-dt))
        A_log = jnp.broadcast_to(jnp.log(jnp.arange(1, D_STATE + 1, dtype=jnp.float32)), (nl, D_INNER, D_STATE)).copy()
        Dp = jnp.ones((nl, D_INNER), dtype=jnp.float32)
        out_w = jax.random.normal(ks[6], (nl, D_MODEL, D_INNER), dtype=jnp.float32) * std
        norm_w = jnp.ones((nl, D_MODEL), dtype=jnp.float32)
        return {'x': x, 'norm_w': norm_w, 'in_proj_w': in_proj_w, 'conv_w': conv_w, 'conv_b': conv_b, 'x_proj_w': x_proj_w, 'dt_w': dt_w, 'dt_b': dt_b, 'A_log': A_log, 'Dp': Dp, 'out_w': out_w}
    _L1_attn_in = _L1_attn_setup()

    def _L1_ffn_setup():
        import jax, jax.numpy as jnp
        import numpy as np
        B, S, D, F, E, K = (4, 256, 128, 512, 8, 2)
        FS = 128
        LN_EPS = 1e-05

        def _swiglu(x, gu_w, dn_w):
            gate, up = jnp.split(x @ gu_w, 2, axis=-1)
            gate = jnp.clip(gate, -10.0, 10.0)
            return jax.nn.silu(gate) * up @ dn_w
        key = jax.random.key(seed)
        ks = jax.random.split(key, 6)
        s = 0.02
        return {'x': jax.random.normal(ks[0], (B, S, D), jnp.float32), 'ln_gamma': jnp.ones((D,), jnp.float32), 'ln_beta': jnp.zeros((D,), jnp.float32), 'router_w': jax.random.normal(ks[1], (D, E), jnp.float32) * s, 'gate_up_w': jax.random.normal(ks[2], (E, D, 2 * F), jnp.float32) * s, 'down_w': jax.random.normal(ks[3], (E, F, D), jnp.float32) * s, 'shared_gate_up_w': jax.random.normal(ks[4], (D, 2 * FS), jnp.float32) * s, 'shared_down_w': jax.random.normal(ks[5], (FS, D), jnp.float32) * s}
    _L1_ffn_in = _L1_ffn_setup()
    _L1_c = _w((lambda *s: np.random.randn(*s).astype(np.float32) * 0.05)(2, 128))
    _L1_wmod = _w((lambda *s: np.random.randn(*s).astype(np.float32) * 0.05)(128, 6 * 128) * 128 ** (-0.5))
    _d = {'L0_attn_x': _L0_attn_in['x'], 'L0_attn_Wq': _L0_attn_in['Wq'], 'L0_attn_Wk': _L0_attn_in['Wk'], 'L0_attn_Wv': _L0_attn_in['Wv'], 'L0_ffn_cn_w1': _L0_ffn_in['cn_w1'], 'L0_ffn_cn_b1': _L0_ffn_in['cn_b1'], 'L0_ffn_cn_w2': _L0_ffn_in['cn_w2'], 'L0_ffn_cn_b2': _L0_ffn_in['cn_b2'], 'L0_ffn_cn_w3': _L0_ffn_in['cn_w3'], 'L0_ffn_cn_b3': _L0_ffn_in['cn_b3'], 'L0_ffn_cn_w4': _L0_ffn_in['cn_w4'], 'L0_ffn_cn_b4': _L0_ffn_in['cn_b4'], 'L0_ffn_gc_w1': _L0_ffn_in['gc_w1'], 'L0_ffn_gc_b1': _L0_ffn_in['gc_b1'], 'L0_ffn_gc_w2': _L0_ffn_in['gc_w2'], 'L0_ffn_gc_b2': _L0_ffn_in['gc_b2'], 'L0_ffn_gc_w3': _L0_ffn_in['gc_w3'], 'L0_ffn_gc_b3': _L0_ffn_in['gc_b3'], 'L0_ffn_adaptive_range': _L0_ffn_in['adaptive_range'], 'L0_c': _L0_c, 'L0_wmod': _L0_wmod, 'L1_attn_norm_w': _L1_attn_in['norm_w'], 'L1_attn_in_proj_w': _L1_attn_in['in_proj_w'], 'L1_attn_conv_w': _L1_attn_in['conv_w'], 'L1_attn_conv_b': _L1_attn_in['conv_b'], 'L1_attn_x_proj_w': _L1_attn_in['x_proj_w'], 'L1_attn_dt_w': _L1_attn_in['dt_w'], 'L1_attn_dt_b': _L1_attn_in['dt_b'], 'L1_attn_A_log': _L1_attn_in['A_log'], 'L1_attn_Dp': _L1_attn_in['Dp'], 'L1_attn_out_w': _L1_attn_in['out_w'], 'L1_ffn_ln_gamma': _L1_ffn_in['ln_gamma'], 'L1_ffn_ln_beta': _L1_ffn_in['ln_beta'], 'L1_ffn_router_w': _L1_ffn_in['router_w'], 'L1_ffn_gate_up_w': _L1_ffn_in['gate_up_w'], 'L1_ffn_down_w': _L1_ffn_in['down_w'], 'L1_ffn_shared_gate_up_w': _L1_ffn_in['shared_gate_up_w'], 'L1_ffn_shared_down_w': _L1_ffn_in['shared_down_w'], 'L1_c': _L1_c, 'L1_wmod': _L1_wmod}
    _x0 = _d['L0_attn_x']
    _d['L0_attn_x'] = jax.random.normal(jax.random.fold_in(jax.random.key(seed), 1), (2, 1024, 128), dtype=_x0.dtype)
    del _x0
    return _d

def reference(L0_attn_x, L0_attn_Wq, L0_attn_Wk, L0_attn_Wv, L0_ffn_cn_w1, L0_ffn_cn_b1, L0_ffn_cn_w2, L0_ffn_cn_b2, L0_ffn_cn_w3, L0_ffn_cn_b3, L0_ffn_cn_w4, L0_ffn_cn_b4, L0_ffn_gc_w1, L0_ffn_gc_b1, L0_ffn_gc_w2, L0_ffn_gc_b2, L0_ffn_gc_w3, L0_ffn_gc_b3, L0_ffn_adaptive_range, L0_c, L0_wmod, L1_attn_norm_w, L1_attn_in_proj_w, L1_attn_conv_w, L1_attn_conv_b, L1_attn_x_proj_w, L1_attn_dt_w, L1_attn_dt_b, L1_attn_A_log, L1_attn_Dp, L1_attn_out_w, L1_ffn_ln_gamma, L1_ffn_ln_beta, L1_ffn_router_w, L1_ffn_gate_up_w, L1_ffn_down_w, L1_ffn_shared_gate_up_w, L1_ffn_shared_down_w, L1_c, L1_wmod):

    def _L0_attn_ref(x, Wq, Wk, Wv):
        import jax, jax.numpy as jnp
        import numpy as np
        NUM_HEADS = 16
        N, S, D = x.shape
        H = NUM_HEADS
        hd = D // H
        q = (x @ Wq.T).reshape(N, S, H, hd).transpose(0, 2, 1, 3)
        k = (x @ Wk.T).reshape(N, S, H, hd).transpose(0, 2, 1, 3)
        v = (x @ Wv.T).reshape(N, S, H, hd).transpose(0, 2, 1, 3)
        energy = jnp.einsum('nhqd,nhkd->nhqk', q, k)
        attn = jax.nn.softmax(energy / jnp.sqrt(jnp.float32(hd)), axis=3)
        out = jnp.einsum('nhql,nhld->nhqd', attn, v)
        return out.transpose(0, 2, 1, 3).reshape(N, S, D)

    def _L0_ffn_ref(x, cn_w1, cn_b1, cn_w2, cn_b2, cn_w3, cn_b3, cn_w4, cn_b4, gc_w1, gc_b1, gc_w2, gc_b2, gc_w3, gc_b3, adaptive_range):
        import jax, jax.numpy as jnp
        import numpy as np
        B, S, DIM = (4, 512, 128)
        BASE_COUPLING = 0.1
        NUM_CYCLES = 3

        def _gelu(x):
            return jax.nn.gelu(x, approximate=False)

        def _coupling_net(h, w1, b1, w2, b2, w3, b3, w4, b4):
            h = _gelu(h @ w1 + b1)
            h = _gelu(h @ w2 + b2)
            h = _gelu(h @ w3 + b3)
            return jax.nn.sigmoid(h @ w4 + b4)

        def _global_net(h, w1, b1, w2, b2, w3, b3):
            h = _gelu(h @ w1 + b1)
            h = _gelu(h @ w2 + b2)
            return jax.nn.sigmoid(h @ w3 + b3)

        def _twist(x):
            o_r, o_i, p_r, p_i = jnp.split(x, 4, axis=-1)
            return jnp.concatenate([p_r, -p_i, -o_r, o_i], axis=-1)
        global_context = x.mean(axis=1, keepdims=True)
        gf = _global_net(global_context, gc_w1, gc_b1, gc_w2, gc_b2, gc_w3, gc_b3)
        out = x
        for _ in range(NUM_CYCLES):
            tf = _coupling_net(out, cn_w1, cn_b1, cn_w2, cn_b2, cn_w3, cn_b3, cn_w4, cn_b4)
            combined = 0.7 * gf + 0.3 * tf
            coupling = BASE_COUPLING + adaptive_range * (combined - 0.5) * 2.0
            out = out + coupling * _twist(out)
        return out

    def _L1_attn_ref(x, norm_w, in_proj_w, conv_w, conv_b, x_proj_w, dt_w, dt_b, A_log, Dp, out_w):
        import math
        import jax, jax.numpy as jnp
        import numpy as np
        from jax import lax
        D_MODEL = 128
        N_LAYERS = 2
        D_STATE = 16
        D_CONV = 4
        EXPAND = 2
        D_INNER = EXPAND * D_MODEL
        DT_RANK = math.ceil(D_MODEL / 16)
        BATCH = 2
        SEQLEN = 128
        BETA = 0.6
        ALPHA = 1.0
        EPS = 1e-05
        DT_MIN, DT_MAX, DT_FLOOR = (0.001, 0.1, 0.0001)

        def _rmsnorm(x, w):
            return x * jax.lax.rsqrt(jnp.mean(x * x, axis=-1, keepdims=True) + EPS) * w

        def _block(x, in_w, cw, cb, xp_w, dtw, dtb, a_log, dp, ow):
            B, L, _ = x.shape
            xz = jnp.einsum('bld,ed->ble', x, in_w)
            xb, z = jnp.split(xz, 2, axis=-1)
            xc = lax.conv_general_dilated(xb.transpose(0, 2, 1), cw[:, None, :], window_strides=(1,), padding=[(D_CONV - 1, 0)], dimension_numbers=('NCH', 'OIH', 'NCH'), feature_group_count=D_INNER)
            xb = jax.nn.silu((xc + cb[None, :, None]).transpose(0, 2, 1))
            dbc = jnp.einsum('ble,re->blr', xb, xp_w)
            delta = dbc[..., :DT_RANK]
            Bm = dbc[..., DT_RANK:DT_RANK + D_STATE]
            Cm = dbc[..., DT_RANK + D_STATE:]
            delta = jax.nn.softplus(jnp.einsum('blr,er->ble', delta, dtw) + dtb)
            dA = jnp.exp(delta[..., None] * -jnp.exp(a_log))
            mi = ALPHA * delta[..., None] * Bm[:, :, None, :] * xb[..., None]

            def scan_fn(carry, inp):
                h, v = carry
                dA_t, mi_t, C_t = inp
                v = BETA * v + mi_t
                h = dA_t * h + v
                y_t = jnp.einsum('ben,bn->be', h, C_t)
                return ((h, v), y_t)
            h0 = jnp.zeros((B, D_INNER, D_STATE), dtype=x.dtype)
            _, ys = lax.scan(scan_fn, (h0, h0), (dA.transpose(1, 0, 2, 3), mi.transpose(1, 0, 2, 3), Cm.transpose(1, 0, 2)))
            y = ys.transpose(1, 0, 2) + dp * xb
            y = y * jax.nn.silu(z)
            return jnp.einsum('ble,de->bld', y, ow)
        for i in range(N_LAYERS):
            x = x + _block(_rmsnorm(x, norm_w[i]), in_proj_w[i], conv_w[i], conv_b[i], x_proj_w[i], dt_w[i], dt_b[i], A_log[i], Dp[i], out_w[i])
        return x

    def _L1_ffn_ref(x, ln_gamma, ln_beta, router_w, gate_up_w, down_w, shared_gate_up_w, shared_down_w):
        import jax, jax.numpy as jnp
        import numpy as np
        B, S, D, F, E, K = (4, 256, 128, 512, 8, 2)
        FS = 128
        LN_EPS = 1e-05

        def _swiglu(x, gu_w, dn_w):
            gate, up = jnp.split(x @ gu_w, 2, axis=-1)
            gate = jnp.clip(gate, -10.0, 10.0)
            return jax.nn.silu(gate) * up @ dn_w
        b, s, d = x.shape
        xf = x.reshape(-1, d)
        mu = jnp.mean(xf, axis=-1, keepdims=True)
        var = jnp.var(xf, axis=-1, keepdims=True)
        xn = (xf - mu) * jax.lax.rsqrt(var + LN_EPS) * ln_gamma + ln_beta
        logits = xn @ router_w
        probs = jax.nn.softmax(logits, axis=-1)
        topv, topi = jax.lax.top_k(probs, K)
        topv = topv / jnp.sum(topv, axis=-1, keepdims=True)
        comb = jnp.sum(jax.nn.one_hot(topi, E, dtype=xn.dtype) * topv[..., None], axis=1)
        out = jnp.zeros_like(xf)
        for e in range(E):
            out = out + comb[:, e:e + 1] * _swiglu(xn, gate_up_w[e], down_w[e])
        out = out + _swiglu(xn, shared_gate_up_w, shared_down_w)
        return out.reshape(b, s, d)
    x = L0_attn_x
    mod = (_silu(L0_c) @ L0_wmod).reshape(L0_c.shape[0], 6, 1, -1)
    sa, ca, ga, sb, cb, gb = (mod[:, 0], mod[:, 1], mod[:, 2], mod[:, 3], mod[:, 4], mod[:, 5])
    ga = (2 * (ga >= 0) - 1) * jnp.maximum(jnp.abs(ga), 0.25)
    gb = (2 * (gb >= 0) - 1) * jnp.maximum(jnp.abs(gb), 0.25)
    h = _layernorm(x, axis=-1) * (1 + ca) + sa
    x = x + ga * _L0_attn_ref(h, L0_attn_Wq, L0_attn_Wk, L0_attn_Wv)
    h = _layernorm(x, axis=-1) * (1 + cb) + sb
    x = x + gb * _L0_ffn_ref(h, L0_ffn_cn_w1, L0_ffn_cn_b1, L0_ffn_cn_w2, L0_ffn_cn_b2, L0_ffn_cn_w3, L0_ffn_cn_b3, L0_ffn_cn_w4, L0_ffn_cn_b4, L0_ffn_gc_w1, L0_ffn_gc_b1, L0_ffn_gc_w2, L0_ffn_gc_b2, L0_ffn_gc_w3, L0_ffn_gc_b3, L0_ffn_adaptive_range)
    mod = (_silu(L1_c) @ L1_wmod).reshape(L1_c.shape[0], 6, 1, -1)
    sa, ca, ga, sb, cb, gb = (mod[:, 0], mod[:, 1], mod[:, 2], mod[:, 3], mod[:, 4], mod[:, 5])
    ga = (2 * (ga >= 0) - 1) * jnp.maximum(jnp.abs(ga), 0.25)
    gb = (2 * (gb >= 0) - 1) * jnp.maximum(jnp.abs(gb), 0.25)
    h = _layernorm(x, axis=-1) * (1 + ca) + sa
    x = x + ga * _L1_attn_ref(h, L1_attn_norm_w, L1_attn_in_proj_w, L1_attn_conv_w, L1_attn_conv_b, L1_attn_x_proj_w, L1_attn_dt_w, L1_attn_dt_b, L1_attn_A_log, L1_attn_Dp, L1_attn_out_w)
    h = _layernorm(x, axis=-1) * (1 + cb) + sb
    x = x + gb * _L1_ffn_ref(h, L1_ffn_ln_gamma, L1_ffn_ln_beta, L1_ffn_router_w, L1_ffn_gate_up_w, L1_ffn_down_w, L1_ffn_shared_gate_up_w, L1_ffn_shared_down_w)
    return x

_drawn_inputs = setup_inputs


def setup_inputs(seed=0):
    import zlib

    import numpy as np

    out = dict(_drawn_inputs(seed))
    spreads = {'L0_ffn_cn_b1': (0.0, 0.8),
     'L0_ffn_cn_b2': (0.0, 0.8),
     'L0_ffn_cn_b3': (0.0, 2.0),
     'L0_ffn_gc_b1': (0.0, 2.0),
     'L0_ffn_gc_b2': (0.0, 2.0),
     'L1_attn_norm_w': (1.0, 0.6),
     'L1_attn_conv_b': (0.0, 0.8),
     'L1_attn_Dp': (1.0, 0.6),
     'L1_ffn_ln_gamma': (1.0, 0.6),
     'L1_ffn_ln_beta': (0.0, 0.8)}
    factors = {'L0_ffn_cn_w1': 8.0,
     'L0_ffn_cn_w2': 8.0,
     'L0_ffn_cn_w3': 8.0,
     'L0_ffn_cn_w4': 8.0,
     'L0_ffn_gc_w1': 64.0,
     'L0_ffn_gc_w2': 64.0,
     'L0_ffn_gc_w3': 21.538,
     'L1_attn_in_proj_w': 8.0,
     'L1_attn_conv_w': 8.0,
     'L1_attn_x_proj_w': 8.0,
     'L1_attn_dt_w': 8.0,
     'L1_attn_dt_b': 8.0,
     'L1_attn_A_log': 8.0,
     'L1_attn_out_w': 8.0,
     'L1_ffn_router_w': 8.0,
     'L1_ffn_gate_up_w': 8.0,
     'L1_ffn_down_w': 8.0,
     'L1_ffn_shared_gate_up_w': 8.0,
     'L1_ffn_shared_down_w': 8.0}
    for name, (base, spread) in spreads.items():
        noise = np.random.default_rng([zlib.crc32(name.encode()), seed]).standard_normal(out[name].shape)
        drawn = base * np.exp(spread * noise) if base else spread * noise
        out[name] = jnp.asarray(drawn.astype(out[name].dtype))
    for name, factor in factors.items():
        out[name] = (out[name] * factor).astype(out[name].dtype)
    return out
```

```python
from contextlib import ExitStack
from itertools import count

import numpy as np

import concourse.bass as bass
from concourse import mybir

F32 = mybir.dt.float32
BF16 = mybir.dt.bfloat16
U32 = mybir.dt.uint32
ALU = mybir.AluOpType
ACT = mybir.ActivationFunctionType
AX_X = mybir.AxisListType.X

P = 128
NB = 2
S = 1024
D = 128
TOK = NB * S
NT = TOK // P
TB = S // P
CH = 512
NC = TOK // CH
H, HD = 16, 8
BH = NB * H
DI, DS, DTR, KW = 256, 16, 8, 4
NBLK = DI // P
NL = 2
E, FF = 8, 512
FB = FF // P
EPS = 1e-5
BETA = 0.6
SHAPES = {}


_keys = count()


class Track:

    def __init__(self, ctx, nc, engine, name):
        self.engine = engine
        self.sem = ctx.enter_context(nc.semaphore(f"done_{name}"))
        self.n = 0
        self.key = next(_keys)
        self.seen = {}

    def __call__(self, instruction):
        instruction.then_inc(self.sem, 1)
        self.n += 1
        return (self.sem, self.n, self.key)

    def need(self, *marks):
        for mark in marks:
            if mark is None:
                continue
            sem, n, key = mark
            if self.seen.get(key, 0) < n:
                self.engine.wait_ge(sem, n)
                self.seen[key] = n

    def last(self):
        return (self.sem, self.n, self.key) if self.n else None


class Arrival:

    def __init__(self, ctx, nc, name):
        self.sem = ctx.enter_context(nc.semaphore(name))
        self.n = 0
        self.key = next(_keys)

    def __call__(self, instruction):
        instruction.then_inc(self.sem, 16)
        self.n += 16

    def mark(self):
        return (self.sem, self.n, self.key)


class Event:

    def __init__(self, ctx, nc, name, engine, before=0, credit=32):
        self.sem = ctx.enter_context(nc.semaphore(name))
        self.credit = credit
        engine.sem_inc(self.sem, credit - before)

    def __call__(self, instruction, by=1):
        instruction.then_inc(self.sem, by)
        return instruction

    def wait(self, engine, count):
        engine.wait_ge(self.sem, count + self.credit)


class Banks:

    def __init__(self, tensors):
        self.tensors = tensors
        self.free = [()] * len(tensors)
        self.at = 0

    def take(self, writer):
        k = self.at % len(self.tensors)
        self.at += 1
        writer.need(*self.free[k])
        return k, self.tensors[k]

    def release(self, k, *marks):
        self.free[k] = marks


def build(nc, A, out):
    ctx = ExitStack()
    with ctx:
        V = Track(ctx, nc, nc.vector, "vector")
        S_ = Track(ctx, nc, nc.scalar, "scalar")
        G = Track(ctx, nc, nc.gpsimd, "gpsimd")
        T = Track(ctx, nc, nc.tensor, "tensor")
        Q = Track(ctx, nc, nc.sync, "sync")
        K = Kernel(nc, ctx, A, out, V, S_, G, T, Q)
        K.constants()
        K.modulation()
        K.attention()
        K.coupling()
        K.mamba()
        K.experts()
        K.store()


class Kernel:
    def __init__(self, nc, ctx, A, out, V, S_, G, T, Q):
        self.nc, self.ctx, self.A, self.out = nc, ctx, A, out
        self.V, self.S, self.G, self.T, self.Q = V, S_, G, T, Q
        self.tracks = (V, S_, G, T)
        self.serial = 0

    def sb(self, scope, name, shape, dt=F32):
        return scope.enter_context(self.nc.sbuf_tensor(name, shape, dt))

    def banks(self, scope, name, n, dt=F32):
        return Banks([scope.enter_context(self.nc.psum_tensor(f"{name}{k}", [P, CH], dt)) for k in range(n)])

    def settle(self):
        for t in self.tracks + (self.Q,):
            t.need(*[o.last() for o in self.tracks])

    def constants(self):
        nc, A, ctx = self.nc, self.A, self.ctx
        sb = lambda n, s, d=F32: self.sb(ctx, n, s, d)
        self.X = sb("x", [P, NT, D])
        self.HT = sb("h_t", [P, TOK])
        self.N = sb("normed", [P, NT, D])
        self.ident = sb("ident", [P, P])
        self.identb = sb("identb", [P, P], BF16)
        self.half = sb("minus_half", [P, NT])
        self.stat = sb("bn_parts", [P, NT, 6])
        self.mv = sb("mean_var", [P, NT, 2])
        self.ve = sb("var_eps", [P, NT])
        self.rs = sb("rstd", [P, NT])
        self.cT = [sb(f"c_t{l}", [P, NB]) for l in range(2)]
        self.sil = [sb(f"silu_c{l}", [P, NB]) for l in range(2)]
        self.silrep = [sb(f"silu_rep{l}", [P, NB, P]) for l in range(2)]
        self.wmod = [sb(f"wmod{l}", [P, 6 * D]) for l in range(2)]
        self.mcol = [sb(f"mod_col{l}", [P, 6, NB]) for l in range(2)]
        self.mrow = [sb(f"mod_row{l}", [P, NB, 6, D]) for l in range(2)]
        self.gtmp = sb("gate_tmp", [P, 2 * D])

        self.in_x = Arrival(ctx, nc, "in_x")
        self.in_c = Arrival(ctx, nc, "in_c")
        self.in_k = Arrival(ctx, nc, "in_k")
        for l in range(2):
            self.in_c(nc.scalar.dma_start(self.cT[l][:], A[f"cT{l}"]))
            self.in_c(nc.scalar.dma_start(self.wmod[l][:], A[f"L{l}_wmod"]))
        for b in range(NB):
            self.in_x(nc.sync.dma_start(self.X[:, b * TB:(b + 1) * TB, :],
                                        A["L0_attn_x"][b].rearrange("(k p) d -> p k d", p=P)))
        self.in_k(nc.sync.dma_start(self.ident[:], A["k_ident"]))
        self.m_half = self.G(nc.gpsimd.memset(self.half[:], -0.5))
        self.V.need(self.in_k.mark())
        self.m_identb = self.V(nc.vector.tensor_copy(self.identb[:], self.ident[:]))

    def modulation(self):
        nc, V, S_, T = self.nc, self.V, self.S, self.T
        with ExitStack() as scope:
            ring = self.banks(scope, "mod_ps", 4)
            for l in range(2):
                S_.need(self.in_c.mark())
                silu = S_(nc.scalar.activation(self.sil[l][:], self.cT[l][:], ACT.Silu))
                V.need(silu)
                rep = V(nc.vector.tensor_copy(self.silrep[l][:],
                                              self.sil[l][:, :, None].to_broadcast([P, NB, P])))
                T.need(silu, self.in_c.mark())
                k, ps = ring.take(T)
                for i in range(6):
                    mm = nc.tensor.matmul(ps[:, i * NB:(i + 1) * NB], self.wmod[l][:, i * D:(i + 1) * D],
                                          self.sil[l][:], start=True, stop=True)
                mm = T(mm)
                V.need(mm)
                col = V(nc.vector.tensor_copy(self.mcol[l][:].rearrange("p i b -> p (i b)"), ps[:, 0:6 * NB]))
                ring.release(k, col)
                V.need(col)
                m = self.mcol[l]
                a = V(nc.vector.tensor_scalar(m[:, 1, :], m[:, 1, :], 1.0, None, ALU.add))
                a = V(nc.vector.tensor_scalar(m[:, 4, :], m[:, 4, :], 1.0, None, ALU.add))
                self.gate(m[:, 2, :], NB)
                self.m_col = self.gate(m[:, 5, :], NB)
                T.need(rep)
                for b in range(NB):
                    for lo, hi in ((0, CH), (CH, 6 * D)):
                        k, ps = ring.take(T)
                        mm = T(nc.tensor.matmul(ps[:, 0:hi - lo], self.silrep[l][:, b, :],
                                                self.wmod[l][:, lo:hi], start=True, stop=True))
                        V.need(mm)
                        row = V(nc.vector.tensor_copy(
                            self.mrow[l][:, b].rearrange("p i d -> p (i d)")[:, lo:hi], ps[:, 0:hi - lo]))
                        ring.release(k, row)
                    V.need(row)
                    r = self.mrow[l]
                    V(nc.vector.tensor_scalar(r[:, b, 1, :], r[:, b, 1, :], 1.0, None, ALU.add))
                    V(nc.vector.tensor_scalar(r[:, b, 4, :], r[:, b, 4, :], 1.0, None, ALU.add))
                    self.gate(r[:, b, 2, :], D)
                    self.m_row = self.gate(r[:, b, 5, :], D)
            self.settle()

    def gate(self, g, n):
        nc, V = self.nc, self.V
        sign, size = self.gtmp[:, 0:n], self.gtmp[:, D:D + n]
        V.need(V.last())
        V(nc.vector.tensor_scalar(sign, g, 0.0, 2.0, ALU.is_ge, ALU.mult))
        m = V(nc.vector.tensor_scalar(size, g, -1.0, None, ALU.mult))
        V.need(m)
        m = V(nc.vector.tensor_tensor(size, size, g, ALU.max))
        V.need(m)
        m = V(nc.vector.tensor_scalar(size, size, 0.25, None, ALU.max))
        V.need(m)
        return V(nc.vector.scalar_tensor_tensor(out=g, in0=sign, scalar=-1.0, in1=size, op0=ALU.add, op1=ALU.mult))

    def rstd(self, src, scale, *marks):
        nc, G = self.nc, self.G
        G.need(self.m_half, *marks)
        a = G(nc.gpsimd.tensor_scalar(self.ve[:], src, scale, EPS, ALU.mult, ALU.add))
        G.need(a)
        return G(nc.gpsimd.tensor_tensor(self.rs[:], self.ve[:], self.half[:], ALU.pow))

    def layer_norm(self, src, *marks):
        nc, V = self.nc, self.V
        V.need(*marks)
        for t in range(NT):
            m = V(nc.vector.bn_stats(self.stat[:, t, :], src[:, t, :]))
        V.need(m)
        for t in range(NT):
            m = V(nc.vector.bn_aggr(self.mv[:, t, :], self.stat[:, t, :]))
        r = self.rstd(self.mv[:, :, 1], 1.0, m)
        V.need(m, r)
        return [V(nc.vector.tensor_scalar(self.N[:, t, :], src[:, t, :], self.mv[:, t, 0:1],
                                          self.rs[:, t:t + 1], ALU.subtract, ALU.mult)) for t in range(NT)]

    def turn(self, ring, marks, scale, bias, extra=()):
        nc, S_, T, V = self.nc, self.S, self.T, self.V
        done = []
        T.need(self.in_k.mark())
        for c in range(NC):
            k, ps = ring.take(T)
            for j in range(4):
                T.need(marks[4 * c + j])
                mm = nc.tensor.transpose(ps[:, j * P:(j + 1) * P], self.N[:, 4 * c + j, :], self.ident[:])
            mm = T(mm)
            b = c // 2
            eng = (S_, V)[c % 2]
            eng.need(mm, *extra)
            dst = self.HT[:, c * CH:(c + 1) * CH]
            if eng is S_:
                m = S_(nc.scalar.activation(dst, ps[:], ACT.Identity, scale=scale(b),
                                            bias=bias(b) if bias else 0.0))
            elif bias:
                m = V(nc.vector.tensor_scalar(dst, ps[:], scale(b), bias(b), ALU.mult, ALU.add))
            else:
                m = V(nc.vector.tensor_scalar(dst, ps[:], scale(b), None, ALU.mult))
            ring.release(k, m)
            done.append(m)
        return done

    def attention(self):
        nc, A, V, S_, G, T, Q = self.nc, self.A, self.V, self.S, self.G, self.T, self.Q
        with ExitStack() as scope:
            sb = lambda n, s, d=F32: self.sb(scope, n, s, d)
            parts = nc.dram_tensor("qk_parts", (2, 3, BH, HD, S), BF16, kind="Internal").ap()
            w = sb("w_qkv", [P, 3, D])
            in_w = Arrival(scope, nc, "in_wqkv")
            for i, n in enumerate(("WqT", "WkT", "WvT")):
                in_w(nc.scalar.dma_start(w[:, i, :], A[n]))
            sel = sb("head_sum", [P, HD + 1])
            in_w(nc.scalar.dma_start(sel[:], A["k_headsum"]))
            vt = sb("v_tok", [P, BH, TB, HD])
            ox = sb("attn_out", [P, BH + 1, TB, HD])
            NS = 4
            qp = [sb(f"q_rows{s}", [P, S], BF16) for s in range(NS)]
            kp = [sb(f"k_rows{s}", [P, S], BF16) for s in range(NS)]
            va = [sb(f"v_cols{s}", [P, TB, 32]) for s in range(2)]
            pt = [sb(f"exp_scores{s}", [P, 4, CH]) for s in range(2)]
            mx = [sb(f"max_halves{s}", [P, TB, 2]) for s in range(2)]
            nm = sb("neg_max", [P, TB])
            nr = sb("neg_max_rest", [P, TB])
            ms = [sb(f"neg_max_parts{s}", [P, 3, TB], BF16) for s in range(2)]
            mt = [sb(f"neg_max_rows{s}", [3 * TB, P], BF16) for s in range(2)]
            ot = [sb(f"av_t{s}", [P, CH]) for s in range(2)]
            rc = sb("recip", [P, TB])

            KR, KM = 96, 99
            for s in range(NS):
                V(nc.vector.memset(qp[s][64:128, :], 0.0))
                V(nc.vector.memset(kp[s][64:96, :], 0.0))
                rows_set = V(nc.vector.memset(kp[s][96:128, :], 1.0))
            for s in range(2):
                a = G(nc.gpsimd.memset(va[s][:], 0.0))
                a = G(nc.gpsimd.memset(pt[s][:], 1.0))
                a = G(nc.gpsimd.memset(ot[s][:], 1.0))
            G.need(a)
            for s in range(2):
                a = G(nc.gpsimd.memset(va[s][:, :, HD:HD + 1], 1.0))
            set_up = a

            normed = self.layer_norm(self.X, self.in_x.mark())
            with ExitStack() as pre:
                ring = self.banks(pre, "pre_ps", 8)
                ht = self.turn(ring, normed, lambda b: self.mcol[0][:, 1, b:b + 1],
                               lambda b: self.mcol[0][:, 0, b:b + 1], (self.m_col,))
                p = [self.sb(pre, f"part{i}", [P, 2, TOK], BF16) for i in range(3)]
                rest = self.sb(pre, "part_rest", [P, 2, TOK])
                T.need(in_w.mark())
                wrote = {}
                to_dram = Arrival(scope, nc, "parts_out")
                for c in range(NC):
                    cs = slice(c * CH, (c + 1) * CH)
                    T.need(ht[c])
                    for side in range(2):
                        k, ps = ring.take(T)
                        mm = T(nc.tensor.matmul(ps[:], w[:, side, :], self.HT[:, cs], start=True, stop=True))
                        S_.need(mm)
                        a = S_(nc.scalar.activation(p[0][:, side, cs], ps[:], ACT.Copy))
                        V.need(a)
                        b_ = V(nc.vector.tensor_tensor(rest[:, side, cs], ps[:], p[0][:, side, cs], ALU.subtract))
                        ring.release(k, b_)
                        V.need(b_)
                        c_ = V(nc.vector.tensor_copy(p[1][:, side, cs], rest[:, side, cs]))
                        G.need(c_)
                        d_ = G(nc.gpsimd.tensor_tensor(p[2][:, side, cs], rest[:, side, cs], p[1][:, side, cs],
                                                       ALU.subtract))
                        wrote[side, c] = (a, c_, d_)
                    if c % 2:
                        b = c // 2
                        for side in range(2):
                            Q.need(*wrote[side, c], *wrote[side, c - 1])
                            for i in range(3):
                                to_dram(nc.sync.dma_start(
                                    parts[side, i, b * H:(b + 1) * H].rearrange("h d t -> (h d) t"),
                                    p[i][:, side, b * S:(b + 1) * S]))
                    k, ps = ring.take(T)
                    for j in range(4):
                        tile = 4 * c + j
                        mm = nc.tensor.matmul(ps[:, j * P:(j + 1) * P], self.HT[:, tile * P:(tile + 1) * P],
                                              w[:, 2, :], start=True, stop=True)
                    mm = T(mm)
                    S_.need(mm)
                    b, k0 = c // 2, (c % 2) * 4
                    for j in range(4):
                        v_done = S_(nc.scalar.activation(
                            vt[:, b * H:(b + 1) * H, k0 + j, :],
                            ps[:, j * P:(j + 1) * P].rearrange("p (h d) -> p h d", h=H), ACT.Copy))
                    ring.release(k, v_done)
                self.settle()
                Q.need(set_up, rows_set)
                Q.engine.wait_ge(to_dram.sem, to_dram.n)
                for t in (V, S_, G, T):
                    t.engine.wait_ge(to_dram.sem, to_dram.n)

            sc1 = scope.enter_context(nc.psum_tensor("score_q", [P, 2, CH], F32))
            sc2 = scope.enter_context(nc.psum_tensor("score_k", [P, 2, 2, CH], F32))
            avp = scope.enter_context(nc.psum_tensor("av_ps", [P, CH], F32))
            mis = scope.enter_context(nc.psum_tensor("misc_ps", [P, CH], F32))
            mtp = mis[:, 0:64].bitcast(BF16)
            op = mis[:, 128:128 + TB * 16].rearrange("p (k d) -> p k d", d=16)

            ev = lambda n, e, before=0: Event(scope, nc, n, e, before)
            loaded = [ev(f"loaded{s}", nc.sync) for s in range(NS)]
            max_in = [ev(f"max_in{s}", nc.sync) for s in range(NS)]
            s1_mm, s1_max = ev("s1_mm", nc.tensor), ev("s1_max", nc.vector)
            split = ev("max_split", nc.vector)
            m_turn, m_copy = ev("max_turn", nc.tensor), ev("max_copy", nc.vector)
            s2_mm, exped = ev("s2_mm", nc.tensor), ev("exped", nc.scalar)
            av_mm, av_out = ev("av_mm", nc.tensor, 2), ev("av_out", nc.scalar, 1)
            o_mm, o_norm = ev("o_mm", nc.tensor, 1), ev("o_norm", nc.vector, 2)
            v_put = ev("v_put", nc.gpsimd)
            ND = 12
            SC = float(HD) ** -0.5

            def load(h, s, turn):
                s2_mm.wait(nc.sync, 8 * (h - 3))
                for i in range(3):
                    loaded[s](nc.sync.dma_start(kp[s][24 * i:24 * i + 24, :], parts[1][:, bass.ds(h, 1)].rearrange("p a d t -> (p a) d t")), 16)
                    for j in range(3):
                        loaded[s](nc.sync.dma_start(qp[s][24 * i + 8 * j:24 * i + 8 * j + 8, :],
                                                    parts[0][i, bass.ds(h, 1)].rearrange("a d t -> (a d) t")), 16)

            def s1_step(h, s, turn, j):
                if j == 0:
                    loaded[s].wait(nc.tensor, 16 * ND * (turn + 1))
                qt, kh = j // 2, j % 2
                s1_max.wait(nc.tensor, 16 * h + j - 1)
                s1_mm(nc.tensor.matmul(sc1[:, j % 2, :], qp[s][0:KR, qt * P:(qt + 1) * P],
                                       kp[s][0:KR, kh * CH:(kh + 1) * CH], start=True, stop=True))

            def s1_reduce(h, s, j):
                if j == 0:
                    split.wait(nc.vector, 5 * (h - 1))
                s1_mm.wait(nc.vector, 16 * h + j + 1)
                s1_max(nc.vector.tensor_reduce(mx[s % 2][:, j // 2, j % 2:j % 2 + 1], sc1[:, j % 2, :], AX_X, ALU.max))

            def max_parts(h, s):
                z, o = mx[s % 2], ms[s % 2]
                s1_max.wait(nc.vector, 16 * h + 16)
                m_turn.wait(nc.vector, h - 1)
                split(nc.vector.tensor_reduce(nm[:], z[:], AX_X, ALU.max, negate=True))
                split.wait(nc.vector, 5 * h + 1)
                split(nc.vector.tensor_copy(o[:, 0, :], nm[:]))
                split.wait(nc.vector, 5 * h + 2)
                split(nc.vector.tensor_tensor(nr[:], nm[:], o[:, 0, :], ALU.subtract))
                split.wait(nc.vector, 5 * h + 3)
                split(nc.vector.tensor_copy(o[:, 1, :], nr[:]))
                split.wait(nc.vector, 5 * h + 4)
                split(nc.vector.tensor_tensor(o[:, 2, :], nr[:], o[:, 1, :], ALU.subtract))

            def max_turn_pe(h, s):
                split.wait(nc.tensor, 5 * h + 5)
                o_norm.wait(nc.tensor, 2 * (h - 2))
                m_turn(nc.tensor.transpose(mtp[0:3 * TB, :], ms[s % 2][:].rearrange("p a k -> p (a k)"),
                                           self.identb[:]))

            def max_copy_dve(h, s, turn):
                m_turn.wait(nc.vector, h + 1)
                sp = (s - 2) % NS
                tp = turn if s >= 2 else turn - 1
                max_in[sp].wait(nc.vector, 48 * (tp + 1))
                m_copy(nc.vector.tensor_copy(mt[s % 2][:], mtp[0:3 * TB, :]))

            def max_rows_in(h, s):
                m_copy.wait(nc.sync, h + 1)
                for i in range(3):
                    max_in[s](nc.sync.dma_start(
                        qp[s][96 + i:97 + i, :].rearrange("a (k q) -> a k q", k=TB),
                        mt[s % 2][TB * i:TB * i + TB, :]), 16)

            def put_v(h, s):
                av_mm.wait(nc.gpsimd, 4 * (h - 1))
                v_put(nc.gpsimd.tensor_copy(va[s % 2][:, :, 0:HD], vt[:, bass.ds(h, 1), :, :]
                                            .rearrange("p a k d -> p (a k) d")))

            def s2_pair(h, s, turn, r):
                if r == 0:
                    max_in[s].wait(nc.tensor, 48 * (turn + 1))
                qh, kt = r // 4, (r % 4) * 2
                exped.wait(nc.tensor, 8 * h + r - 1)
                for j in range(2):
                    mm = nc.tensor.matmul(sc2[:, r % 2, j, :], kp[s][0:KM, (kt + j) * P:(kt + j + 1) * P],
                                          qp[s][0:KM, qh * CH:(qh + 1) * CH], start=True, stop=True)
                s2_mm(mm)

            def exp_pair(h, r):
                if r % 2 == 0:
                    av_mm.wait(nc.scalar, 4 * h + r // 2 - 1)
                s2_mm.wait(nc.scalar, 8 * h + r + 1)
                exped(nc.scalar.activation(pt[(r // 2) % 2][:, (r % 2) * 2:(r % 2) * 2 + 2, :],
                                           sc2[:, r % 2], ACT.Exp, scale=SC))

            def av_quad(h, s, u):
                if u == 0:
                    v_put.wait(nc.tensor, h + 1)
                if u % 2 == 0:
                    av_out.wait(nc.tensor, 2 * h + u // 2)
                exped.wait(nc.tensor, 8 * h + 2 * u + 2)
                for j in range(4):
                    mm = nc.tensor.matmul(avp[32 * j:32 * j + 32, :], va[s % 2][:, 4 * (u % 2) + j, :],
                                          pt[u % 2][:, j, :], start=(u % 2 == 0), stop=(u % 2 == 1))
                av_mm(mm)

            def av_evac(h, qh):
                av_mm.wait(nc.scalar, 4 * h + 2 * qh + 2)
                o_mm.wait(nc.scalar, h)
                av_out(nc.scalar.activation(ot[qh][:], avp[:], ACT.Copy))

            def o_turn(h, turned):
                av_out.wait(nc.tensor, 2 * h + 2)
                m_copy.wait(nc.tensor, turned)
                o_norm.wait(nc.tensor, 2 * h)
                for k in range(TB):
                    mm = nc.tensor.matmul(op[:, k, 0:HD + 1], ot[k // 4][:, (k % 4) * P:(k % 4 + 1) * P], sel[:],
                                          start=True, stop=True)
                o_mm(mm)

            def o_divide(h):
                o_mm.wait(nc.vector, h + 1)
                o_norm(nc.vector.reciprocal(rc[:], op[:, :, HD]))
                o_norm.wait(nc.vector, 2 * h + 1)
                o_norm(nc.vector.tensor_tensor(
                    ox[:, bass.ds(h + 1, 1), :, :].rearrange("p a k d -> p (a k) d"), op[:, :, 0:HD],
                    rc[:, :, None].to_broadcast([P, TB, HD]), ALU.mult))

            def head(h, s, turn, s1=True, mturn=True, ld=True):
                t2 = turn + (s + 2) // NS
                t1 = turn + (s + 1) // NS
                if ld:
                    load(h + 3, (s + 3) % NS, turn + (s + 3) // NS)
                put_v(h, s)
                for r in range(8):
                    s2_pair(h, s, turn, r)
                    exp_pair(h, r)
                    if s1:
                        for j in (2 * r, 2 * r + 1):
                            s1_step(h + 2, (s + 2) % NS, t2, j)
                            s1_reduce(h + 2, s + 2, j)
                    if r == 1:
                        av_quad(h - 1, s - 1, 3)
                        av_evac(h - 1, 1)
                    elif r in (3, 5, 7):
                        av_quad(h, s, (r - 3) // 2)
                        if r == 5:
                            av_evac(h, 0)
                    if r == 2 and mturn:
                        max_turn_pe(h + 1, s + 1)
                        max_copy_dve(h + 1, (s + 1) % NS, t1)
                        max_rows_in(h + 1, (s + 1) % NS)
                    if r == 4:
                        o_turn(h - 1, h + 2 if mturn else BH)
                        o_divide(h - 1)
                if s1:
                    max_parts(h + 2, s + 2)

            for h in range(3):
                load(h, h, 0)
            av_quad(-1, -1, 2)
            for h in range(2):
                for j in range(16):
                    s1_step(h, h, 0, j)
                    s1_reduce(h, h, j)
                max_parts(h, h)
                if h == 0:
                    max_turn_pe(0, 0)
                    max_copy_dve(0, 0, 0)
                    max_rows_in(0, 0)
            with nc.Fori(0, BH // NS - 1) as i:
                for s in range(NS):
                    head(i * NS + s, s, i)
            for s in range(NS):
                h = BH - NS + s
                head(h, s, BH // NS - 1, s1=(h + 2 < BH), mturn=(h + 1 < BH), ld=(h + 3 < BH))
            h = BH - 1
            av_quad(h, NS - 1, 3)
            av_evac(h, 1)
            o_turn(h, BH)
            o_divide(h)

            for e in (nc.vector, nc.gpsimd):
                o_norm.wait(e, 2 * BH)
            tmp = self.N
            for b in range(NB):
                xb = self.X[:, b * TB:(b + 1) * TB, :]
                tb = tmp[:, b * TB:(b + 1) * TB, :]
                for k in range(TB):
                    a = V(nc.vector.tensor_tensor(
                        tb[:, k].rearrange("p (h d) -> p h d", h=H), ox[:, 1 + b * H:1 + (b + 1) * H, k, :],
                        self.mrow[0][:, b, 2, :].rearrange("p (h d) -> p h d", h=H), ALU.mult))
                V.need(a)
                a = V(nc.vector.tensor_tensor(xb, xb, tb, ALU.add))
            for e in (nc.tensor, nc.scalar, nc.gpsimd, nc.sync, nc.vector):
                o_norm.wait(e, 2 * BH)
            self.settle()

    def coupling(self):
        nc, A, V, S_, G, T, Q = self.nc, self.A, self.V, self.S, self.G, self.T, self.Q
        with ExitStack() as scope:
            sb = lambda n, s, d=F32: self.sb(scope, n, s, d)
            dims = {"cn": (D, D, D // 2, D // 4, 1), "gc": (D, D // 2, D // 4, 1)}
            wt, bs = {}, {}
            in_w = Arrival(scope, nc, "in_coupling")
            for net, d in dims.items():
                for i in range(1, len(d)):
                    wt[net, i] = sb(f"{net}_w{i}", [d[i - 1], d[i]])
                    in_w(nc.sync.dma_start(wt[net, i][:], A[f"{net}_w{i}"]))
                    rows = d[i] if d[i] > 1 else P
                    bs[net, i] = sb(f"{net}_b{i}", [rows, 1])
                    src = A[f"{net}_b{i}"]
                    in_w(nc.sync.dma_start(bs[net, i][:], src if d[i] > 1 else src.to_broadcast([P, 1])))
            rng = sb("range", [P, 1])
            in_w(nc.sync.dma_start(rng[:], A["adaptive_range"].to_broadcast([P, 1])))
            twist = sb("twist", [P, P])
            in_w(nc.sync.dma_start(twist[:], A["k_twist"]))
            wlast = {"cn": sb("cn_w4_rep", [D // 4, P]), "gc": sb("gc_w3_rep", [D // 4, P])}
            blast = {"cn": sb("cn_b4_half", [P, 1]), "gc": sb("gc_b3_half", [P, 1])}
            alpha, beta = sb("cpl_alpha", [P, 1]), sb("cpl_beta", [P, NB])
            mean = sb("token_sum", [P, NB])
            g1, g2, g3 = sb("ctx1", [D // 2, NB]), sb("ctx2", [D // 4, NB]), sb("ctx3", [P, NB])
            h1 = [sb(f"net1_{c}", [D, CH]) for c in range(NC)]
            h2 = [sb(f"net2_{c}", [D // 2, CH]) for c in range(NC)]
            h3 = [sb(f"net3_{c}", [D // 4, CH]) for c in range(NC)]
            cp = [sb(f"coupling_{c}", [P, CH]) for c in range(NC)]
            ring = self.banks(scope, "cpl_ps", 8)
            U = self.HT
            V.need(in_w.mark())
            for net, i in (("cn", 4), ("gc", 3)):
                V(nc.vector.tensor_copy(wlast[net][:], wt[net, i][:].to_broadcast([D // 4, P])))
                m_b = V(nc.vector.tensor_scalar(blast[net][:], bs[net, i][:], 0.5, None, ALU.mult))
            m_b = V(nc.vector.tensor_scalar(alpha[:], rng[:], 0.3, None, ALU.mult))

            normed = self.layer_norm(self.X, V.last())
            ht = self.turn(ring, normed, lambda b: self.mcol[0][:, 4, b:b + 1],
                           lambda b: self.mcol[0][:, 3, b:b + 1], (self.m_col,))
            V.need(*ht)
            for b in range(NB):
                m = V(nc.vector.tensor_reduce(mean[:, b:b + 1], U[:, b * S:(b + 1) * S], AX_X, ALU.add))
            T.need(m, in_w.mark(), m_b)
            S_.need(in_w.mark(), m_b)
            src = mean
            for i, dst in ((1, g1), (2, g2), (3, g3)):
                k, ps = ring.take(T)
                n = dst.shape[0]
                w = wlast["gc"][:] if i == 3 else wt["gc", i][:]
                mm = T(nc.tensor.matmul(ps[0:n, 0:NB], w, src[:], start=True, stop=True))
                S_.need(mm)
                if i < 3:
                    m = S_(nc.scalar.activation(dst[:], ps[0:n, 0:NB], ACT.Gelu, bias=bs["gc", i][:],
                                                scale=1.0 / S if i == 1 else 1.0))
                else:
                    m = S_(nc.scalar.activation(dst[:], ps[0:n, 0:NB], ACT.Tanh, bias=blast["gc"][:], scale=0.5))
                ring.release(k, m)
                T.need(m)
                src = dst
            V.need(m)
            m = V(nc.vector.tensor_scalar(beta[:], g3[:], rng[:], 0.7, ALU.mult, ALU.mult))
            V.need(m)
            m = V(nc.vector.tensor_scalar(beta[:], beta[:], 0.1, None, ALU.add))
            V.need(m)

            ready = [(ht[c],) for c in range(NC)]
            turned = [None] * NC
            stages = ((1, D, h1), (2, D // 2, h2), (3, D // 4, h3), (4, P, cp))
            for cycle in range(3):
                marks = [None] * NC
                for i, n, dst in stages:
                    for c in range(NC):
                        cs = slice(c * CH, (c + 1) * CH)
                        src = U[:, cs] if i == 1 else stages[i - 2][2][c][:]
                        w = wlast["cn"] if i == 4 else wt["cn", i]
                        k, ps = ring.take(T)
                        T.need(*(ready[c] if i == 1 else (marks[c],)))
                        mm = T(nc.tensor.matmul(ps[0:n, :], w[:], src, start=True, stop=True))
                        S_.need(mm)
                        if i < 4:
                            marks[c] = S_(nc.scalar.activation(dst[c][:], ps[0:n, :], ACT.Gelu, bias=bs["cn", i][:]))
                        else:
                            marks[c] = S_(nc.scalar.activation(dst[c][:], ps[0:n, :], ACT.Tanh,
                                                               bias=blast["cn"][:], scale=0.5))
                        ring.release(k, marks[c])
                for c in range(NC):
                    cs = slice(c * CH, (c + 1) * CH)
                    b = c // 2
                    k, ps = ring.take(T)
                    mm = T(nc.tensor.matmul(ps[:], twist[:], U[:, cs], start=True, stop=True))
                    V.need(marks[c])
                    m = V(nc.vector.tensor_scalar(cp[c][:], cp[c][:], alpha[:], beta[:, b:b + 1], ALU.mult, ALU.add))
                    V.need(m, mm)
                    m = V(nc.vector.tensor_tensor(cp[c][:], ps[:], cp[c][:], ALU.mult))
                    ring.release(k, m)
                    V.need(m)
                    m = V(nc.vector.tensor_tensor(U[:, cs], U[:, cs], cp[c][:], ALU.add))
                    ready[c] = (m,)
                    S_.need(m)
            for c in range(NC):
                cs = slice(c * CH, (c + 1) * CH)
                b = c // 2
                S_.need(*ready[c])
                m = S_(nc.scalar.activation(h1[c][:], U[:, cs], ACT.Copy, scale=self.mcol[0][:, 5, b:b + 1]))
                T.need(m)
                k, ps = ring.take(T)
                for j in range(4):
                    mm = nc.tensor.transpose(ps[:, j * P:(j + 1) * P], h1[c][:, j * P:(j + 1) * P], self.ident[:])
                mm = T(mm)
                V.need(mm)
                xc = self.X[:, 4 * c:4 * c + 4, :].rearrange("p k d -> p (k d)")
                m = V(nc.vector.tensor_tensor(xc, xc, ps[:], ALU.add))
                ring.release(k, m)
            self.settle()

    def mod_rows(self, dst, src, l, shift, marks):
        nc, V, G = self.nc, self.V, self.G
        done = []
        for b, (eng, e) in enumerate(((V, nc.vector), (G, nc.gpsimd))):
            ts = slice(b * TB, (b + 1) * TB)
            eng.need(self.m_row, *marks[ts])
            row = lambda i: self.mrow[l][:, b, i:i + 1, :].to_broadcast([P, TB, D])
            m = eng(e.tensor_tensor(dst[:, ts, :], src[:, ts, :], row(shift + 1), ALU.mult))
            eng.need(m)
            done += [eng(e.tensor_tensor(dst[:, ts, :], dst[:, ts, :], row(shift), ALU.add))] * TB
        return done

    def mamba(self):
        nc, A, V, S_, G, T, Q = self.nc, self.A, self.V, self.S, self.G, self.T, self.Q
        with ExitStack() as scope:
            sb = lambda n, s, d=F32: self.sb(scope, n, s, d)
            R2 = 2 * DS
            in_w = Arrival(scope, nc, "in_mamba")
            def load(name, shape, src, dt=F32):
                t = sb(name, shape, dt)
                in_w(nc.sync.dma_start(t[:], src))
                return t
            nw = load("norm_w", [P, NL], A["norm_w"])
            cw = load("conv_w", [P, NL, NBLK, KW], A["conv_w"])
            cb = load("conv_b", [P, NL, NBLK], A["conv_b"])
            dtb = load("dt_b", [P, NL, NBLK], A["dt_b"])
            dp = load("d_skip", [P, NL, NBLK], A["Dp"])
            am = load("a_log", [P, NL, NBLK, DS], A["A_log"])
            dtw = load("dt_w", [DTR, NL, DI], A["dt_wT"])
            ow = load("out_w", [P, NBLK, NL, D], A["out_wT"])
            rowsel = load("row_ident", [3 * R2, R2], A["k_rows"])
            iw = sb("in_w", [P, NL, 2 * DI])
            xw = sb("x_proj_w", [P, NBLK, NL, DTR + 3 * R2])
            for l in range(NL):
                in_w(nc.sync.dma_start(iw[:, l, :], A["in_wT"][l]))
                in_w(nc.sync.dma_start(xw[:, :, l, 0:DTR], A["xp_wT"][:, :, l, 0:DTR]))
                for r in range(3):
                    in_w(nc.sync.dma_start(xw[:, :, l, DTR + r * R2:DTR + (r + 1) * R2],
                                           A["xp_wT"][:, :, l, DTR:DTR + R2]))
            sel = sb("row_select", [3 * R2, R2, P], BF16)
            xm = sb("x_mamba", [P, NT, D])
            flat = sb("conv_in", [P, NBLK * NB * (S + KW - 1)])
            xc = flat[:].rearrange("p (k b t) -> p k b t", k=NBLK, b=NB)
            xb = sb("x_inner", [P, NBLK, NB, S])
            zs = sb("silu_z", [P, NBLK, NB, S])
            delta = sb("delta", [P, NBLK, NB, S])
            du = sb("delta_x", [P, NBLK, NB, S])
            dr = sb("delta_low", [DTR, TOK])
            bcr = sb("bc_rest", [3 * R2, CH])
            bcm = sb("bc_mid", [3 * R2, CH], BF16)
            bc = sb("bc_parts", [3 * R2, TOK], BF16)
            ddiag = sb("d_diag", [P, NBLK, P])
            beta = sb("momentum_beta", [P, S])
            bsb = [sb(f"b_row{s}", [P, S]) for s in range(2)]
            csb = [sb(f"c_row{s}", [P, S]) for s in range(2)]
            da = [sb(f"decay{s}", [P, NBLK, S]) for s in range(2)]
            tm = bsb
            mi = [flat[:, s * NBLK * S:(s + 1) * NBLK * S].rearrange("p (k t) -> p k t", k=NBLK) for s in range(2)]
            hh = self.HT[:].rearrange("p (k t) -> p k t", k=NBLK)
            yp = [self.N[:].rearrange("p a d -> p (a d)").rearrange("p (k t) -> p k t", k=NBLK)]

            V.need(in_w.mark())
            m_beta = V(nc.vector.memset(beta[:], BETA))
            m_sel = V(nc.vector.tensor_copy(sel[:], rowsel[:][:, :, None].to_broadcast([3 * R2, R2, P])))
            S_.need(in_w.mark())
            m_a = S_(nc.scalar.activation(am[:].rearrange("p l k n -> p (l k n)"),
                                          am[:].rearrange("p l k n -> p (l k n)"), ACT.Exp))
            V.need(m_a)
            m_a = V(nc.vector.tensor_scalar(am[:].rearrange("p l k n -> p (l k n)"),
                                            am[:].rearrange("p l k n -> p (l k n)"), -1.0, None, ALU.mult))
            normed = self.layer_norm(self.X, V.last())
            xm_ready = self.mod_rows(xm, self.N, 1, 0, normed)
            for l in range(NL):
                xm_ready = self.mamba_layer(l, locals(), xm_ready)
            for b, (eng, e) in enumerate(((V, nc.vector), (G, nc.gpsimd))):
                ts = slice(b * TB, (b + 1) * TB)
                eng.need(*xm_ready)
                row = self.mrow[1][:, b, 2:3, :].to_broadcast([P, TB, D])
                m = eng(e.tensor_tensor(xm[:, ts, :], xm[:, ts, :], row, ALU.mult))
                eng.need(m)
                eng(e.tensor_tensor(self.X[:, ts, :], self.X[:, ts, :], xm[:, ts, :], ALU.add))
            self.settle()

    def mamba_layer(self, l, v, xm_ready):
        nc, V, S_, G, T = self.nc, self.V, self.S, self.G, self.T
        xm, xc, xb, zs, delta, du, dr, bc = (v[n] for n in ("xm", "xc", "xb", "zs", "delta", "du", "dr", "bc"))
        iw, xw, ow, cw, cb, dtw, dtb, nw, am = (v[n] for n in ("iw", "xw", "ow", "cw", "cb", "dtw", "dtb", "nw", "am"))
        R2 = 2 * DS
        with ExitStack() as pre:
            ring = self.banks(pre, f"m{l}_ps", 4)
            wide = [pre.enter_context(nc.psum_tensor(f"m{l}_wide{k}", [P, S], F32)) for k in range(2)]
            wring = Banks(wide)
            V.need(*xm_ready)
            N, ssq = self.N, self.stat[:, :, 0]
            a = V(nc.vector.tensor_tensor(N[:], xm[:], xm[:], ALU.mult))
            V.need(a)
            a = V(nc.vector.tensor_reduce(ssq, N[:], AX_X, ALU.add))
            r = self.rstd(ssq, 1.0 / D, a)
            V.need(r)
            normed = [V(nc.vector.tensor_scalar(N[:, t, :], xm[:, t, :], self.rs[:, t:t + 1], None, ALU.mult))
                      for t in range(NT)]
            ht = self.turn(ring, normed, lambda b: nw[:, l:l + 1], None, (v["in_w"].mark(),))
            V(nc.vector.memset(xc[:, :, :, 0:KW - 1].rearrange("p a b k -> p (a b) k"), 0.0))
            T.need(v["in_w"].mark())
            moved = {}
            for c in range(NC):
                T.need(ht[c])
                b, off = c // 2, (c % 2) * CH
                for blk in range(2 * NBLK):
                    k, ps = ring.take(T)
                    mm = T(nc.tensor.matmul(ps[:], iw[:, l, blk * P:(blk + 1) * P],
                                            self.HT[:, c * CH:(c + 1) * CH], start=True, stop=True))
                    if blk < NBLK:
                        V.need(mm)
                        m = V(nc.vector.tensor_copy(xc[:, blk, b, KW - 1 + off:KW - 1 + off + CH], ps[:]))
                        moved[blk, c] = m
                    else:
                        S_.need(mm)
                        m = S_(nc.scalar.activation(zs[:, blk - NBLK, b, off:off + CH], ps[:], ACT.Silu))
                    ring.release(k, m)
            conv = {}
            for b in range(NB):
                for blk in range(NBLK):
                    V.need(moved[blk, 2 * b], moved[blk, 2 * b + 1])
                    acc = du[:, blk, b, :]
                    m = V(nc.vector.tensor_scalar(acc, xc[:, blk, b, 0:S], cw[:, l, blk, 0:1], None, ALU.mult))
                    for j in range(1, KW):
                        V.need(m)
                        m = V(nc.vector.scalar_tensor_tensor(out=acc, in0=xc[:, blk, b, j:j + S],
                                                             scalar=cw[:, l, blk, j:j + 1], in1=acc,
                                                             op0=ALU.mult, op1=ALU.add))
                    S_.need(m)
                    conv[blk, b] = S_(nc.scalar.activation(xb[:, blk, b, :], acc, ACT.Silu, bias=cb[:, l, blk:blk + 1]))
            low = []
            for c in range(NC):
                b, off = c // 2, (c % 2) * CH
                cs = slice(c * CH, (c + 1) * CH)
                T.need(*[conv[blk, b] for blk in range(NBLK)])
                k, ps = ring.take(T)
                for blk in range(NBLK):
                    mm = nc.tensor.matmul(ps[0:DTR, :], xw[:, blk, l, 0:DTR], xb[:, blk, b, off:off + CH],
                                          start=(blk == 0), stop=(blk == NBLK - 1))
                mm = T(mm)
                V.need(mm)
                low.append(V(nc.vector.tensor_copy(dr[:, cs], ps[0:DTR, :])))
                ring.release(k, low[-1])
                k, ps = ring.take(T)
                for blk in range(NBLK):
                    mm = nc.tensor.matmul(ps[0:3 * R2, :], xw[:, blk, l, DTR:DTR + 3 * R2],
                                          xb[:, blk, b, off:off + CH], start=(blk == 0), stop=(blk == NBLK - 1))
                mm = T(mm)
                S_.need(mm)
                a = S_(nc.scalar.activation(bc[:, cs], ps[0:3 * R2, :], ACT.Copy))
                V.need(a)
                rest, mid = v["bcr"], v["bcm"]
                a = V(nc.vector.tensor_tensor(rest[:], ps[0:3 * R2, :], bc[:, cs], ALU.subtract))
                ring.release(k, a)
                V.need(a)
                a = V(nc.vector.tensor_copy(mid[:], rest[:]))
                V.need(a)
                V(nc.vector.tensor_copy(bc[R2:2 * R2, cs], mid[R2:2 * R2, :]))
                bc_done = V(nc.vector.tensor_tensor(bc[2 * R2:, cs], rest[2 * R2:, :], mid[2 * R2:, :], ALU.subtract))
                V.need(bc_done)
            for b in range(NB):
                for blk in range(NBLK):
                    k, ps = wring.take(T)
                    T.need(low[2 * b], low[2 * b + 1])
                    for c in range(2):
                        mm = nc.tensor.matmul(ps[:, c * CH:(c + 1) * CH], dtw[:, l, blk * P:(blk + 1) * P],
                                              dr[:, b * S + c * CH:b * S + (c + 1) * CH], start=True, stop=True)
                    mm = T(mm)
                    bias = dtb[:, l, blk:blk + 1]
                    e, w = v["tm"]
                    out = delta[:, blk, b, :]
                    S_.need(mm, V.last())
                    a = S_(nc.scalar.activation(e[:], ps[:], ACT.Abs, bias=bias))
                    S_.need(a)
                    x_ = S_(nc.scalar.activation(e[:], e[:], ACT.Exp, scale=-1.0))
                    V.need(a)
                    m = V(nc.vector.tensor_scalar(out, ps[:], bias, 0.0, ALU.add, ALU.max))
                    wring.release(k, m)
                    V.need(x_)
                    a = V(nc.vector.tensor_scalar(w[:], e[:], 1.0, None, ALU.add))
                    V.need(a)
                    m = V(nc.vector.scalar_tensor_tensor(out=e[:], in0=w[:], scalar=-1.0, in1=e[:],
                                                         op0=ALU.add, op1=ALU.subtract))
                    S_.need(m)
                    ln = S_(nc.scalar.activation(w[:], w[:], ACT.Ln))
                    V.need(m)
                    a = V(nc.vector.tensor_tensor(out, out, e[:], ALU.subtract))
                    V.need(a, ln)
                    a = V(nc.vector.tensor_tensor(out, out, w[:], ALU.add))
                    G.need(a, conv[blk, b])
                    du_done = G(nc.gpsimd.tensor_tensor(du[:, blk, b, :], out, xb[:, blk, b, :], ALU.mult))
            for blk in range(NBLK):
                V(nc.vector.tensor_scalar(v["ddiag"][:, blk, :], self.ident[:], v["dp"][:, l, blk:blk + 1], None, ALU.mult))
            self.settle()
        for b in range(NB):
            self.mamba_scan(l, b, v)
        with ExitStack() as post:
            ring = self.banks(post, f"m{l}_out", 4)
            done = []
            for c in range(NC):
                k, ps = ring.take(T)
                for j in range(4):
                    t = 4 * c + j
                    b, off = t // TB, (t % TB) * P
                    for blk in range(NBLK):
                        mm = nc.tensor.matmul(ps[:, j * P:(j + 1) * P], zs[:, blk, b, off:off + P],
                                              ow[:, blk, l, :], start=(blk == 0), stop=(blk == NBLK - 1))
                mm = T(mm)
                V.need(mm)
                x4 = xm[:, 4 * c:4 * c + 4, :].rearrange("p k d -> p (k d)")
                m = V(nc.vector.tensor_tensor(x4, x4, ps[:], ALU.add))
                ring.release(k, m)
                done += [m] * 4
            self.settle()
        return done

    def mamba_scan(self, l, b, v):
        nc, V, S_, G, T = self.nc, self.V, self.S, self.G, self.T
        with ExitStack() as scope:
            yps = scope.enter_context(nc.psum_tensor(f"y{l}{b}", [P, NBLK, S], F32))
            bps = scope.enter_context(nc.psum_tensor(f"b{l}{b}", [P, S], F32))
            cps = scope.enter_context(nc.psum_tensor(f"c{l}{b}", [P, S], F32))
            ev = lambda n, e: Event(scope, nc, f"{n}{l}{b}", e)
            b_mm, c_mm = ev("b_mm", nc.tensor), ev("c_mm", nc.tensor)
            b_out, c_out = ev("b_out", nc.scalar), ev("c_out", nc.scalar)
            decay, mom = ev("decay", nc.scalar), ev("mom", nc.gpsimd)
            vs, hs, ys = ev("v_scan", nc.vector), ev("h_scan", nc.vector), ev("y_mul", nc.vector)
            ysum = ev("y_sum", nc.tensor)
            xb, zs, delta, du, bc, sel = (v[n] for n in ("xb", "zs", "delta", "du", "bc", "sel"))
            am, bsb, csb, da, mi, hh, yp = (v[n] for n in ("am", "bsb", "csb", "da", "mi", "hh", "yp"))
            beta = v["beta"]
            for blk in range(NBLK):
                for c in range(2):
                    nc.tensor.matmul(yps[:, blk, c * CH:(c + 1) * CH], v["ddiag"][:, blk, :],
                                     xb[:, blk, b, c * CH:(c + 1) * CH], start=True, stop=False,
                                     skip_group_check=True)

            def rows(n):
                for ps, r, done, left in ((bps, n, b_mm, b_out), (cps, n + DS, c_mm, c_out)):
                    left.wait(nc.tensor, n)
                    for c in range(2):
                        mm = nc.tensor.matmul(ps[:, c * CH:(c + 1) * CH],
                                              sel[:, bass.ds(r, 1), :].rearrange("k a p -> k (a p)"),
                                              bc[:, b * S + c * CH:b * S + (c + 1) * CH], start=True, stop=True)
                    done(mm)

            def copies(n, s):
                b_mm.wait(nc.scalar, n + 1)
                mom.wait(nc.scalar, 2 * (n - 1))
                b_out(nc.scalar.activation(bsb[s][:], bps[:], ACT.Copy))
                c_mm.wait(nc.scalar, n + 1)
                ys.wait(nc.scalar, 2 * (n - 1))
                c_out(nc.scalar.activation(csb[s][:], cps[:], ACT.Copy))
                hs.wait(nc.scalar, 2 * (n - 1))
                for blk in range(NBLK):
                    decay(nc.scalar.activation(da[s][:, blk, :], delta[:, blk, b, :], ACT.Exp,
                                               scale=am[:, l, blk, bass.ds(n, 1)]))

            def products(n, s):
                b_out.wait(nc.gpsimd, n + 1)
                hs.wait(nc.gpsimd, 2 * (n - 1))
                for blk in range(NBLK):
                    mom(nc.gpsimd.tensor_tensor(mi[s][:, blk, :], du[:, blk, b, :], bsb[s][:], ALU.mult))

            def scans(n, s):
                for blk in range(NBLK):
                    mom.wait(nc.vector, 2 * n + blk + 1)
                    vs(nc.vector.tensor_tensor_scan(mi[s][:, blk, :], beta[:], mi[s][:, blk, :], 0.0, ALU.mult, ALU.add))
                for blk in range(NBLK):
                    vs.wait(nc.vector, 2 * n + blk + 1)
                    decay.wait(nc.vector, 2 * n + blk + 1)
                    hs(nc.vector.tensor_tensor_scan(hh[:, blk, :], da[s][:, blk, :], mi[s][:, blk, :], 0.0,
                                                    ALU.mult, ALU.add))
                c_out.wait(nc.vector, n + 1)
                for blk in range(NBLK):
                    hs.wait(nc.vector, 2 * n + blk + 1)
                    ysum.wait(nc.vector, n)
                    ys(nc.vector.tensor_tensor(yp[0][:, blk, :], hh[:, blk, :], csb[s][:], ALU.mult))

            def sums(n, last=False):
                for blk in range(NBLK):
                    ys.wait(nc.tensor, 2 * n + blk + 1)
                    for c in range(2):
                        mm = nc.tensor.matmul(yps[:, blk, c * CH:(c + 1) * CH], self.ident[:],
                                              yp[0][:, blk, c * CH:(c + 1) * CH], start=False, stop=last,
                                              skip_group_check=True)
                ysum(mm)

            def state(n, s, last=False):
                if not last:
                    rows(n + 1)
                copies(n, s)
                products(n, s)
                scans(n, s)
                sums(n, last)

            rows(0)
            with nc.Fori(0, DS // 2 - 1) as i:
                for s in range(2):
                    state(2 * i + s, s)
            state(DS - 2, 0)
            state(DS - 1, 1, True)
            ysum.wait(nc.vector, DS)
            for blk in range(NBLK):
                V(nc.vector.tensor_tensor(zs[:, blk, b, :], zs[:, blk, b, :], yps[:, blk, :], ALU.mult))
            self.settle()

    def experts(self):
        nc, A, V, S_, G, T, Q = self.nc, self.A, self.V, self.S, self.G, self.T, self.Q
        with ExitStack() as scope:
            sb = lambda n, s, d=F32: self.sb(scope, n, s, d)
            in_w = Arrival(scope, nc, "in_experts")
            gam, bet = sb("ln_gamma", [P, 1]), sb("ln_beta", [P, 1])
            rw, iota = sb("router_w", [P, E]), sb("iota", [P, E])
            sgu, sdn = sb("shared_gate_up", [P, 2 * P]), sb("shared_down", [P, D])
            for t, n in ((gam, "ln_gamma"), (bet, "ln_beta"), (rw, "router_w"), (iota, "k_iota"),
                         (sgu, "shared_gate_up_w"), (sdn, "shared_down_w")):
                in_w(nc.scalar.dma_start(t[:], A[n]))
            gu = [sb(f"gate_up{s}", [P, 2 * FF]) for s in range(2)]
            dn = [sb(f"down{s}", [P, FB, D]) for s in range(2)]
            hm = sb("moe_in", [P, NT, D])
            acc = sb("moe_out", [P, NT, D])
            lg = sb("logits", [P, NT, E])
            top = sb("top_values", [P, NT, 8])
            idx = sb("top_index", [P, NT, 8], U32)
            idf = sb("top_index_f", [P, NT, 8])
            comb = sb("combine", [P, E + 1, NT])
            e2, w1, w2 = sb("exp_second", [P, NT]), sb("weight1", [P, NT]), sb("weight2", [P, NT])
            mk = [sb(f"mask{i}", [P, NT, E]) for i in range(2)]
            gc = [sb(f"gate{i}", [P, CH]) for i in range(2)]
            sg = [sb(f"silu_gate{i}", [P, CH]) for i in range(2)]
            act = [sb(f"hidden{i}", [P, FB, CH]) for i in range(2)]

            got = [Event(scope, nc, f"weights_in{s}", nc.sync) for s in range(2)]
            gu_mm = Event(scope, nc, "gu_mm", nc.tensor)
            clip, gate, hid = (Event(scope, nc, n, e) for n, e in
                               (("clip", nc.vector), ("gate_out", nc.scalar), ("hid", nc.vector)))
            dn_mm = Event(scope, nc, "dn_mm", nc.tensor, 1)
            summed = Event(scope, nc, "summed", nc.vector, 4)

            def fetch(e, s):
                dn_mm.wait(nc.sync, NC * (e - 1))
                got[s](nc.sync.dma_start(gu[s][:], A["gate_up_w"][bass.ds(e, 1)].rearrange("a d f -> (a d) f")), 16)
                got[s](nc.sync.dma_start(dn[s][:], A["down_w"][bass.ds(e, 1)].rearrange("a p k d -> (a p) k d")), 16)

            normed = self.layer_norm(self.X, V.last())
            h_ready = self.mod_rows(hm, self.N, 1, 3, normed)
            G.need(*h_ready)
            G(nc.gpsimd.memset(comb[:, 0, :], 0.0))
            for i in range(2):
                m_zero = G(nc.gpsimd.memset(act[i][:], 0.0))
            m_zero = G(nc.gpsimd.memset(dn[1][:], 0.0))
            normed = self.layer_norm(hm, *h_ready)
            with ExitStack() as pre:
                ring = self.banks(pre, "moe_ps", 8)
                S_.need(in_w.mark())
                ht = self.turn(ring, normed, lambda b: gam[:], lambda b: bet[:], (in_w.mark(),))
                T.need(in_w.mark(), *ht)
                k, ps = ring.take(T)
                for t in range(NT):
                    mm = nc.tensor.matmul(ps[:, t * E:(t + 1) * E], self.HT[:, t * P:(t + 1) * P], rw[:],
                                          start=True, stop=True)
                mm = T(mm)
                V.need(mm)
                m = V(nc.vector.tensor_copy(lg[:].rearrange("p t e -> p (t e)"), ps[:, 0:NT * E]))
                ring.release(k, m)
                V.need(m)
                for t in range(NT):
                    m = V(nc.vector.max(top[:, t, :], lg[:, t, :]))
                V.need(m)
                for t in range(NT):
                    m = V(nc.vector.max_index(idx[:, t, :], top[:, t, :], lg[:, t, :]))
                d = V(nc.vector.tensor_tensor(e2[:], top[:, :, 1], top[:, :, 0], ALU.subtract))
                S_.need(d)
                x_ = S_(nc.scalar.activation(e2[:], e2[:], ACT.Exp))
                V.need(m)
                i_ = V(nc.vector.tensor_copy(idf[:].rearrange("p t e -> p (t e)"), idx[:].rearrange("p t e -> p (t e)")))
                V.need(x_)
                m = V(nc.vector.tensor_scalar(w2[:], e2[:], 1.0, None, ALU.add))
                V.need(m)
                m = V(nc.vector.reciprocal(w1[:], w2[:]))
                V.need(m, i_)
                m = V(nc.vector.tensor_tensor(w2[:], e2[:], w1[:], ALU.mult))
                V.need(m)
                for i, w in ((0, w1), (1, w2)):
                    m = V(nc.vector.tensor_tensor(mk[i][:], idf[:, :, i:i + 1].to_broadcast([P, NT, E]),
                                                  iota[:][:, None, :].to_broadcast([P, NT, E]), ALU.is_equal))
                    V.need(m)
                    m = V(nc.vector.tensor_tensor(mk[i][:], mk[i][:], w[:][:, :, None].to_broadcast([P, NT, E]), ALU.mult))
                V.need(m)
                m_comb = V(nc.vector.tensor_tensor(comb[:, 1:, :].rearrange("p e t -> p t e"), mk[0][:], mk[1][:], ALU.add))
                for c in range(NC):
                    cs = slice(c * CH, (c + 1) * CH)
                    kg, pg = ring.take(T)
                    mg = T(nc.tensor.matmul(pg[:], sgu[:, 0:P], self.HT[:, cs], start=True, stop=True))
                    ku, pu = ring.take(T)
                    mu = T(nc.tensor.matmul(pu[:], sgu[:, P:2 * P], self.HT[:, cs], start=True, stop=True))
                    V.need(mg, S_.last())
                    m = V(nc.vector.tensor_scalar(gc[0][:], pg[:], -10.0, 10.0, ALU.max, ALU.min))
                    ring.release(kg, m)
                    S_.need(m)
                    s = S_(nc.scalar.activation(sg[0][:], gc[0][:], ACT.Silu))
                    V.need(mu, s, T.last())
                    m = V(nc.vector.tensor_tensor(sg[1][:], sg[0][:], pu[:], ALU.mult))
                    ring.release(ku, m)
                    T.need(m)
                    kd, pd = ring.take(T)
                    for j in range(4):
                        mm = nc.tensor.matmul(pd[:, j * P:(j + 1) * P], sg[1][:, j * P:(j + 1) * P], sdn[:],
                                              start=True, stop=True)
                    mm = T(mm)
                    V.need(mm)
                    m = V(nc.vector.tensor_copy(acc[:, 4 * c:4 * c + 4, :].rearrange("p k d -> p (k d)"), pd[:]))
                    ring.release(kd, m)
                self.settle()

            gups = scope.enter_context(nc.psum_tensor("gate_up_ps", [P, 3, 2, CH], F32))
            dps = scope.enter_context(nc.psum_tensor("down_ps", [P, 2, CH], F32))
            Q.need(m_zero)

            def step_up(u, i, s, c, f, kf, behind):
                st = FB * u + f
                if c == 0 and f == 0:
                    got[s].wait(nc.tensor, 32 * (i + 1))
                hid.wait(nc.tensor, st - behind)
                for j in range(2):
                    mm = nc.tensor.matmul(gups[:, kf, j, :], gu[s][:, j * FF + f * P:j * FF + (f + 1) * P],
                                          self.HT[:, c * CH:(c + 1) * CH], start=True, stop=True)
                gu_mm(mm)
                k2 = f % 2
                gu_mm.wait(nc.vector, st + 1)
                gate.wait(nc.vector, st - 1)
                clip(nc.vector.tensor_scalar(gc[k2][:], gups[:, kf, 0, :], -10.0, 10.0, ALU.max, ALU.min))
                clip.wait(nc.scalar, st + 1)
                hid.wait(nc.scalar, st - 1)
                gate(nc.scalar.activation(sg[k2][:], gc[k2][:], ACT.Silu))

            def step_hid(u, c, f, kf):
                st = FB * u + f
                gate.wait(nc.vector, st + 1)
                dn_mm.wait(nc.vector, u - 1)
                hid(nc.vector.tensor_tensor(act[c % 2][:, f, :], sg[f % 2][:], gups[:, kf, 1, :], ALU.mult))

            def down(u, s, c):
                hid.wait(nc.tensor, FB * (u + 1))
                summed.wait(nc.tensor, 4 * (u - 1))
                for j in range(4):
                    for f in range(FB):
                        mm = nc.tensor.matmul(dps[:, c % 2, j * P:(j + 1) * P], act[c % 2][:, f, j * P:(j + 1) * P],
                                              dn[s][:, f, :], start=(f == 0), stop=(f == FB - 1))
                dn_mm(mm)

            def add_up(u, e1, c):
                dn_mm.wait(nc.vector, u + 1)
                for j in range(4):
                    t = 4 * c + j
                    summed.wait(nc.vector, 4 * u)
                    summed(nc.vector.scalar_tensor_tensor(
                        out=acc[:, t, :], in0=dps[:, c % 2, j * P:(j + 1) * P],
                        scalar=comb[:, bass.ds(e1, 1), t], in1=acc[:, t, :], op0=ALU.mult, op1=ALU.add))

            def body(i, experts, fetch_next):
                k = 0
                late = None
                for s in range(2):
                    e = experts[s]
                    for c in range(NC):
                        u = NC * e + c
                        for f in range(FB):
                            step_up(u, i, s, c, f, k % 3, 1 if k < 2 else 2)
                            if late:
                                step_hid(*late)
                            late = (u, c, f, k % 3)
                            if f == 1:
                                down(u - 1, s if c else 1 - s, (c - 1) % NC)
                                add_up(u - 1, e + 1 if c else e, (c - 1) % NC)
                                if c == 0 and fetch_next[s]:
                                    fetch(e + 1, 1 - s)
                            k += 1
                step_hid(*late)

            fetch(0, 0)
            with nc.Fori(0, E // 2 - 1) as i:
                body(i, (2 * i, 2 * i + 1), (True, True))
            body(E // 2 - 1, (E - 2, E - 1), (True, False))
            u = NC * E - 1
            down(u, 1, NC - 1)
            add_up(u, E, NC - 1)
            summed.wait(nc.vector, 4 * NC * E)
            summed.wait(nc.gpsimd, 4 * NC * E)
            for b, (eng, e) in enumerate(((V, nc.vector), (G, nc.gpsimd))):
                ts = slice(b * TB, (b + 1) * TB)
                row = self.mrow[1][:, b, 5:6, :].to_broadcast([P, TB, D])
                m = eng(e.tensor_tensor(acc[:, ts, :], acc[:, ts, :], row, ALU.mult))
                eng.need(m)
                eng(e.tensor_tensor(self.X[:, ts, :], self.X[:, ts, :], acc[:, ts, :], ALU.add))
            self.settle()

    def store(self):
        nc, Q = self.nc, self.Q
        with ExitStack() as scope:
            stored = Arrival(scope, nc, "stored")
            for b in range(NB):
                stored(nc.sync.dma_start(self.out[b].rearrange("(k p) d -> p k d", p=P),
                                         self.X[:, b * TB:(b + 1) * TB, :]))
            nc.sync.wait_ge(stored.sem, stored.n)


_NAMES = ["WqT", "WkT", "WvT", "cn_w1", "cn_w2", "cn_w3", "cn_w4", "cn_b1", "cn_b2", "cn_b3", "cn_b4",
          "gc_w1", "gc_w2", "gc_w3", "gc_b1", "gc_b2", "gc_b3"]


def _layout(inputs):
    f = {k: np.ascontiguousarray(v) for k, v in inputs.items()}
    a = {"L0_attn_x": f["L0_attn_x"]}
    for l in range(2):
        a[f"cT{l}"] = f[f"L{l}_c"].T
        a[f"L{l}_wmod"] = f[f"L{l}_wmod"]
    for n in "qkv":
        a[f"W{n}T"] = f[f"L0_attn_W{n}"].T
    for net, layers in (("cn", 4), ("gc", 3)):
        for i in range(1, layers + 1):
            a[f"{net}_w{i}"] = f[f"L0_ffn_{net}_w{i}"]
            a[f"{net}_b{i}"] = f[f"L0_ffn_{net}_b{i}"][:, None]
    a["adaptive_range"] = f["L0_ffn_adaptive_range"][:, None]
    m = {k[8:]: f[k] for k in f if k.startswith("L1_attn_")}
    a["norm_w"] = m["norm_w"].T
    a["in_wT"] = m["in_proj_w"].transpose(0, 2, 1)
    a["conv_w"] = m["conv_w"].reshape(NL, NBLK, P, KW).transpose(2, 0, 1, 3)
    a["conv_b"] = m["conv_b"].reshape(NL, NBLK, P).transpose(2, 0, 1)
    a["xp_wT"] = m["x_proj_w"].transpose(2, 0, 1).reshape(NBLK, P, NL, DTR + 2 * DS).transpose(1, 0, 2, 3)
    a["dt_wT"] = m["dt_w"].transpose(2, 0, 1)
    a["dt_b"] = m["dt_b"].reshape(NL, NBLK, P).transpose(2, 0, 1)
    a["A_log"] = m["A_log"].reshape(NL, NBLK, P, DS).transpose(2, 0, 1, 3)
    a["Dp"] = m["Dp"].reshape(NL, NBLK, P).transpose(2, 0, 1)
    a["out_wT"] = m["out_w"].transpose(2, 0, 1).reshape(NBLK, P, NL, D).transpose(1, 0, 2, 3)
    a["ln_gamma"] = f["L1_ffn_ln_gamma"][:, None]
    a["ln_beta"] = f["L1_ffn_ln_beta"][:, None]
    a["router_w"] = f["L1_ffn_router_w"]
    a["gate_up_w"] = f["L1_ffn_gate_up_w"]
    a["down_w"] = f["L1_ffn_down_w"].reshape(E, FB, P, D).transpose(0, 2, 1, 3)
    a["shared_gate_up_w"] = f["L1_ffn_shared_gate_up_w"]
    a["shared_down_w"] = f["L1_ffn_shared_down_w"]
    eye = np.eye(P, dtype=np.float32)
    a["k_ident"] = eye
    heads = np.zeros((4, 32, HD + 1), np.float32)
    heads[:, np.arange(HD + 1), np.arange(HD + 1)] = 1.0
    a["k_headsum"] = heads.reshape(P, HD + 1)
    twist = np.zeros((P, P), np.float32)
    for to, frm, sign in ((0, 2, 1.0), (1, 3, -1.0), (2, 0, -1.0), (3, 1, 1.0)):
        twist[32 * frm + np.arange(32), 32 * to + np.arange(32)] = sign
    a["k_twist"] = twist
    a["k_rows"] = np.tile(np.eye(2 * DS, dtype=np.float32), (3, 1))
    a["k_iota"] = np.tile(np.arange(E, dtype=np.float32), (P, 1))
    return {k: np.ascontiguousarray(v) for k, v in a.items()}


def kernel(**inputs):
    import concourse.bacc as bacc
    from concourse.bass_utils import run_bass_kernel_spmd

    nc = bacc.Bacc("TRN2", target_bir_lowering=False, num_devices=1)
    arrays = _layout(inputs)
    args = {n: nc.dram_tensor(f"in_{n}", a.shape, mybir.dt.from_np(a.dtype), kind="ExternalInput").ap()
            for n, a in arrays.items()}
    out = nc.dram_tensor("out", (NB, S, D), F32, kind="ExternalOutput").ap()
    build(nc, args, out)
    r = run_bass_kernel_spmd(nc, [{f"in_{n}": a for n, a in arrays.items()}], core_ids=[0])
    return r.results[0]["out"]
```

```python
from contextlib import ExitStack
from itertools import count

import numpy as np

import concourse.bass as bass
from concourse import mybir

F32 = mybir.dt.float32
BF16 = mybir.dt.bfloat16
U32 = mybir.dt.uint32
ALU = mybir.AluOpType
ACT = mybir.ActivationFunctionType
AX_X = mybir.AxisListType.X

P = 128
NB = 2
S = 1024
D = 128
TOK = NB * S
NT = TOK // P
TB = S // P
CH = 512
NC = TOK // CH
H, HD = 16, 8
BH = NB * H
DI, DS, DTR, KW = 256, 16, 8, 4
NBLK = DI // P
NL = 2
E, FF = 8, 512
FB = FF // P
EPS = 1e-5
BETA = 0.6


_keys = count()


class Track:

    def __init__(self, ctx, nc, engine, name):
        self.engine = engine
        self.sem = ctx.enter_context(nc.semaphore(f"done_{name}"))
        self.n = 0
        self.key = next(_keys)
        self.seen = {}

    def __call__(self, instruction):
        instruction.then_inc(self.sem, 1)
        self.n += 1
        return (self.sem, self.n, self.key)

    def need(self, *marks):
        for mark in marks:
            if mark is None:
                continue
            sem, n, key = mark
            if self.seen.get(key, 0) < n:
                self.engine.wait_ge(sem, n)
                self.seen[key] = n

    def last(self):
        return (self.sem, self.n, self.key) if self.n else None


class Arrival:

    def __init__(self, ctx, nc, name):
        self.sem = ctx.enter_context(nc.semaphore(name))
        self.n = 0
        self.key = next(_keys)

    def __call__(self, instruction):
        instruction.then_inc(self.sem, 16)
        self.n += 16

    def mark(self):
        return (self.sem, self.n, self.key)


class Event:

    def __init__(self, ctx, nc, name, engine, before=0, credit=32):
        self.sem = ctx.enter_context(nc.semaphore(name))
        self.credit = credit
        engine.sem_inc(self.sem, credit - before)

    def __call__(self, instruction, by=1):
        instruction.then_inc(self.sem, by)
        return instruction

    def wait(self, engine, count):
        engine.wait_ge(self.sem, count + self.credit)


class Banks:

    def __init__(self, tensors):
        self.tensors = tensors
        self.free = [()] * len(tensors)
        self.at = 0

    def take(self, writer):
        k = self.at % len(self.tensors)
        self.at += 1
        writer.need(*self.free[k])
        return k, self.tensors[k]

    def release(self, k, *marks):
        self.free[k] = marks


def build(nc, A, out):
    ctx = ExitStack()
    with ctx:
        V = Track(ctx, nc, nc.vector, "vector")
        S_ = Track(ctx, nc, nc.scalar, "scalar")
        G = Track(ctx, nc, nc.gpsimd, "gpsimd")
        T = Track(ctx, nc, nc.tensor, "tensor")
        Q = Track(ctx, nc, nc.sync, "sync")
        K = Kernel(nc, ctx, A, out, V, S_, G, T, Q)
        K.constants()
        K.modulation()
        K.attention()
        K.coupling()
        K.mamba()
        K.experts()
        K.store()


class Kernel:
    def __init__(self, nc, ctx, A, out, V, S_, G, T, Q):
        self.nc, self.ctx, self.A, self.out = nc, ctx, A, out
        self.V, self.S, self.G, self.T, self.Q = V, S_, G, T, Q
        self.tracks = (V, S_, G, T)
        self.serial = 0

    def sb(self, scope, name, shape, dt=F32):
        return scope.enter_context(self.nc.sbuf_tensor(name, shape, dt))

    def banks(self, scope, name, n, dt=F32):
        return Banks([scope.enter_context(self.nc.psum_tensor(f"{name}{k}", [P, CH], dt)) for k in range(n)])

    def settle(self):
        for t in self.tracks + (self.Q,):
            t.need(*[o.last() for o in self.tracks])

    def constants(self):
        nc, A, ctx = self.nc, self.A, self.ctx
        sb = lambda n, s, d=F32: self.sb(ctx, n, s, d)
        self.X = sb("x", [P, NT, D])
        self.HT = sb("h_t", [P, TOK])
        self.N = sb("normed", [P, NT, D])
        self.ident = sb("ident", [P, P])
        self.identb = sb("identb", [P, P], BF16)
        self.half = sb("minus_half", [P, NT])
        self.stat = sb("bn_parts", [P, NT, 6])
        self.mv = sb("mean_var", [P, NT, 2])
        self.ve = sb("var_eps", [P, NT])
        self.rs = sb("rstd", [P, NT])
        self.cT = [sb(f"c_t{l}", [P, NB]) for l in range(2)]
        self.sil = [sb(f"silu_c{l}", [P, NB]) for l in range(2)]
        self.silrep = [sb(f"silu_rep{l}", [P, NB, P]) for l in range(2)]
        self.wmod = [sb(f"wmod{l}", [P, 6 * D]) for l in range(2)]
        self.mcol = [sb(f"mod_col{l}", [P, 6, NB]) for l in range(2)]
        self.mrow = [sb(f"mod_row{l}", [P, NB, 6, D]) for l in range(2)]
        self.gtmp = sb("gate_tmp", [P, 2 * D])

        self.in_x = Arrival(ctx, nc, "in_x")
        self.in_c = Arrival(ctx, nc, "in_c")
        self.in_k = Arrival(ctx, nc, "in_k")
        for l in range(2):
            self.in_c(nc.scalar.dma_start(self.cT[l][:], A[f"cT{l}"]))
            self.in_c(nc.scalar.dma_start(self.wmod[l][:], A[f"L{l}_wmod"]))
        for b in range(NB):
            self.in_x(nc.sync.dma_start(self.X[:, b * TB:(b + 1) * TB, :],
                                        A["L0_attn_x"][b].rearrange("(k p) d -> p k d", p=P)))
        self.in_k(nc.sync.dma_start(self.ident[:], A["k_ident"]))
        self.m_half = self.G(nc.gpsimd.memset(self.half[:], -0.5))
        self.V.need(self.in_k.mark())
        self.m_identb = self.V(nc.vector.tensor_copy(self.identb[:], self.ident[:]))

    def modulation(self):
        nc, V, S_, T = self.nc, self.V, self.S, self.T
        with ExitStack() as scope:
            ring = self.banks(scope, "mod_ps", 4)
            for l in range(2):
                S_.need(self.in_c.mark())
                silu = S_(nc.scalar.activation(self.sil[l][:], self.cT[l][:], ACT.Silu))
                V.need(silu)
                rep = V(nc.vector.tensor_copy(self.silrep[l][:],
                                              self.sil[l][:, :, None].to_broadcast([P, NB, P])))
                T.need(silu, self.in_c.mark())
                k, ps = ring.take(T)
                for i in range(6):
                    mm = nc.tensor.matmul(ps[:, i * NB:(i + 1) * NB], self.wmod[l][:, i * D:(i + 1) * D],
                                          self.sil[l][:], start=True, stop=True)
                mm = T(mm)
                V.need(mm)
                col = V(nc.vector.tensor_copy(self.mcol[l][:].rearrange("p i b -> p (i b)"), ps[:, 0:6 * NB]))
                ring.release(k, col)
                V.need(col)
                m = self.mcol[l]
                a = V(nc.vector.tensor_scalar(m[:, 1, :], m[:, 1, :], 1.0, None, ALU.add))
                a = V(nc.vector.tensor_scalar(m[:, 4, :], m[:, 4, :], 1.0, None, ALU.add))
                self.gate(m[:, 2, :], NB)
                self.m_col = self.gate(m[:, 5, :], NB)
                T.need(rep)
                for b in range(NB):
                    for lo, hi in ((0, CH), (CH, 6 * D)):
                        k, ps = ring.take(T)
                        mm = T(nc.tensor.matmul(ps[:, 0:hi - lo], self.silrep[l][:, b, :],
                                                self.wmod[l][:, lo:hi], start=True, stop=True))
                        V.need(mm)
                        row = V(nc.vector.tensor_copy(
                            self.mrow[l][:, b].rearrange("p i d -> p (i d)")[:, lo:hi], ps[:, 0:hi - lo]))
                        ring.release(k, row)
                    V.need(row)
                    r = self.mrow[l]
                    V(nc.vector.tensor_scalar(r[:, b, 1, :], r[:, b, 1, :], 1.0, None, ALU.add))
                    V(nc.vector.tensor_scalar(r[:, b, 4, :], r[:, b, 4, :], 1.0, None, ALU.add))
                    self.gate(r[:, b, 2, :], D)
                    self.m_row = self.gate(r[:, b, 5, :], D)
            self.settle()

    def gate(self, g, n):
        nc, V = self.nc, self.V
        sign, size = self.gtmp[:, 0:n], self.gtmp[:, D:D + n]
        V.need(V.last())
        V(nc.vector.tensor_scalar(sign, g, 0.0, 2.0, ALU.is_ge, ALU.mult))
        m = V(nc.vector.tensor_scalar(size, g, -1.0, None, ALU.mult))
        V.need(m)
        m = V(nc.vector.tensor_tensor(size, size, g, ALU.max))
        V.need(m)
        m = V(nc.vector.tensor_scalar(size, size, 0.25, None, ALU.max))
        V.need(m)
        return V(nc.vector.scalar_tensor_tensor(out=g, in0=sign, scalar=-1.0, in1=size, op0=ALU.add, op1=ALU.mult))

    def rstd(self, ts, src, scale, *marks):
        nc, G = self.nc, self.G
        G.need(self.m_half, *marks)
        a = G(nc.gpsimd.tensor_scalar(self.ve[:, ts], src, scale, EPS, ALU.mult, ALU.add))
        G.need(a)
        return G(nc.gpsimd.tensor_tensor(self.rs[:, ts], self.ve[:, ts], self.half[:, ts], ALU.pow))

    def layer_norm(self, src, marks=(None,) * NT):
        nc, V, G = self.nc, self.V, self.G
        roots = []
        for b in range(NB):
            tiles = range(b * TB, (b + 1) * TB)
            for t in tiles:
                V.need(marks[t])
                m = V(nc.vector.bn_stats(self.stat[:, t, :], src[:, t, :]))
            V.need(m)
            for t in tiles:
                m = V(nc.vector.bn_aggr(self.mv[:, t, :], self.stat[:, t, :]))
            roots.append(self.rstd(slice(b * TB, (b + 1) * TB), self.mv[:, b * TB:(b + 1) * TB, 1], 1.0, m))
        V.need(m)
        normed = []
        for t in range(NT):
            V.need(roots[t // TB])
            normed.append(V(nc.vector.tensor_scalar(self.N[:, t, :], src[:, t, :], self.mv[:, t, 0:1],
                                                    self.rs[:, t:t + 1], ALU.subtract, ALU.mult)))
        return normed

    def parts(self):
        cuts = (0, TB, 3 * TB // 2, NT)
        return [(t, e, slice(at, to), at // TB) for t, e, at, to in
                zip((self.V, self.V, self.G), (self.nc.vector, self.nc.vector, self.nc.gpsimd), cuts, cuts[1:])]

    def add_gated(self, src, l, i, marks):
        done = []
        for eng, e, ts, b in self.parts():
            n = ts.stop - ts.start
            eng.need(*marks[ts])
            row = self.mrow[l][:, b, i:i + 1, :].to_broadcast([P, n, D])
            m = eng(e.tensor_tensor(src[:, ts, :], src[:, ts, :], row, ALU.mult))
            eng.need(m)
            done += [eng(e.tensor_tensor(self.X[:, ts, :], self.X[:, ts, :], src[:, ts, :], ALU.add))] * n
        return done

    def turn(self, ring, marks, scale, bias, extra=(), to=None):
        nc, S_, T, V = self.nc, self.S, self.T, self.V
        done = []
        T.need(self.in_k.mark())
        for c in range(NC):
            k, ps = ring.take(T)
            for j in range(4):
                T.need(marks[4 * c + j])
                mm = nc.tensor.transpose(ps[:, j * P:(j + 1) * P], self.N[:, 4 * c + j, :], self.ident[:])
            mm = T(mm)
            b = c // 2
            eng = (S_, V)[c % 2]
            eng.need(mm, *extra)
            dst = to(c) if to else self.HT[:, c * CH:(c + 1) * CH]
            if eng is S_:
                m = S_(nc.scalar.activation(dst, ps[:], ACT.Identity, scale=scale(b),
                                            bias=bias(b) if bias else 0.0))
            elif bias:
                m = V(nc.vector.tensor_scalar(dst, ps[:], scale(b), bias(b), ALU.mult, ALU.add))
            else:
                m = V(nc.vector.tensor_scalar(dst, ps[:], scale(b), None, ALU.mult))
            ring.release(k, m)
            done.append(m)
        return done

    def attention(self):
        nc, A, V, S_, G, T, Q = self.nc, self.A, self.V, self.S, self.G, self.T, self.Q
        with ExitStack() as scope:
            sb = lambda n, s, d=F32: self.sb(scope, n, s, d)
            parts = nc.dram_tensor("qk_parts", (2, 3, BH, HD, S), BF16, kind="Internal").ap()
            w = sb("w_qkv", [P, 3, D])
            in_w = Arrival(scope, nc, "in_wqkv")
            for i, n in enumerate(("WqT", "WkT", "WvT")):
                in_w(nc.scalar.dma_start(w[:, i, :], A[n]))
            sel = sb("group_sum", [P, 32])
            in_w(nc.scalar.dma_start(sel[:], A["k_groupsum"]))
            vt = sb("v_tok", [P, BH, TB, HD])
            ox = sb("attn_out", [P, BH + 2, TB, HD])
            NS = 4
            qp = [sb(f"q_rows{s}", [P, S], BF16) for s in range(NS)]
            kp = [sb(f"k_rows{s}", [P, S], BF16) for s in range(NS)]
            va = [sb(f"v_cols{s}", [P, TB, 32]) for s in range(2)]
            pt = [sb(f"exp_scores{s}", [P, 4, CH]) for s in range(2)]
            mx = [sb(f"max_halves{s}", [P, TB, 2]) for s in range(2)]
            nm = sb("neg_max", [P, TB])
            nr = sb("neg_max_rest", [P, TB])
            ms = [sb(f"neg_max_parts{s}", [P, 3, TB], BF16) for s in range(2)]
            mt = [sb(f"neg_max_rows{s}", [3 * TB, P], BF16) for s in range(2)]
            ot = [sb(f"av_t{s}", [P, CH]) for s in range(2)]
            rc = [sb(f"recip{s}", [P, 4, 2]) for s in range(2)]

            KR, KM = 96, 99
            for s in range(NS):
                V(nc.vector.memset(qp[s][64:128, :], 0.0))
                V(nc.vector.memset(kp[s][64:96, :], 0.0))
                rows_set = V(nc.vector.memset(kp[s][96:128, :], 1.0))
            for s in range(2):
                a = G(nc.gpsimd.memset(va[s][:], 0.0))
                a = G(nc.gpsimd.memset(pt[s][:], 1.0))
                a = G(nc.gpsimd.memset(ot[s][:], 1.0))
            G.need(a)
            for s in range(2):
                a = G(nc.gpsimd.memset(va[s][:, :, 16 * s + HD:16 * s + HD + 1], 1.0))
            set_up = a

            normed = self.layer_norm(self.X, (self.in_x.mark(),) * NT)
            with ExitStack() as pre:
                ring = self.banks(pre, "pre_ps", 8)
                ht = self.turn(ring, normed, lambda b: self.mcol[0][:, 1, b:b + 1],
                               lambda b: self.mcol[0][:, 0, b:b + 1], (self.m_col,))
                p = [self.sb(pre, f"part{i}", [P, 2, TOK], BF16) for i in range(3)]
                rest = self.sb(pre, "part_rest", [P, 2, TOK])
                T.need(in_w.mark())
                wrote = {}
                to_dram = Arrival(scope, nc, "parts_out")
                for c in range(NC):
                    cs = slice(c * CH, (c + 1) * CH)
                    T.need(ht[c])
                    for side in range(2):
                        k, ps = ring.take(T)
                        mm = T(nc.tensor.matmul(ps[:], w[:, side, :], self.HT[:, cs], start=True, stop=True))
                        S_.need(mm)
                        a = S_(nc.scalar.activation(p[0][:, side, cs], ps[:], ACT.Copy))
                        V.need(a)
                        b_ = V(nc.vector.tensor_tensor(rest[:, side, cs], ps[:], p[0][:, side, cs], ALU.subtract))
                        ring.release(k, b_)
                        V.need(b_)
                        c_ = V(nc.vector.tensor_copy(p[1][:, side, cs], rest[:, side, cs]))
                        G.need(c_)
                        d_ = G(nc.gpsimd.tensor_tensor(p[2][:, side, cs], rest[:, side, cs], p[1][:, side, cs],
                                                       ALU.subtract))
                        wrote[side, c] = (a, c_, d_)
                    if c % 2:
                        b = c // 2
                        for side in range(2):
                            Q.need(*wrote[side, c], *wrote[side, c - 1])
                            for i in range(3):
                                to_dram(nc.sync.dma_start(
                                    parts[side, i, b * H:(b + 1) * H].rearrange("h d t -> (h d) t"),
                                    p[i][:, side, b * S:(b + 1) * S]))
                    k, ps = ring.take(T)
                    for j in range(4):
                        tile = 4 * c + j
                        mm = nc.tensor.matmul(ps[:, j * P:(j + 1) * P], self.HT[:, tile * P:(tile + 1) * P],
                                              w[:, 2, :], start=True, stop=True)
                    mm = T(mm)
                    S_.need(mm)
                    b, k0 = c // 2, (c % 2) * 4
                    for j in range(4):
                        v_done = S_(nc.scalar.activation(
                            vt[:, b * H:(b + 1) * H, k0 + j, :],
                            ps[:, j * P:(j + 1) * P].rearrange("p (h d) -> p h d", h=H), ACT.Copy))
                    ring.release(k, v_done)
                self.settle()
                Q.need(set_up, rows_set)
                Q.engine.wait_ge(to_dram.sem, to_dram.n)
                for t in (V, S_, G, T):
                    t.engine.wait_ge(to_dram.sem, to_dram.n)

            sc1 = scope.enter_context(nc.psum_tensor("score_q", [P, 2, CH], F32))
            sc2 = scope.enter_context(nc.psum_tensor("score_k", [P, 2, 2, CH], F32))
            avp = scope.enter_context(nc.psum_tensor("av_ps", [P, 2, CH], F32))

            ev = lambda n, e, before=0: Event(scope, nc, n, e, before, 96)
            loaded = [ev(f"loaded{s}", nc.sync) for s in range(NS)]
            max_in = [ev(f"max_in{s}", nc.sync) for s in range(NS)]
            ring_mm = ev("ring_mm", nc.tensor, 33)
            ring_read = ev("ring_read", nc.vector, 33)
            split = ev("max_split", nc.vector)
            s2_mm, exped = ev("s2_mm", nc.tensor), ev("exped", nc.scalar)
            av_mm, av_out = ev("av_mm", nc.tensor, 3), ev("av_out", nc.scalar, 1)
            out_mm = ev("out_mm", nc.tensor, 1)
            recips, divided = ev("recips", nc.vector, 1), ev("divided", nc.vector, 1)
            v_put = ev("v_put", nc.gpsimd)
            ND = 12
            ORDER = ("EBEBBQBEBEBOBQTBEBEBDBQBEBEBBQB", "EBEBBQBEBEBBQTBEBEBBQBEBEBOBQDB")
            SC = float(HD) ** -0.5

            class Ring:
                PAIR = 2 * (2 * TB + 1)
                base, p = -33, 0

                def step(self):
                    g, bank = self.base + self.p, (self.p + self.odd) % 2
                    self.p += 1
                    ring_read.wait(nc.tensor, g - 1)
                    return g, bank

                def enter(self, base, odd):
                    self.base, self.p, self.odd = base, 0, odd

                def here(self):
                    return self.base + self.p

            ring = Ring()

            def load(h, s):
                s2_mm.wait(nc.sync, 8 * (h - 3))
                for i in range(3):
                    loaded[s](nc.sync.dma_start(kp[s][24 * i:24 * i + 24, :],
                                                parts[1][:, bass.ds(h, 1)].rearrange("p a d t -> (p a) d t")), 16)
                    for j in range(3):
                        loaded[s](nc.sync.dma_start(qp[s][24 * i + 8 * j:24 * i + 8 * j + 8, :],
                                                    parts[0][i, bass.ds(h, 1)].rearrange("a d t -> (a d) t")), 16)

            def max_score(h, s, turn, j):
                if j == 0:
                    loaded[s].wait(nc.tensor, 16 * ND * (turn + 1))
                    split.wait(nc.vector, 5 * (h - 1))
                qt, kh = j // 2, j % 2
                g, bank = ring.step()
                ring_mm(nc.tensor.matmul(sc1[:, bank, :], qp[s][0:KR, qt * P:(qt + 1) * P],
                                         kp[s][0:KR, kh * CH:(kh + 1) * CH], start=True, stop=True))
                ring_mm.wait(nc.vector, g + 1)
                ring_read(nc.vector.tensor_reduce(mx[s % 2][:, qt, kh:kh + 1], sc1[:, bank, :], AX_X, ALU.max))

            def max_part(h, s, k, start):
                z, o = mx[s % 2], ms[s % 2]
                if k:
                    split.wait(nc.vector, 5 * h + k)
                else:
                    ring_read.wait(nc.vector, start)
                    ring_mm.wait(nc.vector, start)
                split((lambda: nc.vector.tensor_reduce(nm[:], z[:], AX_X, ALU.max, negate=True),
                       lambda: nc.vector.tensor_copy(o[:, 0, :], nm[:]),
                       lambda: nc.vector.tensor_tensor(nr[:], nm[:], o[:, 0, :], ALU.subtract),
                       lambda: nc.vector.tensor_copy(o[:, 1, :], nr[:]),
                       lambda: nc.vector.tensor_tensor(o[:, 2, :], nr[:], o[:, 1, :], ALU.subtract))[k]())

            def max_turn(h, s, turn):
                split.wait(nc.tensor, 5 * h + 5)
                g, bank = ring.step()
                mtp = sc1[:, bank, 0:64].bitcast(BF16)
                ring_mm(nc.tensor.transpose(mtp[0:3 * TB, :], ms[s % 2][:].rearrange("p a k -> p (a k)"),
                                            self.identb[:]))
                ring_mm.wait(nc.vector, g + 1)
                max_in[(s - 2) % NS].wait(nc.vector, 48 * ((turn if s >= 2 else turn - 1) + 1))
                ring_read(nc.vector.tensor_copy(mt[s % 2][:], mtp[0:3 * TB, :]))
                ring_read.wait(nc.sync, g + 1)
                for i in range(3):
                    max_in[s](nc.sync.dma_start(
                        qp[s][96 + i:97 + i, :].rearrange("a (k q) -> a k q", k=TB),
                        mt[s % 2][TB * i:TB * i + TB, :]), 16)

            def put_v(h, s):
                av_mm.wait(nc.gpsimd, 4 * (h - 1))
                v_put(nc.gpsimd.tensor_copy(va[s % 2][:, :, 16 * (s % 2):16 * (s % 2) + HD],
                                            vt[:, bass.ds(h, 1), :, :].rearrange("p a k d -> p (a k) d")))

            def exp_pair(h, s, turn, r):
                if r == 0:
                    max_in[s].wait(nc.tensor, 48 * (turn + 1))
                qh, kt = r // 4, (r % 4) * 2
                exped.wait(nc.tensor, 8 * h + r - 1)
                for j in range(2):
                    mm = nc.tensor.matmul(sc2[:, r % 2, j, :], kp[s][0:KM, (kt + j) * P:(kt + j + 1) * P],
                                          qp[s][0:KM, qh * CH:(qh + 1) * CH], start=True, stop=True)
                s2_mm(mm)
                if r % 2 == 0:
                    av_mm.wait(nc.scalar, 4 * h + r // 2 - 1)
                s2_mm.wait(nc.scalar, 8 * h + r + 1)
                exped(nc.scalar.activation(pt[(r // 2) % 2][:, (r % 2) * 2:(r % 2) * 2 + 2, :],
                                           sc2[:, r % 2], ACT.Exp, scale=SC))

            def av_quad(h, s, u, pair):
                if u == 0:
                    v_put.wait(nc.tensor, h + 1)
                if s % 2 == 0 and u % 2 == 0:
                    divided.wait(nc.tensor, 2 * pair - 1 + u // 2)
                exped.wait(nc.tensor, 8 * h + 2 * u + 2)
                for j in range(4):
                    mm = nc.tensor.matmul(avp[32 * j:32 * j + 32, u // 2, :], va[s % 2][:, 4 * (u % 2) + j, :],
                                          pt[u % 2][:, j, :], start=(s % 2 == 0 and u % 2 == 0),
                                          stop=(s % 2 == 1 and u % 2 == 1))
                av_mm(mm)

            def av_evac(h, qh, pair):
                av_mm.wait(nc.scalar, 4 * h + 2 * qh + 2)
                out_mm.wait(nc.scalar, 2 * pair - 1 + qh)
                av_out(nc.scalar.activation(ot[qh][:], avp[:, qh, :], ACT.Copy))

            def out_rows(qh):
                return avp[:, qh, 0:P].rearrange("p (k c) -> p k c", c=32)

            def out_turn(pair, qh):
                av_out.wait(nc.tensor, 2 * pair + 1 + qh)
                for k in range(4):
                    mm = nc.tensor.matmul(out_rows(qh)[:, k, :], ot[qh][:, k * P:(k + 1) * P], sel[:],
                                          start=True, stop=True)
                out_mm(mm)

            def divide(pair, qh):
                res = out_rows(qh).rearrange("p k (a c) -> p k a c", a=2)
                divided.wait(nc.vector, 2 * pair - 1 + qh)
                out_mm.wait(nc.vector, 2 * pair + 1 + qh)
                recips(nc.vector.reciprocal(rc[qh][:], res[:, :, :, HD]))
                recips.wait(nc.vector, 2 * pair + 1 + qh)
                divided(nc.vector.tensor_tensor(
                    ox[:, bass.ds(2 * pair + 2, 2), 4 * qh:4 * qh + 4, :].rearrange("p a k d -> p k a d"),
                    res[:, :, :, 0:HD], rc[qh][:][:, :, :, None].to_broadcast([P, 4, 2, HD]), ALU.mult))

            def head(h, s, turn, pair, ahead=3):
                start = ring.here()
                s1, t1, s2, t2 = (s + 1) % NS, turn + (s + 1) // NS, (s + 2) % NS, turn + (s + 2) // NS
                if ahead >= 3:
                    load(h + 3, (s + 3) % NS)
                put_v(h, s)
                done = dict.fromkeys("EQBTOD", 0)
                for step in ORDER[s % 2]:
                    n = done[step]
                    done[step] += 1
                    if step == "E":
                        exp_pair(h, s, turn, n)
                    elif step == "B":
                        if ahead >= 2:
                            max_score(h + 2, s2, t2, n)
                        if ahead >= 1 and n < 5:
                            max_part(h + 1, s1, n, start)
                    elif step == "T" and ahead >= 1:
                        max_turn(h + 1, s1, t1)
                    elif step == "Q" and n == 0:
                        av_quad(h - 1, s - 1, 3, pair - 1)
                        if s % 2 == 0:
                            av_evac(h - 1, 1, pair - 1)
                    elif step == "Q":
                        av_quad(h, s, n - 1, pair)
                        if s % 2 and n == 2:
                            av_evac(h, 0, pair)
                    elif step == "O":
                        out_turn(pair - 1 + s % 2, 1 - s % 2)
                    elif step == "D":
                        divide(pair - 1 + s % 2, 1 - s % 2)

            for h in range(3):
                load(h, h)
            av_quad(-2, -2, 2, -1)
            av_quad(-1, -1, 2, -1)
            av_mm.wait(nc.gpsimd, -1)
            ring.enter(-33, 1)
            for j in range(2 * TB):
                max_score(0, 0, 0, j)
            start = ring.here()
            for j in range(2 * TB):
                max_score(1, 1, 0, j)
                if j < 5:
                    max_part(0, 0, j, start)
                if j == 9:
                    max_turn(0, 0, 0)
            LOOPS = BH // NS - 1
            with nc.Fori(0, LOOPS) as i:
                ring.enter(i * (2 * Ring.PAIR), 0)
                for s in range(NS):
                    head(i * NS + s, s, i, 2 * i + s // 2)
                assert ring.p == 2 * Ring.PAIR
            ring.enter(LOOPS * 2 * Ring.PAIR, 0)
            for s in range(NS):
                h = BH - NS + s
                head(h, s, LOOPS, h // 2, ahead=BH - 1 - h)
            av_quad(BH - 1, NS - 1, 3, BH // 2 - 1)
            av_evac(BH - 1, 1, BH // 2 - 1)
            out_turn(BH // 2 - 1, 1)
            divide(BH // 2 - 1, 1)

            divided.wait(nc.vector, BH)
            tmp = self.N
            for b in range(NB):
                xb = self.X[:, b * TB:(b + 1) * TB, :]
                tb = tmp[:, b * TB:(b + 1) * TB, :]
                for k in range(TB):
                    a = V(nc.vector.tensor_tensor(
                        tb[:, k].rearrange("p (h d) -> p h d", h=H), ox[:, 2 + b * H:2 + (b + 1) * H, k, :],
                        self.mrow[0][:, b, 2, :].rearrange("p (h d) -> p h d", h=H), ALU.mult))
                V.need(a)
                a = V(nc.vector.tensor_tensor(xb, xb, tb, ALU.add))
            for e in (nc.tensor, nc.scalar, nc.gpsimd, nc.sync, nc.vector):
                divided.wait(e, BH)
            self.settle()

    def coupling(self):
        nc, A, V, S_, G, T, Q = self.nc, self.A, self.V, self.S, self.G, self.T, self.Q
        with ExitStack() as scope:
            sb = lambda n, s, d=F32: self.sb(scope, n, s, d)
            dims = {"cn": (D, D, D // 2, D // 4, 1), "gc": (D, D // 2, D // 4, 1)}
            wt, bs = {}, {}
            in_w = Arrival(scope, nc, "in_coupling")
            for net, d in dims.items():
                for i in range(1, len(d)):
                    wt[net, i] = sb(f"{net}_w{i}", [d[i - 1], d[i]])
                    in_w(nc.sync.dma_start(wt[net, i][:], A[f"{net}_w{i}"]))
                    rows = d[i] if d[i] > 1 else P
                    bs[net, i] = sb(f"{net}_b{i}", [rows, 1])
                    src = A[f"{net}_b{i}"]
                    in_w(nc.sync.dma_start(bs[net, i][:], src if d[i] > 1 else src.to_broadcast([P, 1])))
            rng = sb("range", [P, 1])
            in_w(nc.sync.dma_start(rng[:], A["adaptive_range"].to_broadcast([P, 1])))
            twist = sb("twist", [P, P])
            in_w(nc.sync.dma_start(twist[:], A["k_twist"]))
            wlast = {"cn": sb("cn_w4_rep", [D // 4, P]), "gc": sb("gc_w3_rep", [D // 4, P])}
            blast = {"cn": sb("cn_b4_half", [P, 1]), "gc": sb("gc_b3_half", [P, 1])}
            alpha, beta = sb("cpl_alpha", [P, 1]), sb("cpl_beta", [P, NB])
            mean = sb("token_sum", [P, NB])
            g1, g2, g3 = sb("ctx1", [D // 2, NB]), sb("ctx2", [D // 4, NB]), sb("ctx3", [P, NB])
            h1 = [sb(f"net1_{c}", [D, CH]) for c in range(NC)]
            h2 = [sb(f"net2_{c}", [D // 2, CH]) for c in range(NC)]
            h3 = [sb(f"net3_{c}", [D // 4, CH]) for c in range(NC)]
            cp = [sb(f"coupling_{c}", [P, CH]) for c in range(NC)]
            ring = self.banks(scope, "cpl_ps", 8)
            U = self.HT
            V.need(in_w.mark())
            for net, i in (("cn", 4), ("gc", 3)):
                V(nc.vector.tensor_copy(wlast[net][:], wt[net, i][:].to_broadcast([D // 4, P])))
                m_b = V(nc.vector.tensor_scalar(blast[net][:], bs[net, i][:], 0.5, None, ALU.mult))
            m_b = V(nc.vector.tensor_scalar(alpha[:], rng[:], 0.3, None, ALU.mult))

            normed = self.layer_norm(self.X)
            ht = self.turn(ring, normed, lambda b: self.mcol[0][:, 4, b:b + 1],
                           lambda b: self.mcol[0][:, 3, b:b + 1], (self.m_col,))
            V.need(*ht)
            for b in range(NB):
                m = V(nc.vector.tensor_reduce(mean[:, b:b + 1], U[:, b * S:(b + 1) * S], AX_X, ALU.add))
            T.need(m, in_w.mark(), m_b)
            S_.need(in_w.mark(), m_b)
            src = mean
            for i, dst in ((1, g1), (2, g2), (3, g3)):
                k, ps = ring.take(T)
                n = dst.shape[0]
                w = wlast["gc"][:] if i == 3 else wt["gc", i][:]
                mm = T(nc.tensor.matmul(ps[0:n, 0:NB], w, src[:], start=True, stop=True))
                S_.need(mm)
                if i < 3:
                    m = S_(nc.scalar.activation(dst[:], ps[0:n, 0:NB], ACT.Gelu, bias=bs["gc", i][:],
                                                scale=1.0 / S if i == 1 else 1.0))
                else:
                    m = S_(nc.scalar.activation(dst[:], ps[0:n, 0:NB], ACT.Tanh, bias=blast["gc"][:], scale=0.5))
                ring.release(k, m)
                T.need(m)
                src = dst
            V.need(m)
            m = V(nc.vector.tensor_scalar(beta[:], g3[:], rng[:], 0.7, ALU.mult, ALU.mult))
            V.need(m)
            m = V(nc.vector.tensor_scalar(beta[:], beta[:], 0.1, None, ALU.add))
            V.need(m)

            ready = [(ht[c],) for c in range(NC)]
            turned = [None] * NC
            stages = ((1, D, h1), (2, D // 2, h2), (3, D // 4, h3), (4, P, cp))
            for cycle in range(3):
                marks = [None] * NC
                for i, n, dst in stages:
                    for c in range(NC):
                        cs = slice(c * CH, (c + 1) * CH)
                        src = U[:, cs] if i == 1 else stages[i - 2][2][c][:]
                        w = wlast["cn"] if i == 4 else wt["cn", i]
                        k, ps = ring.take(T)
                        T.need(*(ready[c] if i == 1 else (marks[c],)))
                        mm = T(nc.tensor.matmul(ps[0:n, :], w[:], src, start=True, stop=True))
                        S_.need(mm)
                        if i < 4:
                            marks[c] = S_(nc.scalar.activation(dst[c][:], ps[0:n, :], ACT.Gelu, bias=bs["cn", i][:]))
                        else:
                            marks[c] = S_(nc.scalar.activation(dst[c][:], ps[0:n, :], ACT.Tanh,
                                                               bias=blast["cn"][:], scale=0.5))
                        ring.release(k, marks[c])
                for c in range(NC):
                    cs = slice(c * CH, (c + 1) * CH)
                    b = c // 2
                    k, ps = ring.take(T)
                    mm = T(nc.tensor.matmul(ps[:], twist[:], U[:, cs], start=True, stop=True))
                    V.need(marks[c])
                    m = V(nc.vector.tensor_scalar(cp[c][:], cp[c][:], alpha[:], beta[:, b:b + 1], ALU.mult, ALU.add))
                    V.need(m, mm)
                    m = V(nc.vector.tensor_tensor(cp[c][:], ps[:], cp[c][:], ALU.mult))
                    ring.release(k, m)
                    V.need(m)
                    m = V(nc.vector.tensor_tensor(U[:, cs], U[:, cs], cp[c][:], ALU.add))
                    ready[c] = (m,)
                    S_.need(m)
            for c in range(NC):
                cs = slice(c * CH, (c + 1) * CH)
                b = c // 2
                S_.need(*ready[c])
                m = S_(nc.scalar.activation(h1[c][:], U[:, cs], ACT.Copy, scale=self.mcol[0][:, 5, b:b + 1]))
                T.need(m)
                k, ps = ring.take(T)
                for j in range(4):
                    mm = nc.tensor.transpose(ps[:, j * P:(j + 1) * P], h1[c][:, j * P:(j + 1) * P], self.ident[:])
                mm = T(mm)
                V.need(mm)
                xc = self.X[:, 4 * c:4 * c + 4, :].rearrange("p k d -> p (k d)")
                m = V(nc.vector.tensor_tensor(xc, xc, ps[:], ALU.add))
                ring.release(k, m)
            self.settle()

    def mod_rows(self, dst, src, l, shift, marks):
        nc, V, G = self.nc, self.V, self.G
        done = []
        for eng, e, ts, b in self.parts():
            n = ts.stop - ts.start
            eng.need(self.m_row, *marks[ts])
            row = lambda i: self.mrow[l][:, b, i:i + 1, :].to_broadcast([P, n, D])
            m = eng(e.tensor_tensor(dst[:, ts, :], src[:, ts, :], row(shift + 1), ALU.mult))
            eng.need(m)
            done += [eng(e.tensor_tensor(dst[:, ts, :], dst[:, ts, :], row(shift), ALU.add))] * n
        return done

    def mamba(self):
        nc, A, V, S_, G, T, Q = self.nc, self.A, self.V, self.S, self.G, self.T, self.Q
        with ExitStack() as scope:
            sb = lambda n, s, d=F32: self.sb(scope, n, s, d)
            R2 = 2 * DS
            in_w = Arrival(scope, nc, "in_mamba")
            def load(name, shape, src, dt=F32):
                t = sb(name, shape, dt)
                in_w(nc.sync.dma_start(t[:], src))
                return t
            nw = load("norm_w", [P, NL], A["norm_w"])
            cb = load("conv_b", [P, NL, NBLK], A["conv_b"])
            dp = load("d_skip", [P, NL, NBLK], A["Dp"])
            am = load("a_log", [P, NL, NBLK, DS], A["A_log"])
            ow = load("out_w", [P, NBLK, NL, D], A["out_wT"])
            rowsel = load("row_ident", [3 * R2, R2], A["k_rows"])
            iw = sb("in_w", [P, NL, 2 * DI])
            csb = [sb(f"c_row{s}", [P, S]) for s in range(2)]
            cw = [csb[0][:].rearrange("p (j e) -> p j e", j=KW), sb("tap_w", [P, KW, DI])[:]]
            xw = sb("x_proj_w", [P, NBLK, NL, 3 * R2 + DTR])
            LOW = slice(3 * R2, 3 * R2 + DTR)
            dtw = sb("dt_w", [3 * R2 + DTR + 1, NL, DI])
            in_w(nc.scalar.dma_start(dtw[LOW], A["dt_wT"]))
            in_w(nc.scalar.dma_start(dtw[3 * R2 + DTR:], A["dt_b"]))
            for l in range(NL):
                in_w(nc.sync.dma_start(iw[:, l, :], A["in_wT"][l]))
                in_w(nc.scalar.dma_start(cw[l], A["conv_wT"][l:l + 1].to_broadcast([P, KW, DI])))
                in_w(nc.sync.dma_start(xw[:, :, l, LOW], A["xp_wT"][:, :, l, 0:DTR]))
                for r in range(3):
                    in_w(nc.sync.dma_start(xw[:, :, l, r * R2:(r + 1) * R2], A["xp_wT"][:, :, l, DTR:DTR + R2]))
            sel = sb("row_select", [3 * R2, R2, P], BF16)
            xm = sb("x_mamba", [P, NT, D])
            flat = sb("momentum", [P, NBLK * 2 * S])
            hp = flat[:, 0:NB * (S + KW - 1)].rearrange("p (b t) -> p b t", b=NB)
            xb = sb("x_inner", [P, NBLK, NB, S])
            zs = sb("silu_z", [P, NBLK, NB, S])
            delta = sb("delta", [P, NBLK, NB, S])
            du = sb("delta_x", [P, NBLK, NB, S])
            dr = sb("delta_low", [3 * R2 + DTR + 1, TOK])
            bcr = csb[1][0:3 * R2, 0:CH]
            bcm = sb("bc_mid", [3 * R2, CH], BF16)
            bc = sb("bc_parts", [3 * R2, TOK], BF16)
            ddiag = sb("d_diag", [P, NBLK, P])
            beta = sb("momentum_beta", [P, S])
            bsb = [sb(f"b_row{s}", [P, S]) for s in range(2)]
            da = [sb(f"decay{s}", [P, NBLK, S]) for s in range(2)]
            mi = [flat[:, s * NBLK * S:(s + 1) * NBLK * S].rearrange("p (k t) -> p k t", k=NBLK) for s in range(2)]
            hh = self.HT[:].rearrange("p (k t) -> p k t", k=NBLK)
            yp = [self.N[:].rearrange("p a d -> p (a d)").rearrange("p (k t) -> p k t", k=NBLK)]

            G.need(G(nc.gpsimd.memset(beta[:], BETA)))
            m_ones = G(nc.gpsimd.memset(dr[3 * R2:, :], 1.0))
            G.need(m_ones)
            S_.need(in_w.mark())
            m_a = S_(nc.scalar.activation(am[:].rearrange("p l k n -> p (l k n)"),
                                          am[:].rearrange("p l k n -> p (l k n)"), ACT.Exp))
            normed = self.layer_norm(self.X)
            xm_ready = self.mod_rows(xm, self.N, 1, 0, normed)
            first_rms = self.rms_stats(xm, xm_ready)
            V.need(in_w.mark(), m_a)
            for l in range(NL):
                m_taps = V(nc.vector.tensor_tensor(cw[l], cw[l],
                                                   iw[:, l:l + 1, 0:DI].to_broadcast([P, KW, DI]), ALU.mult))
            V(nc.vector.tensor_scalar(am[:].rearrange("p l k n -> p (l k n)"),
                                      am[:].rearrange("p l k n -> p (l k n)"), -1.0, None, ALU.mult))
            G.need(in_w.mark())
            G(nc.gpsimd.tensor_copy(sel[:], rowsel[:][:, :, None].to_broadcast([3 * R2, R2, P])))
            v = locals()
            for l in range(NL):
                with ExitStack() as pre:
                    ring = self.banks(pre, f"m{l}_ps", 4)
                    wide = Banks([pre.enter_context(nc.psum_tensor(f"m{l}_wide{k}", [P, S], F32)) for k in range(2)])
                    if l:
                        xm_ready = self.mamba_out(l - 1, ring, v)
                    rms = self.rms_stats(xm, xm_ready) if l else first_rms
                    self.mamba_inputs(l, ring, wide, v, xm_ready, rms)
                    self.settle()
                self.mamba_scan(l, v)
            with ExitStack() as post:
                xm_ready = self.mamba_out(NL - 1, self.banks(post, "m_out", 4), v)
                self.x_ready = self.add_gated(xm, 1, 2, xm_ready)
                self.settle()

    def rms_stats(self, xm, ready):
        nc, V, S_ = self.nc, self.V, self.S
        N, ssq = self.N, self.stat[:, :, 0]
        roots = []
        for c in range(NC):
            ts = slice(4 * c, 4 * c + 4)
            S_.need(ready[4 * c], ready[4 * c + 3])
            a = S_(nc.scalar.activation(N[:, ts, :], xm[:, ts, :], ACT.Square))
            V.need(a)
            a = V(nc.vector.tensor_reduce(ssq[:, ts], N[:, ts, :], AX_X, ALU.add))
            if c % 2:
                ts = slice(4 * c - 4, 4 * c + 4)
                roots.append(self.rstd(ts, ssq[:, ts], 1.0 / D, a))
        return roots

    def mamba_inputs(self, l, ring, wide, v, xm_ready, rms):
        nc, V, S_, G, T = self.nc, self.V, self.S, self.G, self.T
        xm, hp, xb, zs, delta, du, dr, bc = (v[n] for n in ("xm", "hp", "xb", "zs", "delta", "du", "dr", "bc"))
        iw, xw, cw, cb, dtw, nw, LOW = (v[n] for n in ("iw", "xw", "cw", "cb", "dtw", "nw", "LOW"))
        R2 = 2 * DS
        N = self.N
        V.need(*xm_ready)
        pads = V(nc.vector.memset(hp[:, :, 0:KW - 1], 0.0))
        normed = []
        for t in range(NT):
            V.need(rms[t // TB])
            normed.append(V(nc.vector.tensor_scalar(N[:, t, :], xm[:, t, :], self.rs[:, t:t + 1], None, ALU.mult)))
        chunk = [(c // 2, (c % 2) * CH) for c in range(NC)]
        V.need(v["in_w"].mark())
        ht = self.turn(ring, normed, lambda b: nw[:, l:l + 1], None, (v["in_w"].mark(),),
                       to=lambda c: hp[:, chunk[c][0], KW - 1 + chunk[c][1]:KW - 1 + chunk[c][1] + CH])
        T.need(v["in_w"].mark(), v["m_taps"], v["m_ones"], pads)
        conv, low, ws = {}, {}, {}

        def inner(c, blk):
            b, off = chunk[c]
            T.need(ht[c])
            k, ps = ring.take(T)
            for j in range(KW):
                mm = nc.tensor.matmul(ps[:], cw[l][:, j, blk * P:(blk + 1) * P], hp[:, b, off + j:off + j + CH],
                                      start=(j == 0), stop=(j == KW - 1))
            S_.need(T(mm))
            conv[blk, c] = S_(nc.scalar.activation(xb[:, blk, b, off:off + CH], ps[:], ACT.Silu,
                                                   bias=cb[:, l, blk:blk + 1]))
            ring.release(k, conv[blk, c])

        def gate(c):
            b, off = chunk[c]
            for blk in range(NBLK):
                k, ps = ring.take(T)
                mm = T(nc.tensor.matmul(ps[:], iw[:, l, DI + blk * P:DI + (blk + 1) * P],
                                        hp[:, b, KW - 1 + off:KW - 1 + off + CH], start=True, stop=True))
                S_.need(mm)
                ring.release(k, S_(nc.scalar.activation(zs[:, blk, b, off:off + CH], ps[:], ACT.Silu)))

        def project(c):
            b, off = chunk[c]
            cs = slice(c * CH, (c + 1) * CH)
            T.need(*[conv[blk, c] for blk in range(NBLK)])
            k, ps = ring.take(T)
            for blk in range(NBLK):
                mm = nc.tensor.matmul(ps[0:3 * R2 + DTR, :], xw[:, blk, l, :], xb[:, blk, b, off:off + CH],
                                      start=(blk == 0), stop=(blk == NBLK - 1))
            mm = T(mm)
            S_.need(mm)
            S_(nc.scalar.activation(dr[LOW, cs], ps[LOW, :], ACT.Copy))
            low[c] = S_.last()
            a = S_(nc.scalar.activation(bc[:, cs], ps[0:3 * R2, :], ACT.Copy))
            V.need(a)
            rest, mid = v["bcr"], v["bcm"]
            a = V(nc.vector.tensor_tensor(rest[:], ps[0:3 * R2, :], bc[:, cs], ALU.subtract))
            ring.release(k, a)
            V.need(a)
            a = V(nc.vector.tensor_copy(mid[:], rest[:]))
            V.need(a)
            V(nc.vector.tensor_copy(bc[R2:2 * R2, cs], mid[R2:2 * R2, :]))
            a = V(nc.vector.tensor_tensor(bc[2 * R2:, cs], rest[2 * R2:, :], mid[2 * R2:, :], ALU.subtract))
            V.need(a)

        def softplus(b):
            T.need(low[2 * b], low[2 * b + 1])
            for blk in range(NBLK):
                k, ps = wide.take(T)
                for c in range(2):
                    mm = nc.tensor.matmul(ps[:, c * CH:(c + 1) * CH], dtw[3 * R2:, l, blk * P:(blk + 1) * P],
                                          dr[3 * R2:, b * S + c * CH:b * S + (c + 1) * CH], start=True, stop=True)
                mm = T(mm)
                out, w = delta[:, blk, b, :], du[:, blk, b, :]
                S_.need(mm)
                a = S_(nc.scalar.activation(out, ps[:], ACT.Abs))
                S_.need(a)
                x_ = S_(nc.scalar.activation(out, out, ACT.Exp, scale=-1.0))
                V.need(x_)
                a = V(nc.vector.tensor_scalar(w, out, 1.0, None, ALU.add))
                V.need(a)
                a = V(nc.vector.scalar_tensor_tensor(out=out, in0=w, scalar=-1.0, in1=out,
                                                     op0=ALU.add, op1=ALU.subtract))
                V.need(a)
                a = V(nc.vector.scalar_tensor_tensor(out=out, in0=ps[:], scalar=0.0, in1=out,
                                                     op0=ALU.max, op1=ALU.subtract))
                wide.release(k, a)
                ws[blk, b] = a

        def delta_end(b):
            for blk in range(NBLK):
                out, w = delta[:, blk, b, :], du[:, blk, b, :]
                S_.need(ws[blk, b])
                ln = S_(nc.scalar.activation(w, w, ACT.Ln))
                V.need(ln, ws[blk, b])
                a = V(nc.vector.tensor_tensor(out, out, w, ALU.add))
                eng, e = (G, nc.gpsimd) if b == 0 else (V, nc.vector)
                eng.need(a, conv[blk, 2 * b], conv[blk, 2 * b + 1])
                eng(e.tensor_tensor(w, out, xb[:, blk, b, :], ALU.mult))

        for c in range(NC):
            inner(c, 0)
            if c:
                project(c - 1)
            inner(c, 1)
            if c == 3:
                softplus(0)
        gate(0)
        project(3)
        delta_end(0)
        softplus(1)
        for c in range(1, NC):
            gate(c)
        delta_end(1)
        for blk in range(NBLK):
            G(nc.gpsimd.tensor_scalar(v["ddiag"][:, blk, :], self.ident[:], v["dp"][:, l, blk:blk + 1], None, ALU.mult))

    def mamba_out(self, l, ring, v):
        nc, V, T = self.nc, self.V, self.T
        xm, zs, ow = (v[n] for n in ("xm", "zs", "ow"))
        done = []
        for c in range(NC):
            k, ps = ring.take(T)
            for j in range(4):
                t = 4 * c + j
                b, off = t // TB, (t % TB) * P
                for blk in range(NBLK):
                    mm = nc.tensor.matmul(ps[:, j * P:(j + 1) * P], zs[:, blk, b, off:off + P],
                                          ow[:, blk, l, :], start=(blk == 0), stop=(blk == NBLK - 1))
            mm = T(mm)
            V.need(mm)
            x4 = xm[:, 4 * c:4 * c + 4, :].rearrange("p k d -> p (k d)")
            m = V(nc.vector.tensor_tensor(x4, x4, ps[:], ALU.add))
            ring.release(k, m)
            done += [m] * 4
        return done

    def mamba_scan(self, l, v):
        nc, V, S_, G, T = self.nc, self.V, self.S, self.G, self.T
        with ExitStack() as scope:
            yps = scope.enter_context(nc.psum_tensor(f"y{l}", [P, NBLK, S], F32))
            bps = scope.enter_context(nc.psum_tensor(f"b{l}", [P, S], F32))
            cps = scope.enter_context(nc.psum_tensor(f"c{l}", [P, S], F32))
            ev = lambda n, e: Event(scope, nc, f"{n}{l}", e)
            b_mm, c_mm = ev("b_mm", nc.tensor), ev("c_mm", nc.tensor)
            b_out, c_out = ev("b_out", nc.scalar), ev("c_out", nc.scalar)
            decay, mom = ev("decay", nc.scalar), ev("mom", nc.gpsimd)
            vs, hs, ys = ev("v_scan", nc.vector), ev("h_scan", nc.vector), ev("y_mul", nc.vector)
            yg = ev("y_mul_g", nc.gpsimd)
            GC = 384
            ysum, gated = ev("y_sum", nc.tensor), ev("gated", nc.vector)
            xb, zs, delta, du, bc, sel = (v[n] for n in ("xb", "zs", "delta", "du", "bc", "sel"))
            am, bsb, csb, da, mi, hh, yp = (v[n] for n in ("am", "bsb", "csb", "da", "mi", "hh", "yp"))
            beta = v["beta"]

            def skip(b):
                gated.wait(nc.tensor, 2 * b)
                for blk in range(NBLK):
                    for c in range(2):
                        nc.tensor.matmul(yps[:, blk, c * CH:(c + 1) * CH], v["ddiag"][:, blk, :],
                                         xb[:, blk, b, c * CH:(c + 1) * CH], start=True, stop=False,
                                         skip_group_check=True)

            def gate(b):
                ysum.wait(nc.vector, DS * (b + 1))
                count = V if b == NB - 1 else gated
                for blk in range(NBLK):
                    count(nc.vector.tensor_tensor(zs[:, blk, b, :], zs[:, blk, b, :], yps[:, blk, :], ALU.mult))

            def rows(b, n):
                g = b * DS + n
                for ps, r, done, left in ((bps, n, b_mm, b_out), (cps, n + DS, c_mm, c_out)):
                    left.wait(nc.tensor, g)
                    for c in range(2):
                        mm = nc.tensor.matmul(ps[:, c * CH:(c + 1) * CH],
                                              sel[:, bass.ds(r, 1), :].rearrange("k a p -> k (a p)"),
                                              bc[:, b * S + c * CH:b * S + (c + 1) * CH], start=True, stop=True)
                    done(mm)

            def copies(b, n, s):
                g = b * DS + n
                b_mm.wait(nc.scalar, g + 1)
                mom.wait(nc.scalar, 2 * (g - 1))
                b_out(nc.scalar.activation(bsb[s][:], bps[:], ACT.Copy))
                c_mm.wait(nc.scalar, g + 1)
                ys.wait(nc.scalar, 2 * (g - 1))
                yg.wait(nc.scalar, g - 1)
                c_out(nc.scalar.activation(csb[s][:], cps[:], ACT.Copy))
                hs.wait(nc.scalar, 2 * (g - 1))
                for blk in range(NBLK):
                    decay(nc.scalar.activation(da[s][:, blk, :], delta[:, blk, b, :], ACT.Exp,
                                               scale=am[:, l, blk, bass.ds(n, 1)]))

            def products(b, n, s):
                g = b * DS + n
                b_out.wait(nc.gpsimd, g + 1)
                hs.wait(nc.gpsimd, 2 * (g - 1))
                for blk in range(NBLK):
                    mom(nc.gpsimd.tensor_tensor(mi[s][:, blk, :], du[:, blk, b, :], bsb[s][:], ALU.mult))

            def scans(b, n, s, opening=False):
                g = b * DS + n
                for blk in range(NBLK):
                    mom.wait(nc.vector, 2 * g + blk + 1)
                    vs(nc.vector.tensor_tensor_scan(mi[s][:, blk, :], beta[:], mi[s][:, blk, :], 0.0, ALU.mult, ALU.add))
                for blk in range(NBLK):
                    vs.wait(nc.vector, 2 * g + blk + 1)
                    decay.wait(nc.vector, 2 * g + blk + 1)
                    yg.wait(nc.vector, g)
                    hs(nc.vector.tensor_tensor_scan(hh[:, blk, :], da[s][:, blk, :], mi[s][:, blk, :], 0.0,
                                                    ALU.mult, ALU.add))
                if opening:
                    gate(b - 1)
                c_out.wait(nc.vector, g + 1)
                ysum.wait(nc.vector, g)
                for blk, end in ((0, S), (1, GC)):
                    hs.wait(nc.vector, 2 * g + blk + 1)
                    ys(nc.vector.tensor_tensor(yp[0][:, blk, 0:end], hh[:, blk, 0:end], csb[s][:, 0:end], ALU.mult))

            def y_rest(b, n, s):
                g = b * DS + n
                c_out.wait(nc.gpsimd, g + 1)
                ysum.wait(nc.gpsimd, g)
                hs.wait(nc.gpsimd, 2 * g + 2)
                yg(nc.gpsimd.tensor_tensor(yp[0][:, 1, GC:], hh[:, 1, GC:], csb[s][:, GC:], ALU.mult))

            def sums(b, n, last=False):
                g = b * DS + n
                for blk in range(NBLK):
                    ys.wait(nc.tensor, 2 * g + blk + 1)
                    if blk:
                        yg.wait(nc.tensor, g + 1)
                    for c in range(2):
                        mm = nc.tensor.matmul(yps[:, blk, c * CH:(c + 1) * CH], self.ident[:],
                                              yp[0][:, blk, c * CH:(c + 1) * CH], start=False, stop=last,
                                              skip_group_check=True)
                ysum(mm)

            def state(b, n, s):
                peeled = isinstance(n, int)
                ahead = lambda k: divmod(b * DS + n + k, DS) if peeled else (b, n + k)
                if ahead(2)[0] < NB:
                    rows(*ahead(2))
                copies(b, n, s)
                if ahead(1)[0] < NB:
                    products(*ahead(1), 1 - s)
                opening = peeled and n == 0 and b > 0
                scans(b, n, s, opening)
                y_rest(b, n, s)
                if opening:
                    skip(b)
                sums(b, n, peeled and n == DS - 1)

            rows(0, 0)
            rows(0, 1)
            skip(0)
            products(0, 0, 0)
            for b in range(NB):
                first = 2 * min(b, 1)
                for n in range(first):
                    state(b, n, n % 2)
                with nc.Fori(0, DS // 2 - 1 - first // 2) as i:
                    for s in range(2):
                        state(b, 2 * i + first + s, s)
                for n in (DS - 2, DS - 1):
                    state(b, n, n % 2)
            gate(NB - 1)
            self.settle()

    def experts(self):
        nc, A, V, S_, G, T, Q = self.nc, self.A, self.V, self.S, self.G, self.T, self.Q
        with ExitStack() as scope:
            sb = lambda n, s, d=F32: self.sb(scope, n, s, d)
            in_w = Arrival(scope, nc, "in_experts")
            gam, bet = sb("ln_gamma", [P, 1]), sb("ln_beta", [P, 1])
            rw, iota = sb("router_w", [P, E]), sb("iota", [P, E])
            sgu, sdn = sb("shared_gate_up", [P, 2 * P]), sb("shared_down", [P, D])
            for t, n in ((gam, "ln_gamma"), (bet, "ln_beta"), (rw, "router_w"), (iota, "k_iota"),
                         (sgu, "shared_gate_up_w"), (sdn, "shared_down_w")):
                in_w(nc.scalar.dma_start(t[:], A[n]))
            gu = [sb(f"gate_up{s}", [P, 2 * FF]) for s in range(2)]
            dn = [sb(f"down{s}", [P, FB, D]) for s in range(2)]
            hm = sb("moe_in", [P, NT, D])
            acc = sb("moe_out", [P, NT, D])
            lg = sb("logits", [P, NT, E])
            top = sb("top_values", [P, NT, 8])
            idx = sb("top_index", [P, NT, 8], U32)
            idf = sb("top_index_f", [P, NT, 8])
            comb = sb("combine", [P, E + 1, NT])
            e2, w1, w2 = sb("exp_second", [P, NT]), sb("weight1", [P, NT]), sb("weight2", [P, NT])
            mk = [sb(f"mask{i}", [P, NT, E]) for i in range(2)]
            gc = [sb(f"gate{i}", [P, CH]) for i in range(2)]
            sg = [sb(f"silu_gate{i}", [P, CH]) for i in range(2)]
            act = [sb(f"hidden{i}", [P, FB, CH]) for i in range(2)]

            got = [Event(scope, nc, f"weights_in{s}", nc.sync) for s in range(2)]
            gu_mm = Event(scope, nc, "gu_mm", nc.tensor)
            clip, gate, hid = (Event(scope, nc, n, e) for n, e in
                               (("clip", nc.vector), ("gate_out", nc.scalar), ("hid", nc.vector)))
            dn_mm = Event(scope, nc, "dn_mm", nc.tensor, 1)
            summed = Event(scope, nc, "summed", nc.vector, 4)

            def fetch(e, s):
                dn_mm.wait(nc.sync, NC * (e - 1))
                got[s](nc.sync.dma_start(gu[s][:], A["gate_up_w"][bass.ds(e, 1)].rearrange("a d f -> (a d) f")), 16)
                got[s](nc.sync.dma_start(dn[s][:], A["down_w"][bass.ds(e, 1)].rearrange("a p k d -> (a p) k d")), 16)

            normed = self.layer_norm(self.X, self.x_ready)
            h_ready = self.mod_rows(hm, self.N, 1, 3, normed)
            G.need(*h_ready)
            G(nc.gpsimd.memset(comb[:, 0, :], 0.0))
            G(nc.gpsimd.memset(act[1][:], 0.0))
            m_zero = G(nc.gpsimd.memset(dn[1][:], 0.0))
            normed = self.layer_norm(hm, h_ready)
            with ExitStack() as pre:
                ring = self.banks(pre, "moe_ps", 8)
                S_.need(in_w.mark())
                ht = self.turn(ring, normed, lambda b: gam[:], lambda b: bet[:], (in_w.mark(),))
                T.need(in_w.mark())
                hidden, opened = [None] * NC, []
                def shared_up(c):
                    cs = slice(c * CH, (c + 1) * CH)
                    T.need(ht[c])
                    kg, pg = ring.take(T)
                    mg = T(nc.tensor.matmul(pg[:], sgu[:, 0:P], self.HT[:, cs], start=True, stop=True))
                    ku, pu = ring.take(T)
                    mu = T(nc.tensor.matmul(pu[:], sgu[:, P:2 * P], self.HT[:, cs], start=True, stop=True))
                    V.need(mg, hidden[c - 2] if c > 1 else None)
                    m = V(nc.vector.tensor_scalar(gc[c % 2][:], pg[:], -10.0, 10.0, ALU.max, ALU.min))
                    ring.release(kg, m)
                    S_.need(m)
                    s = S_(nc.scalar.activation(sg[c % 2][:], gc[c % 2][:], ACT.Silu))
                    V.need(mu, s)
                    hidden[c] = V(nc.vector.tensor_tensor(act[0][:, c, :], sg[c % 2][:], pu[:], ALU.mult))
                    ring.release(ku, hidden[c])
                    S_.need(hidden[c])
                shared_up(0)
                shared_up(1)
                T.need(*ht)
                k, ps = ring.take(T)
                for t in range(NT):
                    mm = nc.tensor.matmul(ps[:, t * E:(t + 1) * E], self.HT[:, t * P:(t + 1) * P], rw[:],
                                          start=True, stop=True)
                mm = T(mm)
                shared_up(2)
                shared_up(3)
                V.need(mm)
                m = logits = V(nc.vector.tensor_copy(lg[:].rearrange("p t e -> p (t e)"), ps[:, 0:NT * E]))
                ring.release(k, m)
                for c in range(NC):
                    T.need(hidden[c])
                    kd, pd = ring.take(T)
                    for j in range(4):
                        mm = nc.tensor.matmul(pd[:, j * P:(j + 1) * P], act[0][:, c, j * P:(j + 1) * P], sdn[:],
                                              start=True, stop=True)
                    mm = down_done = T(mm)
                    S_.need(mm)
                    opened.append(S_(nc.scalar.activation(acc[:, 4 * c:4 * c + 4, :].rearrange("p k d -> p (k d)"),
                                                          pd[:], ACT.Copy)))
                    ring.release(kd, opened[-1])
                V.need(m)
                for t in range(NT):
                    m = V(nc.vector.max(top[:, t, :], lg[:, t, :]))
                V.need(m)
                for t in range(NT):
                    m = V(nc.vector.max_index(idx[:, t, :], top[:, t, :], lg[:, t, :]))
                d = V(nc.vector.tensor_tensor(e2[:], top[:, :, 1], top[:, :, 0], ALU.subtract))
                S_.need(d)
                x_ = S_(nc.scalar.activation(e2[:], e2[:], ACT.Exp))
                V.need(m)
                i_ = V(nc.vector.tensor_copy(idf[:].rearrange("p t e -> p (t e)"), idx[:].rearrange("p t e -> p (t e)")))
                V.need(x_)
                m = V(nc.vector.tensor_scalar(w2[:], e2[:], 1.0, None, ALU.add))
                V.need(m)
                m = V(nc.vector.reciprocal(w1[:], w2[:]))
                V.need(m, i_)
                m = V(nc.vector.tensor_tensor(w2[:], e2[:], w1[:], ALU.mult))
                V.need(m)
                for i, w in ((0, w1), (1, w2)):
                    m = V(nc.vector.tensor_tensor(mk[i][:], idf[:, :, i:i + 1].to_broadcast([P, NT, E]),
                                                  iota[:][:, None, :].to_broadcast([P, NT, E]), ALU.is_equal))
                    V.need(m)
                    m = V(nc.vector.tensor_tensor(mk[i][:], mk[i][:], w[:][:, :, None].to_broadcast([P, NT, E]), ALU.mult))
                V.need(m)
                m_comb = V(nc.vector.tensor_tensor(comb[:, 1:, :].rearrange("p e t -> p t e"), mk[0][:], mk[1][:], ALU.add))
            T.need(*hidden, *opened, logits, m_zero)
            S_.need(*hidden)
            V.need(*opened, down_done, m_comb, m_zero)

            gups = scope.enter_context(nc.psum_tensor("gate_up_ps", [P, 3, 2, CH], F32))
            dps = scope.enter_context(nc.psum_tensor("down_ps", [P, 2, CH], F32))
            Q.need(m_zero)

            def step_up(u, i, s, c, f, kf, behind):
                st = FB * u + f
                if c == 0 and f == 0:
                    got[s].wait(nc.tensor, 32 * (i + 1))
                hid.wait(nc.tensor, st - behind)
                for j in range(2):
                    mm = nc.tensor.matmul(gups[:, kf, j, :], gu[s][:, j * FF + f * P:j * FF + (f + 1) * P],
                                          self.HT[:, c * CH:(c + 1) * CH], start=True, stop=True)
                gu_mm(mm)
                k2 = f % 2
                gu_mm.wait(nc.vector, st + 1)
                gate.wait(nc.vector, st - 1)
                clip(nc.vector.tensor_scalar(gc[k2][:], gups[:, kf, 0, :], -10.0, 10.0, ALU.max, ALU.min))
                clip.wait(nc.scalar, st + 1)
                hid.wait(nc.scalar, st - 1)
                gate(nc.scalar.activation(sg[k2][:], gc[k2][:], ACT.Silu))

            def step_hid(u, c, f, kf):
                st = FB * u + f
                gate.wait(nc.vector, st + 1)
                dn_mm.wait(nc.vector, u - 1)
                hid(nc.vector.tensor_tensor(act[c % 2][:, f, :], sg[f % 2][:], gups[:, kf, 1, :], ALU.mult))

            def down(u, s, c):
                hid.wait(nc.tensor, FB * (u + 1))
                summed.wait(nc.tensor, 4 * (u - 1))
                for j in range(4):
                    for f in range(FB):
                        mm = nc.tensor.matmul(dps[:, c % 2, j * P:(j + 1) * P], act[c % 2][:, f, j * P:(j + 1) * P],
                                              dn[s][:, f, :], start=(f == 0), stop=(f == FB - 1))
                dn_mm(mm)

            def add_up(u, e1, c):
                dn_mm.wait(nc.vector, u + 1)
                for j in range(4):
                    t = 4 * c + j
                    summed.wait(nc.vector, 4 * u)
                    summed(nc.vector.scalar_tensor_tensor(
                        out=acc[:, t, :], in0=dps[:, c % 2, j * P:(j + 1) * P],
                        scalar=comb[:, bass.ds(e1, 1), t], in1=acc[:, t, :], op0=ALU.mult, op1=ALU.add))

            def body(i, experts, fetch_next):
                k = 0
                late = None
                for s in range(2):
                    e = experts[s]
                    for c in range(NC):
                        u = NC * e + c
                        for f in range(FB):
                            step_up(u, i, s, c, f, k % 3, 1 if k < 2 else 2)
                            if late:
                                step_hid(*late)
                            late = (u, c, f, k % 3)
                            if f == 1:
                                down(u - 1, s if c else 1 - s, (c - 1) % NC)
                                add_up(u - 1, e + 1 if c else e, (c - 1) % NC)
                                if c == 0 and fetch_next[s]:
                                    fetch(e + 1, 1 - s)
                            k += 1
                step_hid(*late)

            fetch(0, 0)
            with nc.Fori(0, E // 2 - 1) as i:
                body(i, (2 * i, 2 * i + 1), (True, True))
            body(E // 2 - 1, (E - 2, E - 1), (True, False))
            u = NC * E - 1
            down(u, 1, NC - 1)
            add_up(u, E, NC - 1)
            summed.wait(nc.vector, 4 * NC * E)
            summed.wait(nc.gpsimd, 4 * NC * E)
            self.add_gated(acc, 1, 5, [None] * NT)
            self.settle()

    def store(self):
        nc, Q = self.nc, self.Q
        with ExitStack() as scope:
            stored = Arrival(scope, nc, "stored")
            for b in range(NB):
                stored(nc.sync.dma_start(self.out[b].rearrange("(k p) d -> p k d", p=P),
                                         self.X[:, b * TB:(b + 1) * TB, :]))
            nc.sync.wait_ge(stored.sem, stored.n)


_NAMES = ["WqT", "WkT", "WvT", "cn_w1", "cn_w2", "cn_w3", "cn_w4", "cn_b1", "cn_b2", "cn_b3", "cn_b4",
          "gc_w1", "gc_w2", "gc_w3", "gc_b1", "gc_b2", "gc_b3"]


def _layout(inputs):
    f = {k: np.ascontiguousarray(v) for k, v in inputs.items()}
    a = {"L0_attn_x": f["L0_attn_x"]}
    for l in range(2):
        a[f"cT{l}"] = f[f"L{l}_c"].T
        a[f"L{l}_wmod"] = f[f"L{l}_wmod"]
    for n in "qkv":
        a[f"W{n}T"] = f[f"L0_attn_W{n}"].T
    for net, layers in (("cn", 4), ("gc", 3)):
        for i in range(1, layers + 1):
            a[f"{net}_w{i}"] = f[f"L0_ffn_{net}_w{i}"]
            a[f"{net}_b{i}"] = f[f"L0_ffn_{net}_b{i}"][:, None]
    a["adaptive_range"] = f["L0_ffn_adaptive_range"][:, None]
    m = {k[8:]: f[k] for k in f if k.startswith("L1_attn_")}
    a["norm_w"] = m["norm_w"].T
    a["in_wT"] = m["in_proj_w"].transpose(0, 2, 1)
    a["conv_wT"] = m["conv_w"].reshape(NL, DI, KW).transpose(0, 2, 1)
    a["conv_b"] = m["conv_b"].reshape(NL, NBLK, P).transpose(2, 0, 1)
    a["xp_wT"] = m["x_proj_w"].transpose(2, 0, 1).reshape(NBLK, P, NL, DTR + 2 * DS).transpose(1, 0, 2, 3)
    a["dt_wT"] = m["dt_w"].transpose(2, 0, 1)
    a["dt_b"] = m["dt_b"][None]
    a["A_log"] = m["A_log"].reshape(NL, NBLK, P, DS).transpose(2, 0, 1, 3)
    a["Dp"] = m["Dp"].reshape(NL, NBLK, P).transpose(2, 0, 1)
    a["out_wT"] = m["out_w"].transpose(2, 0, 1).reshape(NBLK, P, NL, D).transpose(1, 0, 2, 3)
    a["ln_gamma"] = f["L1_ffn_ln_gamma"][:, None]
    a["ln_beta"] = f["L1_ffn_ln_beta"][:, None]
    a["router_w"] = f["L1_ffn_router_w"]
    a["gate_up_w"] = f["L1_ffn_gate_up_w"]
    a["down_w"] = f["L1_ffn_down_w"].reshape(E, FB, P, D).transpose(0, 2, 1, 3)
    a["shared_gate_up_w"] = f["L1_ffn_shared_gate_up_w"]
    a["shared_down_w"] = f["L1_ffn_shared_down_w"]
    eye = np.eye(P, dtype=np.float32)
    a["k_ident"] = eye
    a["k_groupsum"] = np.tile(np.eye(32, dtype=np.float32), (4, 1))
    twist = np.zeros((P, P), np.float32)
    for to, frm, sign in ((0, 2, 1.0), (1, 3, -1.0), (2, 0, -1.0), (3, 1, 1.0)):
        twist[32 * frm + np.arange(32), 32 * to + np.arange(32)] = sign
    a["k_twist"] = twist
    a["k_rows"] = np.tile(np.eye(2 * DS, dtype=np.float32), (3, 1))
    a["k_iota"] = np.tile(np.arange(E, dtype=np.float32), (P, 1))
    return {k: np.ascontiguousarray(v) for k, v in a.items()}


def kernel(**inputs):
    import concourse.bacc as bacc
    from concourse.bass_utils import run_bass_kernel_spmd

    nc = bacc.Bacc("TRN2", target_bir_lowering=False, num_devices=1)
    arrays = _layout(inputs)
    args = {n: nc.dram_tensor(f"in_{n}", a.shape, mybir.dt.from_np(a.dtype), kind="ExternalInput").ap()
            for n, a in arrays.items()}
    out = nc.dram_tensor("out", (NB, S, D), F32, kind="ExternalOutput").ap()
    build(nc, args, out)
    r = run_bass_kernel_spmd(nc, [{f"in_{n}": a for n, a in arrays.items()}], core_ids=[0])
    return r.results[0]["out"]
```

```python
from contextlib import ExitStack
from itertools import count

import numpy as np

import concourse.bass as bass
from concourse import mybir

F32 = mybir.dt.float32
BF16 = mybir.dt.bfloat16
U32 = mybir.dt.uint32
ALU = mybir.AluOpType
ACT = mybir.ActivationFunctionType
AX_X = mybir.AxisListType.X

P = 128
NB = 2
S = 1024
D = 128
TOK = NB * S
NT = TOK // P
TB = S // P
CH = 512
NC = TOK // CH
H, HD = 16, 8
BH = NB * H
DI, DS, DTR, KW = 256, 16, 8, 4
NBLK = DI // P
NL = 2
E, FF = 8, 512
FB = FF // P
EPS = 1e-5
BETA = 0.6
CPL_COLS = ("cn_b1", "cn_b2", "cn_b3", "cn_w4", "cn_b4", "gc_b1", "gc_b2", "gc_w3", "gc_b3", "adaptive_range")


_keys = count()


class Track:

    def __init__(self, ctx, nc, engine, name):
        self.engine = engine
        self.sem = ctx.enter_context(nc.semaphore(f"done_{name}"))
        self.n = 0
        self.key = next(_keys)
        self.seen = {}

    def __call__(self, instruction):
        instruction.then_inc(self.sem, 1)
        self.n += 1
        return (self.sem, self.n, self.key)

    def need(self, *marks):
        for mark in marks:
            if mark is None:
                continue
            sem, n, key = mark
            if self.seen.get(key, 0) < n:
                self.engine.wait_ge(sem, n)
                self.seen[key] = n

    def last(self):
        return (self.sem, self.n, self.key) if self.n else None


class Arrival:

    def __init__(self, ctx, nc, name):
        self.sem = ctx.enter_context(nc.semaphore(name))
        self.n = 0
        self.key = next(_keys)

    def __call__(self, instruction):
        instruction.then_inc(self.sem, 16)
        self.n += 16

    def mark(self):
        return (self.sem, self.n, self.key)


class Event:

    def __init__(self, ctx, nc, name, engine, before=0, credit=32):
        self.sem = ctx.enter_context(nc.semaphore(name))
        self.credit = credit
        engine.sem_inc(self.sem, credit - before)

    def __call__(self, instruction, by=1):
        instruction.then_inc(self.sem, by)
        return instruction

    def wait(self, engine, count):
        engine.wait_ge(self.sem, count + self.credit)


class Banks:

    def __init__(self, tensors):
        self.tensors = tensors
        self.free = [()] * len(tensors)
        self.at = 0

    def take(self, writer):
        k = self.at % len(self.tensors)
        self.at += 1
        writer.need(*self.free[k])
        return k, self.tensors[k]

    def release(self, k, *marks):
        self.free[k] = marks


def build(nc, A, out):
    ctx = ExitStack()
    with ctx:
        V = Track(ctx, nc, nc.vector, "vector")
        S_ = Track(ctx, nc, nc.scalar, "scalar")
        G = Track(ctx, nc, nc.gpsimd, "gpsimd")
        T = Track(ctx, nc, nc.tensor, "tensor")
        Q = Track(ctx, nc, nc.sync, "sync")
        K = Kernel(nc, ctx, A, out, V, S_, G, T, Q)
        K.constants()
        K.attention()
        K.coupling()
        K.mamba()
        K.experts()
        K.store()


class Kernel:
    def __init__(self, nc, ctx, A, out, V, S_, G, T, Q):
        self.nc, self.ctx, self.A, self.out = nc, ctx, A, out
        self.V, self.S, self.G, self.T, self.Q = V, S_, G, T, Q
        self.tracks = (V, S_, G, T)
        self.serial = 0

    def sb(self, scope, name, shape, dt=F32):
        return scope.enter_context(self.nc.sbuf_tensor(name, shape, dt))

    def banks(self, scope, name, n, dt=F32):
        return Banks([scope.enter_context(self.nc.psum_tensor(f"{name}{k}", [P, CH], dt)) for k in range(n)])

    def settle(self):
        for t in self.tracks + (self.Q,):
            t.need(*[o.last() for o in self.tracks])

    def constants(self):
        nc, A, ctx = self.nc, self.A, self.ctx
        sb = lambda n, s, d=F32: self.sb(ctx, n, s, d)
        self.X = sb("x", [P, NT, D])
        self.HT = sb("h_t", [P, TOK])
        self.N = sb("normed", [P, NT, D])
        self.ident = sb("ident", [P, P])
        self.identb = sb("identb", [P, P], BF16)
        self.half = sb("minus_half", [P, NT])
        self.stat = sb("bn_parts", [P, NT, 6])
        self.mv = sb("mean_var", [P, NT, 2])
        self.ve = sb("var_eps", [P, NT])
        self.rs = sb("rstd", [P, NT])
        self.cT = [sb(f"c_t{l}", [P, NB]) for l in range(2)]
        self.sil = [sb(f"silu_c{l}", [P, NB]) for l in range(2)]
        self.silrep = [sb(f"silu_rep{l}", [P, NB, P]) for l in range(2)]
        self.wmod = [sb(f"wmod{l}", [P, 6 * D]) for l in range(2)]
        self.mcol = [sb(f"mod_col{l}", [P, 6, NB]) for l in range(2)]
        self.mrow = [sb(f"mod_row{l}", [P, NB, 6, D]) for l in range(2)]
        self.gtmp = {n: sb(f"gate_tmp{n}", [P, 2 * n]) for n in (NB, NB * D)}

        self.in_x = Arrival(ctx, nc, "in_x")
        self.in_c = Arrival(ctx, nc, "in_c")
        self.in_k = Arrival(ctx, nc, "in_k")
        for l in range(2):
            self.in_c(nc.scalar.dma_start(self.cT[l][:], A[f"cT{l}"]))
            self.in_c(nc.scalar.dma_start(self.wmod[l][:], A[f"L{l}_wmod"]))
        for b in range(NB):
            self.in_x(nc.sync.dma_start(self.X[:, b * TB:(b + 1) * TB, :],
                                        A["L0_attn_x"][b].rearrange("(k p) d -> p k d", p=P)))
        self.in_k(nc.sync.dma_start(self.ident[:], A["k_ident"]))
        self.m_half = self.G(nc.gpsimd.memset(self.half[:], -0.5))
        self.S.need(self.in_k.mark())
        self.m_identb = self.S(nc.scalar.activation(self.identb[:], self.ident[:], ACT.Copy))

    def mod_cols(self, l, ring):
        nc, V, S_, T = self.nc, self.V, self.S, self.T
        S_.need(self.in_c.mark())
        self.m_silu = S_(nc.scalar.activation(self.sil[l][:], self.cT[l][:], ACT.Silu))
        T.need(self.m_silu, self.in_c.mark())
        k, ps = ring.take(T)
        for i in range(6):
            mm = nc.tensor.matmul(ps[:, i * NB:(i + 1) * NB], self.wmod[l][:, i * D:(i + 1) * D],
                                  self.sil[l][:], start=True, stop=True)
        V.need(T(mm))
        m = self.mcol[l]
        col = V(nc.vector.tensor_copy(m[:].rearrange("p i b -> p (i b)"), ps[:, 0:6 * NB]))
        ring.release(k, col)
        self.m_col = self.finish_mod(V, nc.vector, lambda i: m[:, i, :], col)

    def mod_rows_of(self, l, ring):
        nc, V, S_, T, G = self.nc, self.V, self.S, self.T, self.G
        V.need(self.m_silu)
        T.need(V(nc.vector.tensor_copy(self.silrep[l][:], self.sil[l][:, :, None].to_broadcast([P, NB, P]))))
        for b in range(NB):
            for lo, hi in ((0, CH), (CH, 6 * D)):
                k, ps = ring.take(T)
                S_.need(T(nc.tensor.matmul(ps[:, 0:hi - lo], self.silrep[l][:, b, :], self.wmod[l][:, lo:hi],
                                           start=True, stop=True)))
                row = S_(nc.scalar.activation(self.mrow[l][:, b].rearrange("p i d -> p (i d)")[:, lo:hi],
                                              ps[:, 0:hi - lo], ACT.Copy))
                ring.release(k, row)
        return G, nc.gpsimd, lambda i: self.mrow[l][:, :, i, :], row

    def finish_mod(self, eng, e, part, mark):
        eng.need(mark)
        for i in (1, 4):
            mark = eng(e.tensor_scalar(part(i), part(i), 1.0, None, ALU.add))
        for i in (2, 5):
            eng.need(mark)
            g = part(i)
            shape = list(g.shape)[1:]
            n = int(np.prod(shape))
            tmp = [self.gtmp[n][:, k * n:(k + 1) * n] for k in range(2)]
            if len(shape) == 2:
                tmp = [t.rearrange("p (b d) -> p b d", b=shape[0]) for t in tmp]
            sign, size = tmp
            for step in (lambda: e.tensor_scalar(sign, g, 0.0, 2.0, ALU.is_ge, ALU.mult),
                         lambda: e.tensor_scalar(sign, sign, 1.0, None, ALU.subtract),
                         lambda: e.tensor_tensor(size, sign, g, ALU.mult),
                         lambda: e.tensor_scalar(size, size, 0.25, None, ALU.max)):
                m = eng(step())
                eng.need(m)
            mark = eng(e.tensor_tensor(g, sign, size, ALU.mult))
        return mark

    def rstd(self, ts, src, scale, *marks):
        nc, G = self.nc, self.G
        G.need(self.m_half, *marks)
        a = G(nc.gpsimd.tensor_scalar(self.ve[:, ts], src, scale, EPS, ALU.mult, ALU.add))
        G.need(a)
        return G(nc.gpsimd.tensor_tensor(self.rs[:, ts], self.ve[:, ts], self.half[:, ts], ALU.pow))

    def layer_norm(self, src, marks=(None,) * NT):
        nc, V, G = self.nc, self.V, self.G
        roots = []
        for b in range(NB):
            tiles = range(b * TB, (b + 1) * TB)
            for t in tiles:
                V.need(marks[t])
                m = V(nc.vector.bn_stats(self.stat[:, t, :], src[:, t, :]))
            V.need(m)
            for t in tiles:
                m = V(nc.vector.bn_aggr(self.mv[:, t, :], self.stat[:, t, :]))
            roots.append(self.rstd(slice(b * TB, (b + 1) * TB), self.mv[:, b * TB:(b + 1) * TB, 1], 1.0, m))
        V.need(m)
        normed = []
        for t in range(NT):
            V.need(roots[t // TB])
            normed.append(V(nc.vector.tensor_scalar(self.N[:, t, :], src[:, t, :], self.mv[:, t, 0:1],
                                                    self.rs[:, t:t + 1], ALU.subtract, ALU.mult)))
        return normed

    def parts(self):
        cuts = (0, TB, 3 * TB // 2, NT)
        return [(t, e, slice(at, to), at // TB) for t, e, at, to in
                zip((self.V, self.V, self.G), (self.nc.vector, self.nc.vector, self.nc.gpsimd), cuts, cuts[1:])]

    def add_gated(self, src, l, i, marks):
        done = []
        for eng, e, ts, b in self.parts():
            n = ts.stop - ts.start
            eng.need(*marks[ts])
            row = self.mrow[l][:, b, i:i + 1, :].to_broadcast([P, n, D])
            m = eng(e.tensor_tensor(src[:, ts, :], src[:, ts, :], row, ALU.mult))
            eng.need(m)
            done += [eng(e.tensor_tensor(self.X[:, ts, :], self.X[:, ts, :], src[:, ts, :], ALU.add))] * n
        return done

    def turn(self, ring, marks, scale, bias, extra=(), to=None):
        nc, S_, T, V = self.nc, self.S, self.T, self.V
        done = []
        T.need(self.in_k.mark())
        for c in range(NC):
            k, ps = ring.take(T)
            for j in range(4):
                T.need(marks[4 * c + j])
                mm = nc.tensor.transpose(ps[:, j * P:(j + 1) * P], self.N[:, 4 * c + j, :], self.ident[:])
            mm = T(mm)
            b = c // 2
            eng = (S_, V)[c % 2]
            eng.need(mm, *extra)
            dst = to(c) if to else self.HT[:, c * CH:(c + 1) * CH]
            if eng is S_:
                m = S_(nc.scalar.activation(dst, ps[:], ACT.Identity, scale=scale(b),
                                            bias=bias(b) if bias else 0.0))
            elif bias:
                m = V(nc.vector.tensor_scalar(dst, ps[:], scale(b), bias(b), ALU.mult, ALU.add))
            else:
                m = V(nc.vector.tensor_scalar(dst, ps[:], scale(b), None, ALU.mult))
            ring.release(k, m)
            done.append(m)
        return done

    def attention(self):
        nc, A, V, S_, G, T, Q = self.nc, self.A, self.V, self.S, self.G, self.T, self.Q
        with ExitStack() as scope:
            sb = lambda n, s, d=F32: self.sb(scope, n, s, d)
            parts = nc.dram_tensor("qk_parts", (2, 3, BH, HD, S), BF16, kind="Internal").ap()
            w = sb("w_qkv", [P, 3, D])
            in_w = Arrival(scope, nc, "in_wqkv")
            for i, n in enumerate(("WqT", "WkT", "WvT")):
                in_w(nc.scalar.dma_start(w[:, i, :], A[n]))
            sel = sb("group_sum", [P, 32])
            in_w(nc.scalar.dma_start(sel[:], A["k_groupsum"]))
            vt = sb("v_tok", [P, BH, TB, HD])
            ox = sb("attn_out", [P, BH + 2, TB, HD])
            NS = 4
            qp = [sb(f"q_rows{s}", [P, S], BF16) for s in range(NS)]
            kp = [sb(f"k_rows{s}", [P, S], BF16) for s in range(NS)]
            va = [sb(f"v_cols{s}", [P, TB, 32]) for s in range(2)]
            pt = [sb(f"exp_scores{s}", [P, 4, CH]) for s in range(2)]
            mx = [sb(f"max_halves{s}", [P, TB, 2]) for s in range(2)]
            nm = sb("neg_max", [P, TB])
            nr = sb("neg_max_rest", [P, TB])
            ms = [sb(f"neg_max_parts{s}", [P, 3, TB], BF16) for s in range(2)]
            mt = [sb(f"neg_max_rows{s}", [3 * TB, P], BF16) for s in range(2)]
            ot = [sb(f"av_t{s}", [P, CH]) for s in range(2)]
            rc = [sb(f"recip{s}", [P, 4, 2]) for s in range(2)]

            KR, KM = 96, 99
            for s in range(NS):
                V(nc.vector.memset(qp[s][64:128, :], 0.0))
                V(nc.vector.memset(kp[s][64:96, :], 0.0))
                rows_set = V(nc.vector.memset(kp[s][96:128, :], 1.0))
            for s in range(2):
                a = G(nc.gpsimd.memset(va[s][:], 0.0))
                a = G(nc.gpsimd.memset(pt[s][:], 1.0))
                a = G(nc.gpsimd.memset(ot[s][:], 1.0))
            G.need(a)
            for s in range(2):
                a = G(nc.gpsimd.memset(va[s][:, :, 16 * s + HD:16 * s + HD + 1], 1.0))
            set_up = a

            ev = lambda n, e, before=0: Event(scope, nc, n, e, before, 96)
            loaded = [ev(f"loaded{s}", nc.sync) for s in range(NS)]
            max_in = [ev(f"max_in{s}", nc.sync) for s in range(NS)]
            ring_mm = ev("ring_mm", nc.tensor, 33)
            ring_read = ev("ring_read", nc.vector, 33)
            split = ev("max_split", nc.vector)
            s2_mm, exped = ev("s2_mm", nc.tensor), ev("exped", nc.scalar)
            av_mm, av_out = ev("av_mm", nc.tensor, 3), ev("av_out", nc.scalar, 1)
            out_mm = ev("out_mm", nc.tensor, 1)
            recips, divided = ev("recips", nc.vector, 1), ev("divided", nc.vector, 1)
            v_put = ev("v_put", nc.gpsimd)
            ND = 12
            ORDER = ("EBEBBQBEBEBOBQTBEBEBDBQBEBEBBQB", "EBEBBQBEBEBBQTBEBEBBQBEBEBOBQDB")
            SC = float(HD) ** -0.5

            def load(h, s):
                s2_mm.wait(nc.sync, 8 * (h - 3))
                for i in range(3):
                    loaded[s](nc.sync.dma_start(kp[s][24 * i:24 * i + 24, :],
                                                parts[1][:, bass.ds(h, 1)].rearrange("p a d t -> (p a) d t")), 16)
                    for j in range(3):
                        loaded[s](nc.sync.dma_start(qp[s][24 * i + 8 * j:24 * i + 8 * j + 8, :],
                                                    parts[0][i, bass.ds(h, 1)].rearrange("a d t -> (a d) t")), 16)

            normed = self.layer_norm(self.X, (self.in_x.mark(),) * NT)
            with ExitStack() as pre:
                ring = self.banks(pre, "pre_ps", 8)
                self.mod_cols(0, ring)
                rows = [self.mod_rows_of(0, ring)]
                ht = self.turn(ring, normed, lambda b: self.mcol[0][:, 1, b:b + 1],
                               lambda b: self.mcol[0][:, 0, b:b + 1], (self.m_col,))
                p = [self.sb(pre, f"part{i}", [P, 2, TOK], BF16) for i in range(3)]
                rest = self.sb(pre, "part_rest", [P, 2, TOK])
                T.need(in_w.mark())
                wrote = {}
                to_dram = [Arrival(scope, nc, f"parts_out{b}") for b in range(NB)]
                for c in range(NC):
                    cs = slice(c * CH, (c + 1) * CH)
                    T.need(ht[c])
                    for side in range(2):
                        k, ps = ring.take(T)
                        mm = T(nc.tensor.matmul(ps[:], w[:, side, :], self.HT[:, cs], start=True, stop=True))
                        S_.need(mm)
                        a = S_(nc.scalar.activation(p[0][:, side, cs], ps[:], ACT.Copy))
                        V.need(a)
                        b_ = V(nc.vector.tensor_tensor(rest[:, side, cs], ps[:], p[0][:, side, cs], ALU.subtract))
                        ring.release(k, b_)
                        V.need(b_)
                        c_ = V(nc.vector.tensor_copy(p[1][:, side, cs], rest[:, side, cs]))
                        G.need(c_)
                        d_ = G(nc.gpsimd.tensor_tensor(p[2][:, side, cs], rest[:, side, cs], p[1][:, side, cs],
                                                       ALU.subtract))
                        wrote[side, c] = (a, c_, d_)
                    if c % 2:
                        b = c // 2
                        for side in range(2):
                            Q.need(*wrote[side, c], *wrote[side, c - 1])
                            for i in range(3):
                                to_dram[b](nc.sync.dma_start(
                                    parts[side, i, b * H:(b + 1) * H].rearrange("h d t -> (h d) t"),
                                    p[i][:, side, b * S:(b + 1) * S]))
                    k, ps = ring.take(T)
                    for j in range(4):
                        tile = 4 * c + j
                        mm = nc.tensor.matmul(ps[:, j * P:(j + 1) * P], self.HT[:, tile * P:(tile + 1) * P],
                                              w[:, 2, :], start=True, stop=True)
                    mm = T(mm)
                    S_.need(mm)
                    b, k0 = c // 2, (c % 2) * 4
                    for j in range(4):
                        v_done = S_(nc.scalar.activation(
                            vt[:, b * H:(b + 1) * H, k0 + j, :],
                            ps[:, j * P:(j + 1) * P].rearrange("p (h d) -> p h d", h=H), ACT.Copy))
                    ring.release(k, v_done)
                Q.need(set_up, rows_set)
                Q.engine.wait_ge(to_dram[0].sem, to_dram[0].n)
                for h in range(3):
                    load(h, h)
                Q.engine.wait_ge(to_dram[1].sem, to_dram[1].n)
                self.mod_cols(1, ring)
                rows.append(self.mod_rows_of(1, ring))
                self.settle()

            sc1 = scope.enter_context(nc.psum_tensor("score_q", [P, 2, CH], F32))
            sc2 = scope.enter_context(nc.psum_tensor("score_k", [P, 2, 2, CH], F32))
            avp = scope.enter_context(nc.psum_tensor("av_ps", [P, 2, CH], F32))

            class Ring:
                PAIR = 2 * (2 * TB + 1)
                base, p = -33, 0

                def step(self):
                    g, bank = self.base + self.p, (self.p + self.odd) % 2
                    self.p += 1
                    ring_read.wait(nc.tensor, g - 1)
                    return g, bank

                def enter(self, base, odd):
                    self.base, self.p, self.odd = base, 0, odd

                def here(self):
                    return self.base + self.p

            ring = Ring()

            def max_score(h, s, turn, j):
                if j == 0:
                    loaded[s].wait(nc.tensor, 16 * ND * (turn + 1))
                    split.wait(nc.vector, 5 * (h - 1))
                qt, kh = j // 2, j % 2
                g, bank = ring.step()
                ring_mm(nc.tensor.matmul(sc1[:, bank, :], qp[s][0:KR, qt * P:(qt + 1) * P],
                                         kp[s][0:KR, kh * CH:(kh + 1) * CH], start=True, stop=True))
                ring_mm.wait(nc.vector, g + 1)
                ring_read(nc.vector.tensor_reduce(mx[s % 2][:, qt, kh:kh + 1], sc1[:, bank, :], AX_X, ALU.max))

            def max_part(h, s, k, start):
                z, o, e = mx[s % 2], ms[s % 2], nc.vector
                if k:
                    split.wait(e, 5 * h + k)
                else:
                    ring_read.wait(e, start)
                    ring_mm.wait(e, start)
                split((lambda: e.tensor_reduce(nm[:], z[:], AX_X, ALU.max, negate=True),
                       lambda: e.tensor_copy(o[:, 0, :], nm[:]),
                       lambda: e.tensor_tensor(nr[:], nm[:], o[:, 0, :], ALU.subtract),
                       lambda: e.tensor_copy(o[:, 1, :], nr[:]),
                       lambda: e.tensor_tensor(o[:, 2, :], nr[:], o[:, 1, :], ALU.subtract))[k]())

            def max_turn(h, s, turn):
                split.wait(nc.tensor, 5 * h + 5)
                g, bank = ring.step()
                mtp = sc1[:, bank, 0:64].bitcast(BF16)
                ring_mm(nc.tensor.transpose(mtp[0:3 * TB, :], ms[s % 2][:].rearrange("p a k -> p (a k)"),
                                            self.identb[:]))
                ring_mm.wait(nc.vector, g + 1)
                max_in[(s - 2) % NS].wait(nc.vector, 48 * ((turn if s >= 2 else turn - 1) + 1))
                ring_read(nc.vector.tensor_copy(mt[s % 2][:], mtp[0:3 * TB, :]))
                ring_read.wait(nc.sync, g + 1)
                for i in range(3):
                    max_in[s](nc.sync.dma_start(
                        qp[s][96 + i:97 + i, :].rearrange("a (k q) -> a k q", k=TB),
                        mt[s % 2][TB * i:TB * i + TB, :]), 16)

            def put_v(h, s):
                av_mm.wait(nc.gpsimd, 4 * (h - 1))
                v_put(nc.gpsimd.tensor_copy(va[s % 2][:, :, 16 * (s % 2):16 * (s % 2) + HD],
                                            vt[:, bass.ds(h, 1), :, :].rearrange("p a k d -> p (a k) d")))

            def exp_pair(h, s, turn, r):
                if r == 0:
                    max_in[s].wait(nc.tensor, 48 * (turn + 1))
                qh, kt = r // 4, (r % 4) * 2
                exped.wait(nc.tensor, 8 * h + r - 1)
                for j in range(2):
                    mm = nc.tensor.matmul(sc2[:, r % 2, j, :], kp[s][0:KM, (kt + j) * P:(kt + j + 1) * P],
                                          qp[s][0:KM, qh * CH:(qh + 1) * CH], start=True, stop=True)
                s2_mm(mm)
                if r % 2 == 0:
                    av_mm.wait(nc.scalar, 4 * h + r // 2 - 1)
                s2_mm.wait(nc.scalar, 8 * h + r + 1)
                exped(nc.scalar.activation(pt[(r // 2) % 2][:, (r % 2) * 2:(r % 2) * 2 + 2, :],
                                           sc2[:, r % 2], ACT.Exp, scale=SC))

            def av_quad(h, s, u, pair):
                if u == 0:
                    v_put.wait(nc.tensor, h + 1)
                if s % 2 == 0 and u % 2 == 0:
                    divided.wait(nc.tensor, 2 * pair - 1 + u // 2)
                exped.wait(nc.tensor, 8 * h + 2 * u + 2)
                for j in range(4):
                    mm = nc.tensor.matmul(avp[32 * j:32 * j + 32, u // 2, :], va[s % 2][:, 4 * (u % 2) + j, :],
                                          pt[u % 2][:, j, :], start=(s % 2 == 0 and u % 2 == 0),
                                          stop=(s % 2 == 1 and u % 2 == 1))
                av_mm(mm)

            def av_evac(h, qh, pair):
                av_mm.wait(nc.scalar, 4 * h + 2 * qh + 2)
                out_mm.wait(nc.scalar, 2 * pair - 1 + qh)
                av_out(nc.scalar.activation(ot[qh][:], avp[:, qh, :], ACT.Copy))

            def out_rows(qh):
                return avp[:, qh, 0:P].rearrange("p (k c) -> p k c", c=32)

            def out_turn(pair, qh):
                av_out.wait(nc.tensor, 2 * pair + 1 + qh)
                for k in range(4):
                    mm = nc.tensor.matmul(out_rows(qh)[:, k, :], ot[qh][:, k * P:(k + 1) * P], sel[:],
                                          start=True, stop=True)
                out_mm(mm)

            def divide(pair, qh):
                res = out_rows(qh).rearrange("p k (a c) -> p k a c", a=2)
                divided.wait(nc.vector, 2 * pair - 1 + qh)
                out_mm.wait(nc.vector, 2 * pair + 1 + qh)
                recips(nc.vector.reciprocal(rc[qh][:], res[:, :, :, HD]))
                recips.wait(nc.vector, 2 * pair + 1 + qh)
                divided(nc.vector.tensor_tensor(
                    ox[:, bass.ds(2 * pair + 2, 2), 4 * qh:4 * qh + 4, :].rearrange("p a k d -> p k a d"),
                    res[:, :, :, 0:HD], rc[qh][:][:, :, :, None].to_broadcast([P, 4, 2, HD]), ALU.mult))

            def head(h, s, turn, pair, ahead=3):
                start = ring.here()
                s1, t1, s2, t2 = (s + 1) % NS, turn + (s + 1) // NS, (s + 2) % NS, turn + (s + 2) // NS
                if ahead >= 3:
                    load(h + 3, (s + 3) % NS)
                put_v(h, s)
                done = dict.fromkeys("EQBTOD", 0)
                for step in ORDER[s % 2]:
                    n = done[step]
                    done[step] += 1
                    if step == "E":
                        exp_pair(h, s, turn, n)
                    elif step == "B":
                        if ahead >= 2:
                            max_score(h + 2, s2, t2, n)
                        if ahead >= 1 and n < 5:
                            max_part(h + 1, s1, n, start)
                    elif step == "T" and ahead >= 1:
                        max_turn(h + 1, s1, t1)
                    elif step == "Q" and n == 0:
                        av_quad(h - 1, s - 1, 3, pair - 1)
                        if s % 2 == 0:
                            av_evac(h - 1, 1, pair - 1)
                    elif step == "Q":
                        av_quad(h, s, n - 1, pair)
                        if s % 2 and n == 2:
                            av_evac(h, 0, pair)
                    elif step == "O":
                        out_turn(pair - 1 + s % 2, 1 - s % 2)
                    elif step == "D":
                        divide(pair - 1 + s % 2, 1 - s % 2)

            av_quad(-2, -2, 2, -1)
            av_quad(-1, -1, 2, -1)
            av_mm.wait(nc.gpsimd, -1)
            ring.enter(-33, 1)
            for j in range(2 * TB):
                max_score(0, 0, 0, j)
            start = ring.here()
            for j in range(2 * TB):
                max_score(1, 1, 0, j)
                if j < 5:
                    max_part(0, 0, j, start)
                if j == 9:
                    max_turn(0, 0, 0)
            LOOPS = BH // NS - 1
            with nc.Fori(0, LOOPS) as i:
                ring.enter(i * (2 * Ring.PAIR), 0)
                for s in range(NS):
                    head(i * NS + s, s, i, 2 * i + s // 2)
                assert ring.p == 2 * Ring.PAIR
            ring.enter(LOOPS * 2 * Ring.PAIR, 0)
            for s in range(NS):
                h = BH - NS + s
                head(h, s, LOOPS, h // 2, ahead=BH - 1 - h)
                if s < 2:
                    self.m_row = self.finish_mod(*rows[s])
            av_quad(BH - 1, NS - 1, 3, BH // 2 - 1)
            av_evac(BH - 1, 1, BH // 2 - 1)
            out_turn(BH // 2 - 1, 1)
            divide(BH // 2 - 1, 1)

            divided.wait(nc.vector, BH)
            tmp = self.N
            for b in range(NB):
                xb = self.X[:, b * TB:(b + 1) * TB, :]
                tb = tmp[:, b * TB:(b + 1) * TB, :]
                for k in range(TB):
                    a = V(nc.vector.tensor_tensor(
                        tb[:, k].rearrange("p (h d) -> p h d", h=H), ox[:, 2 + b * H:2 + (b + 1) * H, k, :],
                        self.mrow[0][:, b, 2, :].rearrange("p (h d) -> p h d", h=H), ALU.mult))
                V.need(a)
                a = V(nc.vector.tensor_tensor(xb, xb, tb, ALU.add))
            for e in (nc.tensor, nc.scalar, nc.gpsimd, nc.sync, nc.vector):
                divided.wait(e, BH)
            self.settle()

    def coupling(self):
        nc, A, V, S_, G, T, Q = self.nc, self.A, self.V, self.S, self.G, self.T, self.Q
        with ExitStack() as scope:
            sb = lambda n, s, d=F32: self.sb(scope, n, s, d)
            in_w = Arrival(scope, nc, "in_coupling")
            cols = sb("coupling_cols", [P, len(CPL_COLS)])
            in_w(nc.sync.dma_start(cols[:], A["cpl_cols"]))
            wt = {}
            for k, (n, d) in enumerate((("cn_w1", (D, D)), ("cn_w2", (D, D // 2)), ("cn_w3x2", (D, D // 4)),
                                        ("gc_w1", (D, D // 2)), ("gc_w2", (D // 2, D // 4)))):
                wt[n] = sb(n, d)
                in_w((nc.sync, nc.scalar)[k % 2].dma_start(wt[n][:], A[n]))
            col = lambda n, rows=P: cols[0:rows, CPL_COLS.index(n):CPL_COLS.index(n) + 1]
            bs = {("cn", i): col(f"cn_b{i}") for i in (1, 2, 3)}
            bs["gc", 1], bs["gc", 2] = col("gc_b1", D // 2), col("gc_b2", D // 4)
            rng = col("adaptive_range")
            twist = sb("twist", [P, P])
            in_w(nc.sync.dma_start(twist[:], A["k_twist"]))
            wlast = {"cn": sb("cn_w4_rep", [P, P]), "gc": sb("gc_w3_rep", [D // 4, P])}
            blast = {"cn": sb("cn_b4_half", [P, 1]), "gc": sb("gc_b3_half", [P, 1])}
            alpha, beta = sb("cpl_alpha", [P, 1]), sb("cpl_beta", [P, NB])
            mean = sb("token_sum", [P, NB])
            g1, g2, g3 = sb("ctx1", [D // 2, NB]), sb("ctx2", [D // 4, NB]), sb("ctx3", [P, NB])
            h1 = [sb(f"net1_{c}", [D, CH]) for c in range(NC)]
            h2 = [sb(f"net2_{c}", [P, CH]) for c in range(2)]
            h3 = sb("net3", [P, CH])
            assert NC == 4
            cp = [sb(f"coupling_{c}", [P, CH]) for c in range(NC)]
            ring = self.banks(scope, "cpl_ps", 8)
            U = self.HT
            normed = self.layer_norm(self.X)
            V.need(in_w.mark())
            for net, i in (("cn", 4), ("gc", 3)):
                rows = wlast[net].shape[0]
                V(nc.vector.tensor_copy(wlast[net][:], col(f"{net}_w{i}", rows).to_broadcast([rows, P])))
                m_b = V(nc.vector.tensor_scalar(blast[net][:], col(f"{net}_b{i}"), 0.5, None, ALU.mult))
            m_b = V(nc.vector.tensor_scalar(alpha[:], rng, 0.3, None, ALU.mult))
            ht = self.turn(ring, normed, lambda b: self.mcol[0][:, 4, b:b + 1],
                           lambda b: self.mcol[0][:, 3, b:b + 1], (self.m_col,))
            for b in range(NB):
                V.need(ht[2 * b], ht[2 * b + 1])
                means = V(nc.vector.tensor_reduce(mean[:, b:b + 1], U[:, b * S:(b + 1) * S], AX_X, ALU.add))
            T.need(in_w.mark(), m_b)
            S_.need(in_w.mark(), m_b)

            def context(i, src, dst, mark):
                T.need(mark)
                k, ps = ring.take(T)
                n = dst.shape[0]
                w = wlast["gc"][:] if i == 3 else wt[f"gc_w{i}"][:]
                mm = T(nc.tensor.matmul(ps[0:n, 0:NB], w, src[:], start=True, stop=True))
                S_.need(mm)
                if i < 3:
                    m = S_(nc.scalar.activation(dst[:], ps[0:n, 0:NB], ACT.Gelu, bias=bs["gc", i],
                                                scale=1.0 / S if i == 1 else 1.0))
                else:
                    m = S_(nc.scalar.activation(dst[:], ps[0:n, 0:NB], ACT.Tanh, bias=blast["gc"][:], scale=0.5))
                ring.release(k, m)
                if i == 3:
                    V.need(m)
                    m = V(nc.vector.tensor_scalar(beta[:], g3[:], rng, 0.7, ALU.mult, ALU.mult))
                    V.need(m)
                    m = V(nc.vector.tensor_scalar(beta[:], beta[:], 0.1, None, ALU.add))
                    V.need(m)
                return m

            ready = [(ht[c],) for c in range(NC)]
            turned = [None] * NC
            def twisted(c):
                k, ps = ring.take(T)
                turned[c] = k, ps, T(nc.tensor.matmul(ps[:], twist[:], U[:, c * CH:(c + 1) * CH],
                                                      start=True, stop=True))

            def couple(c):
                cs = slice(c * CH, (c + 1) * CH)
                b = c // 2
                k, ps, mm = turned[c]
                V.need(marks[c])
                m = V(nc.vector.tensor_scalar(cp[c][:], cp[c][:], alpha[:], beta[:, b:b + 1], ALU.mult, ALU.add))
                V.need(m, mm)
                m = V(nc.vector.tensor_tensor(cp[c][:], ps[:], cp[c][:], ALU.mult))
                ring.release(k, m)
                V.need(m)
                m = V(nc.vector.tensor_tensor(U[:, cs], U[:, cs], cp[c][:], ALU.add))
                ready[c] = (m,)

            def activate(k, ps, mm, func, dst, net_bias, scale=1.0):
                S_.need(mm)
                m = S_(nc.scalar.activation(dst[:], ps[:], func, bias=net_bias[:], scale=scale))
                ring.release(k, m)
                return m

            for cycle in range(3):
                marks = [None] * NC
                for c in range(NC):
                    k, ps = ring.take(T)
                    T.need(*ready[c])
                    mm = T(nc.tensor.matmul(ps[:], wt["cn_w1"][:], U[:, c * CH:(c + 1) * CH], start=True, stop=True))
                    marks[c] = activate(k, ps, mm, ACT.Gelu, h1[c], bs["cn", 1])
                if cycle == 0:
                    means = context(1, mean, g1, means)
                half = []
                for pair in range(2):
                    k, ps = ring.take(T)
                    for j in range(2):
                        T.need(marks[2 * pair + j])
                        mm = nc.tensor.matmul(ps[j * 64:j * 64 + 64, :], wt["cn_w2"][:], h1[2 * pair + j][:],
                                              start=True, stop=True)
                    half.append(activate(k, ps, T(mm), ACT.Gelu, h2[pair], bs["cn", 2]))
                twisted(0)
                if cycle == 0:
                    means = context(2, g1, g2, means)
                twisted(1)
                k, ps = ring.take(T)
                T.need(*half)
                for c in range(NC):
                    rows = slice(c % 2 * 64, c % 2 * 64 + 64)
                    mm = nc.tensor.matmul(ps[c * 32:c * 32 + 32, :], wt["cn_w3x2"][rows, :], h2[c // 2][rows, :],
                                          start=True, stop=True)
                m = activate(k, ps, T(mm), ACT.Gelu, h3, bs["cn", 3])
                twisted(2)
                if cycle == 0:
                    means = context(3, g2, g3, means)
                T.need(m)
                for c in range(NC):
                    k, ps = ring.take(T)
                    rows = slice(c * 32, c * 32 + 32)
                    mm = T(nc.tensor.matmul(ps[:], wlast["cn"][rows, :], h3[rows, :], start=True, stop=True))
                    S_.need(*ready[c])
                    marks[c] = activate(k, ps, mm, ACT.Tanh, cp[c], blast["cn"], 0.5)
                    if c == 0:
                        twisted(3)
                    couple(c)
            for c in range(NC):
                cs = slice(c * CH, (c + 1) * CH)
                b = c // 2
                S_.need(*ready[c])
                m = S_(nc.scalar.activation(h1[c][:], U[:, cs], ACT.Copy, scale=self.mcol[0][:, 5, b:b + 1]))
                T.need(m)
                k, ps = ring.take(T)
                for j in range(4):
                    mm = nc.tensor.transpose(ps[:, j * P:(j + 1) * P], h1[c][:, j * P:(j + 1) * P], self.ident[:])
                mm = T(mm)
                V.need(mm)
                xc = self.X[:, 4 * c:4 * c + 4, :].rearrange("p k d -> p (k d)")
                m = V(nc.vector.tensor_tensor(xc, xc, ps[:], ALU.add))
                ring.release(k, m)
            self.settle()

    def mod_rows(self, dst, src, l, shift, marks):
        nc, V, G = self.nc, self.V, self.G
        done = []
        for eng, e, ts, b in self.parts():
            n = ts.stop - ts.start
            eng.need(self.m_row, *marks[ts])
            row = lambda i: self.mrow[l][:, b, i:i + 1, :].to_broadcast([P, n, D])
            m = eng(e.tensor_tensor(dst[:, ts, :], src[:, ts, :], row(shift + 1), ALU.mult))
            eng.need(m)
            done += [eng(e.tensor_tensor(dst[:, ts, :], dst[:, ts, :], row(shift), ALU.add))] * n
        return done

    def mamba(self):
        nc, A, V, S_, G, T, Q = self.nc, self.A, self.V, self.S, self.G, self.T, self.Q
        with ExitStack() as scope:
            sb = lambda n, s, d=F32: self.sb(scope, n, s, d)
            R2 = 2 * DS
            in_w = Arrival(scope, nc, "in_mamba")
            def load(name, shape, src, dt=F32):
                t = sb(name, shape, dt)
                in_w(nc.sync.dma_start(t[:], src))
                return t
            nw = load("norm_w", [P, NL], A["norm_w"])
            cb = load("conv_b", [P, NL, NBLK], A["conv_b"])
            cwc = load("conv_w", [P, NL, KW], A["conv_w_last"])
            dp = load("d_skip", [P, NL, NBLK], A["Dp"])
            am = load("a_log", [P, NL, NBLK, DS], A["A_log"])
            ow = load("out_w", [P, NBLK, NL, D], A["out_wT"])
            rowsel = load("row_ident", [3 * R2, R2], A["k_rows"])
            iw = sb("in_w", [P, NL, 2 * DI])
            csb = [sb(f"c_row{s}", [P, S]) for s in range(2)]
            cw = [csb[0][:].rearrange("p (j e) -> p j e", j=KW), sb("tap_w", [P, KW, DI])[:]]
            xw = sb("x_proj_w", [P, NBLK, NL, 3 * R2 + DTR])
            LOW = slice(3 * R2, 3 * R2 + DTR)
            dtw = sb("dt_w", [3 * R2 + DTR + 1, NL, DI])
            in_w(nc.scalar.dma_start(dtw[LOW], A["dt_wT"]))
            in_w(nc.scalar.dma_start(dtw[3 * R2 + DTR:], A["dt_b"]))
            in_w(nc.sync.dma_start(iw[:], A["in_wT"]))
            in_w(nc.sync.dma_start(xw[:], A["xp_wT"]))
            for l in range(NL):
                in_w(nc.scalar.dma_start(cw[l], A["conv_wT"][l:l + 1].to_broadcast([P, KW, DI])))
            sel = sb("row_select", [3 * R2, R2, P], BF16)
            xm = sb("x_mamba", [P, NT, D])
            flat = sb("momentum", [P, NBLK * 2 * S])
            hp = flat[:, 0:NB * (S + KW - 1)].rearrange("p (b t) -> p b t", b=NB)
            xb = sb("x_inner", [P, NBLK, NB, S])
            zs = sb("silu_z", [P, NBLK, NB, S])
            delta = sb("delta", [P, NBLK, NB, S])
            du = sb("delta_x", [P, NBLK, NB, S])
            dr = sb("delta_low", [3 * R2 + DTR + 1, TOK])
            bcr = csb[1][0:3 * R2, 0:CH]
            bcm = sb("bc_mid", [3 * R2, CH], BF16)
            bc = sb("bc_parts", [3 * R2, TOK], BF16)
            ddiag = sb("d_diag", [P, NBLK, P])
            beta = sb("momentum_beta", [P, S])
            bsb = [sb(f"b_row{s}", [P, S]) for s in range(2)]
            da = [sb(f"decay{s}", [P, NBLK, S]) for s in range(2)]
            mi = [flat[:, s * NBLK * S:(s + 1) * NBLK * S].rearrange("p (k t) -> p k t", k=NBLK) for s in range(2)]
            hh = self.HT[:].rearrange("p (k t) -> p k t", k=NBLK)
            yp = [self.N[:].rearrange("p a d -> p (a d)").rearrange("p (k t) -> p k t", k=NBLK)]

            G.need(G(nc.gpsimd.memset(beta[:], BETA)))
            m_ones = G(nc.gpsimd.memset(dr[3 * R2:, :], 1.0))
            G.need(m_ones)
            normed = self.layer_norm(self.X)
            xm_ready = self.mod_rows(xm, self.N, 1, 0, normed)
            first_rms = self.rms_stats(xm, xm_ready)
            S_.need(in_w.mark())
            m_a = S_(nc.scalar.activation(am[:].rearrange("p l k n -> p (l k n)"),
                                          am[:].rearrange("p l k n -> p (l k n)"), ACT.Exp))
            V.need(in_w.mark(), m_a)
            for l in range(NL):
                m_taps = V(nc.vector.tensor_tensor(cw[l], cw[l],
                                                   iw[:, l:l + 1, 0:DI].to_broadcast([P, KW, DI]), ALU.mult))
            V(nc.vector.tensor_scalar(am[:].rearrange("p l k n -> p (l k n)"),
                                      am[:].rearrange("p l k n -> p (l k n)"), -1.0, None, ALU.mult))
            G.need(in_w.mark())
            G(nc.gpsimd.tensor_copy(sel[:], rowsel[:][:, :, None].to_broadcast([3 * R2, R2, P])))
            v = locals()
            for l in range(NL):
                with ExitStack() as pre:
                    ring = self.banks(pre, f"m{l}_ps", 4)
                    wide = Banks([pre.enter_context(nc.psum_tensor(f"m{l}_wide{k}", [P, S], F32)) for k in range(2)])
                    if l:
                        xm_ready = self.mamba_out(l - 1, ring, v, done)
                    rms = self.rms_stats(xm, xm_ready) if l else first_rms
                    self.mamba_inputs(l, ring, wide, v, xm_ready, rms)
                done = self.mamba_scan(l, v)
            with ExitStack() as post:
                xm_ready = self.mamba_out(NL - 1, self.banks(post, "m_out", 4), v, done)
                self.x_ready = self.add_gated(xm, 1, 2, xm_ready)
                self.settle()

    def rms_stats(self, xm, ready):
        nc, V, S_ = self.nc, self.V, self.S
        N, ssq = self.N, self.stat[:, :, 0]
        roots = []
        for c in range(NC):
            ts = slice(4 * c, 4 * c + 4)
            S_.need(ready[4 * c], ready[4 * c + 3])
            a = S_(nc.scalar.activation(N[:, ts, :], xm[:, ts, :], ACT.Square))
            V.need(a)
            a = V(nc.vector.tensor_reduce(ssq[:, ts], N[:, ts, :], AX_X, ALU.add))
            if c % 2:
                ts = slice(4 * c - 4, 4 * c + 4)
                roots.append(self.rstd(ts, ssq[:, ts], 1.0 / D, a))
        return roots

    def mamba_inputs(self, l, ring, wide, v, xm_ready, rms):
        nc, V, S_, G, T = self.nc, self.V, self.S, self.G, self.T
        xm, hp, xb, zs, delta, du, dr, bc = (v[n] for n in ("xm", "hp", "xb", "zs", "delta", "du", "dr", "bc"))
        iw, xw, cw, cb, dtw, nw, LOW = (v[n] for n in ("iw", "xw", "cw", "cb", "dtw", "nw", "LOW"))
        R2 = 2 * DS
        N = self.N
        V.need(*xm_ready)
        pads = V(nc.vector.memset(hp[:, :, 0:KW - 1], 0.0))
        for b in range(NB):
            V(nc.vector.memset(v["da"][b][:, 0, 0:KW - 1], 0.0))
        normed = []
        for t in range(NT):
            V.need(rms[t // TB])
            normed.append(V(nc.vector.tensor_scalar(N[:, t, :], xm[:, t, :], self.rs[:, t:t + 1], None, ALU.mult)))
        chunk = [(c // 2, (c % 2) * CH) for c in range(NC)]
        V.need(v["in_w"].mark())
        ht = self.turn(ring, normed, lambda b: nw[:, l:l + 1], None, (v["in_w"].mark(),),
                       to=lambda c: hp[:, chunk[c][0], KW - 1 + chunk[c][1]:KW - 1 + chunk[c][1] + CH])
        T.need(v["in_w"].mark(), v["m_taps"], v["m_ones"], pads)
        conv, low, ws = {}, {}, {}
        for blk in range(NBLK):
            G(nc.gpsimd.tensor_scalar(v["ddiag"][:, blk, :], self.ident[:], v["dp"][:, l, blk:blk + 1], None, ALU.mult))

        def inner_last(c):
            b, off = chunk[c]
            blk = NBLK - 1
            xin = v["da"][b][:].rearrange("p k t -> p (k t)")
            acc = v["mi"][1][:, blk, (c % 2) * CH:(c % 2 + 1) * CH]
            k, ps = ring.take(T)
            S_.need(T(nc.tensor.matmul(ps[:], iw[:, l, blk * P:(blk + 1) * P],
                                       hp[:, b, KW - 1 + off:KW - 1 + off + CH], start=True, stop=True)))
            m = S_(nc.scalar.activation(xin[:, KW - 1 + off:KW - 1 + off + CH], ps[:], ACT.Copy))
            ring.release(k, m)
            V.need(m, conv[blk, c - 2] if c > 1 else None)
            m = V(nc.vector.tensor_scalar(acc, xin[:, off:off + CH], v["cwc"][:, l, 0:1], None, ALU.mult))
            for j in range(1, KW):
                V.need(m)
                m = V(nc.vector.scalar_tensor_tensor(out=acc, in0=xin[:, off + j:off + j + CH],
                                                     scalar=v["cwc"][:, l, j:j + 1], in1=acc,
                                                     op0=ALU.mult, op1=ALU.add))
            def finish():
                S_.need(m)
                conv[blk, c] = S_(nc.scalar.activation(xb[:, blk, b, off:off + CH], acc, ACT.Silu,
                                                       bias=cb[:, l, blk:blk + 1]))
            return finish

        def inner(c, blk):
            b, off = chunk[c]
            T.need(ht[c])
            k, ps = ring.take(T)
            for j in range(KW):
                mm = nc.tensor.matmul(ps[:], cw[l][:, j, blk * P:(blk + 1) * P], hp[:, b, off + j:off + j + CH],
                                      start=(j == 0), stop=(j == KW - 1))
            S_.need(T(mm))
            conv[blk, c] = S_(nc.scalar.activation(xb[:, blk, b, off:off + CH], ps[:], ACT.Silu,
                                                   bias=cb[:, l, blk:blk + 1]))
            ring.release(k, conv[blk, c])

        def gate(c):
            b, off = chunk[c]
            for blk in range(NBLK):
                k, ps = ring.take(T)
                mm = T(nc.tensor.matmul(ps[:], iw[:, l, DI + blk * P:DI + (blk + 1) * P],
                                        hp[:, b, KW - 1 + off:KW - 1 + off + CH], start=True, stop=True))
                S_.need(mm)
                ring.release(k, S_(nc.scalar.activation(zs[:, blk, b, off:off + CH], ps[:], ACT.Silu)))

        def project(c):
            b, off = chunk[c]
            cs = slice(c * CH, (c + 1) * CH)
            T.need(*[conv[blk, c] for blk in range(NBLK)])
            k, ps = ring.take(T)
            for blk in range(NBLK):
                mm = nc.tensor.matmul(ps[0:3 * R2 + DTR, :], xw[:, blk, l, :], xb[:, blk, b, off:off + CH],
                                      start=(blk == 0), stop=(blk == NBLK - 1))
            mm = T(mm)
            S_.need(mm)
            S_(nc.scalar.activation(dr[LOW, cs], ps[LOW, :], ACT.Copy))
            low[c] = S_.last()
            a = S_(nc.scalar.activation(bc[:, cs], ps[0:3 * R2, :], ACT.Copy))
            V.need(a)
            rest, mid = v["bcr"], v["bcm"]
            a = V(nc.vector.tensor_tensor(rest[:], ps[0:3 * R2, :], bc[:, cs], ALU.subtract))
            ring.release(k, a)
            V.need(a)
            a = V(nc.vector.tensor_copy(mid[:], rest[:]))
            V.need(a)
            V(nc.vector.tensor_copy(bc[R2:2 * R2, cs], mid[R2:2 * R2, :]))
            a = V(nc.vector.tensor_tensor(bc[2 * R2:, cs], rest[2 * R2:, :], mid[2 * R2:, :], ALU.subtract))
            V.need(a)

        def softplus(b):
            T.need(low[2 * b], low[2 * b + 1])
            for blk in range(NBLK):
                k, ps = wide.take(T)
                for c in range(2):
                    mm = nc.tensor.matmul(ps[:, c * CH:(c + 1) * CH], dtw[3 * R2:, l, blk * P:(blk + 1) * P],
                                          dr[3 * R2:, b * S + c * CH:b * S + (c + 1) * CH], start=True, stop=True)
                mm = T(mm)
                out, w = delta[:, blk, b, :], du[:, blk, b, :]
                S_.need(mm)
                a = S_(nc.scalar.activation(out, ps[:], ACT.Abs))
                S_.need(a)
                x_ = S_(nc.scalar.activation(out, out, ACT.Exp, scale=-1.0))
                V.need(x_)
                a = V(nc.vector.tensor_scalar(w, out, 1.0, None, ALU.add))
                V.need(a)
                a = V(nc.vector.scalar_tensor_tensor(out=out, in0=w, scalar=-1.0, in1=out,
                                                     op0=ALU.add, op1=ALU.subtract))
                V.need(a)
                a = V(nc.vector.scalar_tensor_tensor(out=out, in0=ps[:], scalar=0.0, in1=out,
                                                     op0=ALU.max, op1=ALU.subtract))
                wide.release(k, a)
                ws[blk, b] = a

        def delta_end(b):
            for blk in range(NBLK):
                out, w = delta[:, blk, b, :], du[:, blk, b, :]
                S_.need(ws[blk, b])
                ln = S_(nc.scalar.activation(w, w, ACT.Ln))
                V.need(ln, ws[blk, b])
                a = V(nc.vector.tensor_tensor(out, out, w, ALU.add))
                eng, e = (G, nc.gpsimd) if b == 0 else (V, nc.vector)
                eng.need(a, conv[blk, 2 * b], conv[blk, 2 * b + 1])
                eng(e.tensor_tensor(w, out, xb[:, blk, b, :], ALU.mult))

        for c in range(NC):
            finish = inner_last(c)
            inner(c, 0)
            if c == 3:
                softplus(0)
            finish()
            if c:
                project(c - 1)
        gate(0)
        project(3)
        delta_end(0)
        softplus(1)
        for c in range(1, NC):
            gate(c)
        up_to_here = (ws[0, 1], ws[1, 1], S_.last(), T.last(), G.last())
        delta_end(1)
        for t in (T, S_, G, V):
            t.need(*up_to_here)


    def mamba_out(self, l, ring, v, rows_left):
        nc, V, T = self.nc, self.V, self.T
        xm, zs, ow = (v[n] for n in ("xm", "zs", "ow"))
        done = []
        last_y = V.last()
        rows_left()
        for c in range(NC):
            if c == NC - NC // NB:
                T.need(last_y)
            k, ps = ring.take(T)
            for j in range(4):
                t = 4 * c + j
                b, off = t // TB, (t % TB) * P
                for blk in range(NBLK):
                    mm = nc.tensor.matmul(ps[:, j * P:(j + 1) * P], zs[:, blk, b, off:off + P],
                                          ow[:, blk, l, :], start=(blk == 0), stop=(blk == NBLK - 1))
            mm = T(mm)
            V.need(mm)
            x4 = xm[:, 4 * c:4 * c + 4, :].rearrange("p k d -> p (k d)")
            m = V(nc.vector.tensor_tensor(x4, x4, ps[:], ALU.add))
            ring.release(k, m)
            done += [m] * 4
        return done

    def mamba_scan(self, l, v):
        nc, V, S_, G, T = self.nc, self.V, self.S, self.G, self.T
        with ExitStack() as scope:
            bps = scope.enter_context(nc.psum_tensor(f"b{l}", [P, S], F32))
            cps = scope.enter_context(nc.psum_tensor(f"c{l}", [P, S], F32))
            yps = scope.enter_context(nc.psum_tensor(f"y{l}", [P, NBLK, S], F32))
            ev = lambda n, e: Event(scope, nc, f"{n}{l}", e)
            b_mm, c_mm = ev("b_mm", nc.tensor), ev("c_mm", nc.tensor)
            b_out, c_out = ev("b_out", nc.scalar), ev("c_out", nc.scalar)
            decay, mom = ev("decay", nc.scalar), ev("mom", nc.gpsimd)
            vs, hs, ys = ev("v_scan", nc.vector), ev("h_scan", nc.vector), ev("y_mul", nc.vector)
            yg = ev("y_mul_g", nc.gpsimd)
            GC = 320
            whole = ev("y_whole", nc.tensor)
            ysum, gated = ev("y_sum", nc.tensor), ev("gated", nc.vector)
            xb, zs, delta, du, bc, sel = (v[n] for n in ("xb", "zs", "delta", "du", "bc", "sel"))
            am, bsb, csb, da, mi, hh, yp = (v[n] for n in ("am", "bsb", "csb", "da", "mi", "hh", "yp"))
            beta = v["beta"]

            def skip(b):
                gated.wait(nc.tensor, 2 * b)
                for blk in range(NBLK):
                    for c in range(2):
                        nc.tensor.matmul(yps[:, blk, c * CH:(c + 1) * CH], v["ddiag"][:, blk, :],
                                         xb[:, blk, b, c * CH:(c + 1) * CH], start=True, stop=False,
                                         skip_group_check=True)

            def gate(b):
                count = V if b == NB - 1 else gated
                for blk in range(NBLK):
                    if blk == 0:
                        whole.wait(nc.vector, b + 1)
                    else:
                        ysum.wait(nc.vector, DS * (b + 1))
                    count(nc.vector.tensor_tensor(zs[:, blk, b, :], zs[:, blk, b, :], yps[:, blk, :], ALU.mult))

            def rows(b, n):
                g = b * DS + n
                for ps, r, done, left in ((bps, n, b_mm, b_out), (cps, n + DS, c_mm, c_out)):
                    left.wait(nc.tensor, g)
                    for c in range(2):
                        mm = nc.tensor.matmul(ps[:, c * CH:(c + 1) * CH],
                                              sel[:, bass.ds(r, 1), :].rearrange("k a p -> k (a p)"),
                                              bc[:, b * S + c * CH:b * S + (c + 1) * CH], start=True, stop=True)
                    done(mm)

            def copies(b, n, s):
                g = b * DS + n
                b_mm.wait(nc.scalar, g + 1)
                mom.wait(nc.scalar, 2 * (g - 1))
                b_out(nc.scalar.activation(bsb[s][:], bps[:], ACT.Copy))
                c_mm.wait(nc.scalar, g + 1)
                ys.wait(nc.scalar, 2 * (g - 1))
                yg.wait(nc.scalar, g - 1)
                c_out(nc.scalar.activation(csb[s][:], cps[:], ACT.Copy))
                hs.wait(nc.scalar, 2 * (g - 1))
                for blk in range(NBLK):
                    decay(nc.scalar.activation(da[s][:, blk, :], delta[:, blk, b, :], ACT.Exp,
                                               scale=am[:, l, blk, bass.ds(n, 1)]))

            def products(b, n, s):
                g = b * DS + n
                b_out.wait(nc.gpsimd, g + 1)
                hs.wait(nc.gpsimd, 2 * (g - 1))
                for blk in range(NBLK):
                    mom(nc.gpsimd.tensor_tensor(mi[s][:, blk, :], du[:, blk, b, :], bsb[s][:], ALU.mult))

            def scans(b, n, s, opening=False):
                g = b * DS + n
                for blk in range(NBLK):
                    mom.wait(nc.vector, 2 * g + blk + 1)
                    vs(nc.vector.tensor_tensor_scan(mi[s][:, blk, :], beta[:], mi[s][:, blk, :], 0.0, ALU.mult, ALU.add))
                for blk in range(NBLK):
                    vs.wait(nc.vector, 2 * g + blk + 1)
                    decay.wait(nc.vector, 2 * g + blk + 1)
                    yg.wait(nc.vector, g)
                    hs(nc.vector.tensor_tensor_scan(hh[:, blk, :], da[s][:, blk, :], mi[s][:, blk, :], 0.0,
                                                    ALU.mult, ALU.add))
                if opening:
                    gate(b - 1)
                c_out.wait(nc.vector, g + 1)
                ysum.wait(nc.vector, g)
                for blk, end in ((0, S), (1, GC)):
                    hs.wait(nc.vector, 2 * g + blk + 1)
                    ys(nc.vector.tensor_tensor(yp[0][:, blk, 0:end], hh[:, blk, 0:end], csb[s][:, 0:end], ALU.mult))

            def y_rest(b, n, s):
                g = b * DS + n
                c_out.wait(nc.gpsimd, g + 1)
                ysum.wait(nc.gpsimd, g)
                hs.wait(nc.gpsimd, 2 * g + 2)
                yg(nc.gpsimd.tensor_tensor(yp[0][:, 1, GC:], hh[:, 1, GC:], csb[s][:, GC:], ALU.mult))

            def sums(b, n, last=False):
                g = b * DS + n
                for blk in range(NBLK):
                    ys.wait(nc.tensor, 2 * g + blk + 1)
                    if blk:
                        yg.wait(nc.tensor, g + 1)
                    for c in range(2):
                        mm = nc.tensor.matmul(yps[:, blk, c * CH:(c + 1) * CH], self.ident[:],
                                              yp[0][:, blk, c * CH:(c + 1) * CH], start=False, stop=last,
                                              skip_group_check=True)
                    if last and blk == 0:
                        whole(mm)
                ysum(mm)

            def state(b, n, s):
                peeled = isinstance(n, int)
                ahead = lambda k: divmod(b * DS + n + k, DS) if peeled else (b, n + k)
                if ahead(2)[0] < NB:
                    rows(*ahead(2))
                copies(b, n, s)
                if ahead(1)[0] < NB:
                    products(*ahead(1), 1 - s)
                opening = peeled and n == 0 and b > 0
                scans(b, n, s, opening)
                y_rest(b, n, s)
                if opening:
                    skip(b)
                sums(b, n, peeled and n == DS - 1)

            rows(0, 0)
            rows(0, 1)
            skip(0)
            products(0, 0, 0)
            for b in range(NB):
                first = 2 * min(b, 1)
                for n in range(first):
                    state(b, n, n % 2)
                with nc.Fori(0, DS // 2 - 1 - first // 2) as i:
                    for s in range(2):
                        state(b, 2 * i + first + s, s)
                for n in (DS - 2, DS - 1):
                    state(b, n, n % 2)
            gate(NB - 1)

        def rows_left():
            b_out.wait(nc.tensor, NB * DS)
            c_out.wait(nc.tensor, NB * DS)
            gated.wait(nc.tensor, 2 * (NB - 1))
        return rows_left

    def experts(self):
        nc, A, V, S_, G, T, Q = self.nc, self.A, self.V, self.S, self.G, self.T, self.Q
        with ExitStack() as scope:
            sb = lambda n, s, d=F32: self.sb(scope, n, s, d)
            in_w = Arrival(scope, nc, "in_experts")
            gam, bet = sb("ln_gamma", [P, 1]), sb("ln_beta", [P, 1])
            rw, iota = sb("router_w", [P, E]), sb("iota", [P, E])
            sgu, sdn = sb("shared_gate_up", [P, 2 * P]), sb("shared_down", [P, D])
            for t, n in ((gam, "ln_gamma"), (bet, "ln_beta"), (rw, "router_w"), (iota, "k_iota"),
                         (sgu, "shared_gate_up_w"), (sdn, "shared_down_w")):
                in_w(nc.scalar.dma_start(t[:], A[n]))
            gu = [sb(f"gate_up{s}", [P, 2 * FF]) for s in range(2)]
            dn = [sb(f"down{s}", [P, FB, D]) for s in range(2)]
            hm = sb("moe_in", [P, NT, D])
            acc = sb("moe_out", [P, NT, D])
            lg = sb("logits", [P, NT, E])
            top = sb("top_values", [P, NT, 8])
            idx = sb("top_index", [P, NT, 8], U32)
            idf = sb("top_index_f", [P, NT, 8])
            comb = sb("combine", [P, E + 1, NT])
            e2, w1, w2 = sb("exp_second", [P, NT]), sb("weight1", [P, NT]), sb("weight2", [P, NT])
            mk = [sb(f"mask{i}", [P, NT, E]) for i in range(2)]
            gc = [sb(f"gate{i}", [P, CH]) for i in range(2)]
            sg = [sb(f"silu_gate{i}", [P, CH]) for i in range(2)]
            act = [sb(f"hidden{i}", [P, FB, CH]) for i in range(2)]

            got = [Event(scope, nc, f"weights_in{s}", nc.sync) for s in range(2)]
            gu_mm = Event(scope, nc, "gu_mm", nc.tensor)
            clip, gate, hid = (Event(scope, nc, n, e) for n, e in
                               (("clip", nc.vector), ("gate_out", nc.scalar), ("hid", nc.vector)))
            dn_mm = Event(scope, nc, "dn_mm", nc.tensor, 1)
            summed = Event(scope, nc, "summed", nc.vector, 4)

            def fetch(e, s):
                dn_mm.wait(nc.sync, NC * (e - 1))
                got[s](nc.sync.dma_start(gu[s][:], A["gate_up_w"][bass.ds(e, 1)].rearrange("a d f -> (a d) f")), 16)
                got[s](nc.sync.dma_start(dn[s][:], A["down_w"][bass.ds(e, 1)].rearrange("a p k d -> (a p) k d")), 16)

            normed = self.layer_norm(self.X, self.x_ready)
            h_ready = self.mod_rows(hm, self.N, 1, 3, normed)
            G.need(*h_ready)
            G(nc.gpsimd.memset(comb[:, 0, :], 0.0))
            G(nc.gpsimd.memset(act[1][:], 0.0))
            m_zero = G(nc.gpsimd.memset(dn[1][:], 0.0))
            normed = self.layer_norm(hm, h_ready)
            with ExitStack() as pre:
                ring = self.banks(pre, "moe_ps", 8)
                S_.need(in_w.mark())
                ht = self.turn(ring, normed, lambda b: gam[:], lambda b: bet[:], (in_w.mark(),))
                T.need(in_w.mark())
                hidden, opened = [None] * NC, []
                def shared_up(c):
                    cs = slice(c * CH, (c + 1) * CH)
                    T.need(ht[c])
                    kg, pg = ring.take(T)
                    mg = T(nc.tensor.matmul(pg[:], sgu[:, 0:P], self.HT[:, cs], start=True, stop=True))
                    ku, pu = ring.take(T)
                    mu = T(nc.tensor.matmul(pu[:], sgu[:, P:2 * P], self.HT[:, cs], start=True, stop=True))
                    V.need(mg, hidden[c - 2] if c > 1 else None)
                    m = V(nc.vector.tensor_scalar(gc[c % 2][:], pg[:], -10.0, 10.0, ALU.max, ALU.min))
                    ring.release(kg, m)
                    S_.need(m)
                    s = S_(nc.scalar.activation(sg[c % 2][:], gc[c % 2][:], ACT.Silu))
                    V.need(mu, s)
                    hidden[c] = V(nc.vector.tensor_tensor(act[0][:, c, :], sg[c % 2][:], pu[:], ALU.mult))
                    ring.release(ku, hidden[c])
                    S_.need(hidden[c])
                shared_up(0)
                shared_up(1)
                T.need(*ht)
                k, ps = ring.take(T)
                for t in range(NT):
                    mm = nc.tensor.matmul(ps[:, t * E:(t + 1) * E], self.HT[:, t * P:(t + 1) * P], rw[:],
                                          start=True, stop=True)
                mm = T(mm)
                shared_up(2)
                shared_up(3)
                V.need(mm)
                m = logits = V(nc.vector.tensor_copy(lg[:].rearrange("p t e -> p (t e)"), ps[:, 0:NT * E]))
                ring.release(k, m)
                for c in range(NC):
                    T.need(hidden[c])
                    kd, pd = ring.take(T)
                    for j in range(4):
                        mm = nc.tensor.matmul(pd[:, j * P:(j + 1) * P], act[0][:, c, j * P:(j + 1) * P], sdn[:],
                                              start=True, stop=True)
                    mm = down_done = T(mm)
                    S_.need(mm)
                    opened.append(S_(nc.scalar.activation(acc[:, 4 * c:4 * c + 4, :].rearrange("p k d -> p (k d)"),
                                                          pd[:], ACT.Copy)))
                    ring.release(kd, opened[-1])
                V.need(m)
                for t in range(NT):
                    m = V(nc.vector.max(top[:, t, :], lg[:, t, :]))
                V.need(m)
                for t in range(NT):
                    m = V(nc.vector.max_index(idx[:, t, :], top[:, t, :], lg[:, t, :]))
                d = V(nc.vector.tensor_tensor(e2[:], top[:, :, 1], top[:, :, 0], ALU.subtract))
                S_.need(d)
                x_ = S_(nc.scalar.activation(e2[:], e2[:], ACT.Exp))
                V.need(m)
                i_ = V(nc.vector.tensor_copy(idf[:].rearrange("p t e -> p (t e)"), idx[:].rearrange("p t e -> p (t e)")))
                V.need(x_)
                m = V(nc.vector.tensor_scalar(w2[:], e2[:], 1.0, None, ALU.add))
                V.need(m)
                m = V(nc.vector.reciprocal(w1[:], w2[:]))
                V.need(m, i_)
                m = V(nc.vector.tensor_tensor(w2[:], e2[:], w1[:], ALU.mult))
                V.need(m)
                for i, w in ((0, w1), (1, w2)):
                    m = V(nc.vector.tensor_tensor(mk[i][:], idf[:, :, i:i + 1].to_broadcast([P, NT, E]),
                                                  iota[:][:, None, :].to_broadcast([P, NT, E]), ALU.is_equal))
                    V.need(m)
                    m = V(nc.vector.tensor_tensor(mk[i][:], mk[i][:], w[:][:, :, None].to_broadcast([P, NT, E]), ALU.mult))
                V.need(m)
                m_comb = V(nc.vector.tensor_tensor(comb[:, 1:, :].rearrange("p e t -> p t e"), mk[0][:], mk[1][:], ALU.add))
            T.need(*hidden, *opened, logits, m_zero)
            S_.need(*hidden)
            V.need(*opened, down_done, m_comb, m_zero)

            gups = scope.enter_context(nc.psum_tensor("gate_up_ps", [P, 3, 2, CH], F32))
            dps = scope.enter_context(nc.psum_tensor("down_ps", [P, 2, CH], F32))
            Q.need(m_zero)

            def step_up(u, i, s, c, f, kf, behind):
                st = FB * u + f
                if c == 0 and f == 0:
                    got[s].wait(nc.tensor, 32 * (i + 1))
                hid.wait(nc.tensor, st - behind)
                for j in range(2):
                    mm = nc.tensor.matmul(gups[:, kf, j, :], gu[s][:, j * FF + f * P:j * FF + (f + 1) * P],
                                          self.HT[:, c * CH:(c + 1) * CH], start=True, stop=True)
                gu_mm(mm)
                k2 = f % 2
                gu_mm.wait(nc.vector, st + 1)
                gate.wait(nc.vector, st - 1)
                clip(nc.vector.tensor_scalar(gc[k2][:], gups[:, kf, 0, :], -10.0, 10.0, ALU.max, ALU.min))
                clip.wait(nc.scalar, st + 1)
                hid.wait(nc.scalar, st - 1)
                gate(nc.scalar.activation(sg[k2][:], gc[k2][:], ACT.Silu))

            def step_hid(u, c, f, kf):
                st = FB * u + f
                gate.wait(nc.vector, st + 1)
                dn_mm.wait(nc.vector, u - 1)
                hid(nc.vector.tensor_tensor(act[c % 2][:, f, :], sg[f % 2][:], gups[:, kf, 1, :], ALU.mult))

            def down(u, s, c):
                hid.wait(nc.tensor, FB * (u + 1))
                summed.wait(nc.tensor, 4 * (u - 1))
                for j in range(4):
                    for f in range(FB):
                        mm = nc.tensor.matmul(dps[:, c % 2, j * P:(j + 1) * P], act[c % 2][:, f, j * P:(j + 1) * P],
                                              dn[s][:, f, :], start=(f == 0), stop=(f == FB - 1))
                dn_mm(mm)

            def add_up(u, e1, c):
                dn_mm.wait(nc.vector, u + 1)
                for j in range(4):
                    t = 4 * c + j
                    summed.wait(nc.vector, 4 * u)
                    summed(nc.vector.scalar_tensor_tensor(
                        out=acc[:, t, :], in0=dps[:, c % 2, j * P:(j + 1) * P],
                        scalar=comb[:, bass.ds(e1, 1), t], in1=acc[:, t, :], op0=ALU.mult, op1=ALU.add))

            def body(i, experts, fetch_next):
                k = 0
                late = None
                for s in range(2):
                    e = experts[s]
                    for c in range(NC):
                        u = NC * e + c
                        for f in range(FB):
                            step_up(u, i, s, c, f, k % 3, 1 if k < 2 else 2)
                            if late:
                                step_hid(*late)
                            late = (u, c, f, k % 3)
                            if f == 1:
                                down(u - 1, s if c else 1 - s, (c - 1) % NC)
                                add_up(u - 1, e + 1 if c else e, (c - 1) % NC)
                                if c == 0 and fetch_next[s]:
                                    fetch(e + 1, 1 - s)
                            k += 1
                step_hid(*late)

            fetch(0, 0)
            with nc.Fori(0, E // 2 - 1) as i:
                body(i, (2 * i, 2 * i + 1), (True, True))
            body(E // 2 - 1, (E - 2, E - 1), (True, False))
            u = NC * E - 1
            down(u, 1, NC - 1)
            add_up(u, E, NC - 1)
            summed.wait(nc.vector, 4 * NC * E)
            summed.wait(nc.gpsimd, 4 * NC * E)
            self.add_gated(acc, 1, 5, [None] * NT)
            self.settle()

    def store(self):
        nc, Q = self.nc, self.Q
        with ExitStack() as scope:
            stored = Arrival(scope, nc, "stored")
            for b in range(NB):
                stored(nc.sync.dma_start(self.out[b].rearrange("(k p) d -> p k d", p=P),
                                         self.X[:, b * TB:(b + 1) * TB, :]))
            nc.sync.wait_ge(stored.sem, stored.n)



def _layout(inputs):
    f = {k: np.ascontiguousarray(v) for k, v in inputs.items()}
    a = {"L0_attn_x": f["L0_attn_x"]}
    for l in range(2):
        a[f"cT{l}"] = f[f"L{l}_c"].T
        a[f"L{l}_wmod"] = f[f"L{l}_wmod"]
    for n in "qkv":
        a[f"W{n}T"] = f[f"L0_attn_W{n}"].T
    for n in ("cn_w1", "cn_w2", "gc_w1", "gc_w2"):
        a[n] = f[f"L0_ffn_{n}"]
    a["cn_w3x2"] = np.tile(f["L0_ffn_cn_w3"], (2, 1))
    a["cpl_cols"] = np.stack([np.resize(f[f"L0_ffn_{n}"], P) for n in CPL_COLS], axis=1)
    m = {k[8:]: f[k] for k in f if k.startswith("L1_attn_")}
    a["norm_w"] = m["norm_w"].T
    a["in_wT"] = m["in_proj_w"].transpose(2, 0, 1)
    a["conv_wT"] = m["conv_w"].reshape(NL, DI, KW).transpose(0, 2, 1)
    a["conv_b"] = m["conv_b"].reshape(NL, NBLK, P).transpose(2, 0, 1)
    xp = m["x_proj_w"].transpose(2, 0, 1).reshape(NBLK, P, NL, DTR + 2 * DS).transpose(1, 0, 2, 3)
    a["xp_wT"] = np.concatenate([xp[..., DTR:]] * 3 + [xp[..., :DTR]], axis=-1)
    a["conv_w_last"] = m["conv_w"].reshape(NL, NBLK, P, KW)[:, NBLK - 1].transpose(1, 0, 2)
    a["dt_wT"] = m["dt_w"].transpose(2, 0, 1)
    a["dt_b"] = m["dt_b"][None]
    a["A_log"] = m["A_log"].reshape(NL, NBLK, P, DS).transpose(2, 0, 1, 3)
    a["Dp"] = m["Dp"].reshape(NL, NBLK, P).transpose(2, 0, 1)
    a["out_wT"] = m["out_w"].transpose(2, 0, 1).reshape(NBLK, P, NL, D).transpose(1, 0, 2, 3)
    a["ln_gamma"] = f["L1_ffn_ln_gamma"][:, None]
    a["ln_beta"] = f["L1_ffn_ln_beta"][:, None]
    a["router_w"] = f["L1_ffn_router_w"]
    a["gate_up_w"] = f["L1_ffn_gate_up_w"]
    a["down_w"] = f["L1_ffn_down_w"].reshape(E, FB, P, D).transpose(0, 2, 1, 3)
    a["shared_gate_up_w"] = f["L1_ffn_shared_gate_up_w"]
    a["shared_down_w"] = f["L1_ffn_shared_down_w"]
    eye = np.eye(P, dtype=np.float32)
    a["k_ident"] = eye
    a["k_groupsum"] = np.tile(np.eye(32, dtype=np.float32), (4, 1))
    twist = np.zeros((P, P), np.float32)
    for to, frm, sign in ((0, 2, 1.0), (1, 3, -1.0), (2, 0, -1.0), (3, 1, 1.0)):
        twist[32 * frm + np.arange(32), 32 * to + np.arange(32)] = sign
    a["k_twist"] = twist
    a["k_rows"] = np.tile(np.eye(2 * DS, dtype=np.float32), (3, 1))
    a["k_iota"] = np.tile(np.arange(E, dtype=np.float32), (P, 1))
    return {k: np.ascontiguousarray(v) for k, v in a.items()}


def kernel(**inputs):
    import concourse.bacc as bacc
    from concourse.bass_utils import run_bass_kernel_spmd

    nc = bacc.Bacc("TRN2", target_bir_lowering=False, num_devices=1)
    arrays = _layout(inputs)
    args = {n: nc.dram_tensor(f"in_{n}", a.shape, mybir.dt.from_np(a.dtype), kind="ExternalInput").ap()
            for n, a in arrays.items()}
    out = nc.dram_tensor("out", (NB, S, D), F32, kind="ExternalOutput").ap()
    build(nc, args, out)
    r = run_bass_kernel_spmd(nc, [{f"in_{n}": a for n, a in arrays.items()}], core_ids=[0])
    return r.results[0]["out"]
```
